# Optimizing a Trainium2 kernel written in Bass

```python
import numpy as np
import jax
import jax.numpy as jnp

def _softmax(x, axis=-1):
    return jax.nn.softmax(x, axis=axis)

def _gelu(x):
    return jax.nn.gelu(x, approximate=True)

def _silu(x):
    return jax.nn.silu(x)

def _sigmoid(x):
    return jax.nn.sigmoid(x)

def _layernorm(x, axis=-1, eps=1e-05):
    m = jnp.mean(x, axis=axis, keepdims=True)
    v = jnp.var(x, axis=axis, keepdims=True)
    return (x - m) / jnp.sqrt(v + eps)

def _scatter_add(tgt, idx, src, axis=0):
    return tgt.at[idx].add(src)

def _segment_sum(src, seg, n):
    return jax.ops.segment_sum(src, seg, n)
kernel_name = 'mk_seq_postln_d4_jaxref_r8_20ae4c'

def setup_inputs(seed: int=0):
    np.random.seed(seed)
    _w = jnp.asarray

    def _L0_attn_setup():
        import jax, jax.numpy as jnp
        import numpy as np
        NUM_HEADS = 16

        def _heads(t, B, N, H, hd):
            return t.reshape(B, N, H, hd).transpose(0, 2, 1, 3)
        key = jax.random.key(seed)
        ks = jax.random.split(key, 9)
        B, N, D = (2, 256, 128)
        w = 0.02
        return {'x': jax.random.normal(ks[0], (B, N, D), dtype=jnp.float32), 'wq': jax.random.normal(ks[1], (D, D), dtype=jnp.float32) * w, 'bq': jax.random.normal(ks[2], (D,), dtype=jnp.float32) * w, 'wk': jax.random.normal(ks[3], (D, D), dtype=jnp.float32) * w, 'bk': jax.random.normal(ks[4], (D,), dtype=jnp.float32) * w, 'wv': jax.random.normal(ks[5], (D, D), dtype=jnp.float32) * w, 'bv': jax.random.normal(ks[6], (D,), dtype=jnp.float32) * w, 'wo': jax.random.normal(ks[7], (D, D), dtype=jnp.float32) * w, 'bo': jax.random.normal(ks[8], (D,), dtype=jnp.float32) * w}
    _L0_attn_in = _L0_attn_setup()

    def _L0_ffn_setup():
        import jax, jax.numpy as jnp
        import numpy as np
        B, S, D = (2, 256, 128)
        H, HKV = (16, 4)
        HD = D // H
        F, E, K = (256, 8, 2)
        THETA = 10000.0
        EPS = 1e-05

        def _rmsnorm(x, w):
            return x * jax.lax.rsqrt(jnp.mean(x * x, axis=-1, keepdims=True) + EPS) * w

        def _rope_cos_sin(seq_len, head_dim, theta):
            inv_freq = 1.0 / theta ** (jnp.arange(0, head_dim, 2, dtype=jnp.float32) / head_dim)
            freqs = jnp.arange(seq_len, dtype=jnp.float32)[:, None] * inv_freq
            return (jnp.cos(freqs), jnp.sin(freqs))

        def _apply_rope(x, cos, sin):
            x1, x2 = jnp.split(x, 2, axis=-1)
            c = cos[None, :, None, :]
            s = sin[None, :, None, :]
            return jnp.concatenate([x1 * c - x2 * s, x2 * c + x1 * s], axis=-1)
        key = jax.random.key(seed)
        ks = jax.random.split(key, 12)
        s = 0.02
        return {'hidden_states': jax.random.normal(ks[0], (B, S, D), jnp.float32), 'ln1_w': 1.0 + 0.1 * jax.random.normal(ks[1], (D,), jnp.float32), 'ln2_w': 1.0 + 0.1 * jax.random.normal(ks[2], (D,), jnp.float32), 'Wq': s * jax.random.normal(ks[3], (D, H * HD), jnp.float32), 'Wk': s * jax.random.normal(ks[4], (D, HKV * HD), jnp.float32), 'Wv': s * jax.random.normal(ks[5], (D, HKV * HD), jnp.float32), 'Wo': s * jax.random.normal(ks[6], (H * HD, D), jnp.float32), 'Wr': s * jax.random.normal(ks[7], (D, E), jnp.float32), 'Wg': s * jax.random.normal(ks[8], (E, D, F), jnp.float32), 'Wu': s * jax.random.normal(ks[9], (E, D, F), jnp.float32), 'Wd': s * jax.random.normal(ks[10], (E, F, D), jnp.float32)}
    _L0_ffn_in = _L0_ffn_setup()

    def _L1_attn_setup():
        import jax, jax.numpy as jnp
        import numpy as np
        key = jax.random.key(seed)
        k0, k1, k2, k3 = jax.random.split(key, 4)
        B, T, D = (4, 256, 128)
        s = 1.0 / np.sqrt(D)
        return {'inputs': jax.random.normal(k0, (B, T, D), dtype=jnp.float32), 'Wq': jax.random.normal(k1, (D, D), dtype=jnp.float32) * s, 'Wk': jax.random.normal(k2, (D, D), dtype=jnp.float32) * s, 'Wv': jax.random.normal(k3, (D, D), dtype=jnp.float32) * s}
    _L1_attn_in = _L1_attn_setup()

    def _L1_ffn_setup():
        import jax, jax.numpy as jnp
        import numpy as np
        B, S, H = (1, 256, 128)
        E, K = (16, 4)
        G, TG = (4, 2)
        I_MOE = 64
        N_SH = 2
        SCALE = 2.5

        def _mlp(x, gw, uw, dw):
            return jax.nn.silu(x @ gw.T) * (x @ uw.T) @ dw.T

        def _route(x2d, router_weight, e_bias):
            T = x2d.shape[0]
            scores = jax.nn.sigmoid(x2d @ router_weight.T)
            sc = scores + e_bias[None, :]
            group_scores = jnp.sum(jax.lax.top_k(sc.reshape(T, G, E // G), 2)[0], axis=-1)
            _, gidx = jax.lax.top_k(group_scores, TG)
            gmask = jnp.zeros((T, G), sc.dtype).at[jnp.arange(T)[:, None], gidx].set(1.0)
            smask = jnp.repeat(gmask, E // G, axis=1)
            masked = jnp.where(smask > 0, sc, 0.0)
            _, tidx = jax.lax.top_k(masked, K)
            tw = jnp.take_along_axis(scores, tidx, axis=1)
            tw = tw / (jnp.sum(tw, axis=-1, keepdims=True) + 1e-20)
            tw = tw * SCALE
            return (tidx, tw)

        def _moe_forward(hidden_states, router_weight, e_bias, gate_w, up_w, down_w, sh_gate_w, sh_up_w, sh_down_w):
            orig_shape = hidden_states.shape
            x = hidden_states.reshape(-1, H)
            T = x.shape[0]
            tidx, tw = _route(x, router_weight, e_bias)
            g = jnp.einsum('th,eih->tei', x, gate_w)
            u = jnp.einsum('th,eih->tei', x, up_w)
            h = jax.nn.silu(g) * u
            yo = jnp.einsum('tei,ehi->teh', h, down_w)
            combine = jnp.zeros((T, E), tw.dtype).at[jnp.arange(T)[:, None], tidx].add(tw)
            routed = jnp.einsum('te,teh->th', combine, yo)
            shared = _mlp(hidden_states.reshape(-1, H), sh_gate_w, sh_up_w, sh_down_w)
            return (routed + shared).reshape(orig_shape)
        key = jax.random.key(seed)
        ks = jax.random.split(key, 9)
        s = 0.02
        return {'hidden_states': jax.random.normal(ks[0], (B, S, H), jnp.float32), 'router_weight': jax.random.normal(ks[1], (E, H), jnp.float32) * s, 'e_bias': jnp.zeros((E,), jnp.float32), 'gate_w': jax.random.normal(ks[2], (E, I_MOE, H), jnp.float32) * s, 'up_w': jax.random.normal(ks[3], (E, I_MOE, H), jnp.float32) * s, 'down_w': jax.random.normal(ks[4], (E, H, I_MOE), jnp.float32) * s, 'sh_gate_w': jax.random.normal(ks[5], (N_SH * I_MOE, H), jnp.float32) * s, 'sh_up_w': jax.random.normal(ks[6], (N_SH * I_MOE, H), jnp.float32) * s, 'sh_down_w': jax.random.normal(ks[7], (H, N_SH * I_MOE), jnp.float32) * s}
    _L1_ffn_in = _L1_ffn_setup()

    def _L2_attn_setup():
        import jax, jax.numpy as jnp
        import numpy as np
        EMBED_DIM = 128
        N_HEADS = 16
        KV_SIZE = 64
        CLIP_DIST = 10
        SLEN = 128
        BSZ = 8
        key = jax.random.key(seed)
        ks = jax.random.split(key, 7)
        s = 0.02
        inputs = jax.random.normal(ks[0], (SLEN, BSZ, EMBED_DIM), dtype=jnp.float32)
        W_in = jax.random.normal(ks[1], (3 * N_HEADS * KV_SIZE, EMBED_DIM), dtype=jnp.float32) * s
        b_in = jnp.zeros((3 * N_HEADS * KV_SIZE,), dtype=jnp.float32)
        k_dist_emb = jax.random.normal(ks[2], (CLIP_DIST + 1, KV_SIZE), dtype=jnp.float32) * s
        v_dist_emb = jax.random.normal(ks[3], (CLIP_DIST + 1, KV_SIZE), dtype=jnp.float32) * s
        W_out = jax.random.normal(ks[4], (EMBED_DIM, N_HEADS * KV_SIZE), dtype=jnp.float32) * s
        b_out = jnp.zeros((EMBED_DIM,), dtype=jnp.float32)
        return {'inputs': inputs, 'W_in': W_in, 'b_in': b_in, 'k_dist_emb': k_dist_emb, 'v_dist_emb': v_dist_emb, 'W_out': W_out, 'b_out': b_out}
    _L2_attn_in = _L2_attn_setup()

    def _L2_ffn_setup():
        import jax, jax.numpy as jnp
        import numpy as np
        NUM_HEAVY = 128
        N_ITERS = 50
        FETCH_K_RATIO = 9.0 / 8.0
        EPS = 1.0

        def rmsnorm(x, gamma):
            scale = gamma.shape[0] ** 0.5
            normed = x / jnp.maximum(jnp.linalg.norm(x, axis=-1, keepdims=True), 1e-12)
            return normed * scale * gamma

        def feedforward(x, gamma, w1, b1, w2, b2):
            h = rmsnorm(x, gamma)
            h = jax.nn.gelu(h @ w1.T + b1, approximate=False)
            return h @ w2.T + b2

        def coor_descent(s, n_iters, k, eps):
            logk = jnp.log(jnp.asarray(k, s.dtype))
            a0 = jnp.zeros_like(s[..., :1])
            b0 = -s

            def body(carry, _):
                a, b = carry
                a = eps * (logk - jax.nn.logsumexp((s + b) / eps, axis=-1, keepdims=True))
                b = -jax.nn.relu(s + a)
                return ((a, b), None)
            (a, b), _ = jax.lax.scan(body, (a0, b0), None, length=n_iters)
            return jnp.exp((s + a + b) / eps)
        key = jax.random.key(seed)
        ks = jax.random.split(key, 12)
        b, n, dim = (8, 1024, 128)
        d_light, d_heavy = (int(dim * 0.5), dim * 4)

        def lin(k, dout, din):
            bound = 1.0 / np.sqrt(din)
            k1, k2 = jax.random.split(k)
            w = jax.random.uniform(k1, (dout, din), jnp.float32, -bound, bound)
            bb = jax.random.uniform(k2, (dout,), jnp.float32, -bound, bound)
            return (w, bb)
        x = jax.random.normal(ks[0], (b, n, dim), jnp.float32)
        routing_token = jax.random.normal(ks[1], (dim,), jnp.float32)
        w1_l, b1_l = lin(ks[2], d_light, dim)
        w2_l, b2_l = lin(ks[3], dim, d_light)
        w1_h, b1_h = lin(ks[4], d_heavy, dim)
        w2_h, b2_h = lin(ks[5], dim, d_heavy)
        return dict(x=x, routing_token=routing_token, gamma_l=jnp.ones((dim,), jnp.float32), w1_l=w1_l, b1_l=b1_l, w2_l=w2_l, b2_l=b2_l, gamma_h=jnp.ones((dim,), jnp.float32), w1_h=w1_h, b1_h=b1_h, w2_h=w2_h, b2_h=b2_h)
    _L2_ffn_in = _L2_ffn_setup()

    def _L3_attn_setup():
        import jax, jax.numpy as jnp
        import numpy as np
        B, T, D, H = (4, 256, 128, 16)
        HEAD_DIM = D // H
        LOCAL_WINDOW = 64

        def _rotate_half(t):
            t1, t2 = jnp.split(t, 2, axis=-1)
            return jnp.concatenate([-t2, t1], axis=-1)

        def _apply_rope(q, k):
            Tq, d = (q.shape[2], q.shape[3])
            half = d // 2
            theta = 1.0 / 10000.0 ** (jnp.arange(half, dtype=jnp.float32) / half)
            pos = jnp.arange(Tq, dtype=jnp.float32)
            freqs = pos[:, None] * theta[None, :]
            freqs = jnp.concatenate([freqs, freqs], axis=-1)
            cos = jnp.cos(freqs)[None, None]
            sin = jnp.sin(freqs)[None, None]
            q = q * cos + _rotate_half(q) * sin
            k = k * cos + _rotate_half(k) * sin
            return (q, k)
        key = jax.random.key(seed)
        k1, k2, k3 = jax.random.split(key, 3)
        x = jax.random.normal(k1, (B, T, D), dtype=jnp.float32)
        Wqkv = jax.random.normal(k2, (D, 3 * D), dtype=jnp.float32) * 0.02
        Wout = jax.random.normal(k3, (D, D), dtype=jnp.float32) * 0.02
        return {'x': x, 'Wqkv': Wqkv, 'Wout': Wout}
    _L3_attn_in = _L3_attn_setup()

    def _L3_ffn_setup():
        import jax, jax.numpy as jnp
        import numpy as np
        D_MODEL = 128
        D_FF = 512
        NUM_EXPERTS = 8
        B, N = (16, 128)
        key = jax.random.key(seed)
        ks = jax.random.split(key, 7)
        s_in = 1.0 / np.sqrt(D_MODEL)
        s_ff = 1.0 / np.sqrt(D_FF)
        return {'x': jax.random.normal(ks[0], (B, N, D_MODEL), dtype=jnp.float32), 'Wr': jax.random.uniform(ks[1], (D_MODEL, NUM_EXPERTS), jnp.float32, -s_in, s_in), 'br': jax.random.uniform(ks[2], (NUM_EXPERTS,), jnp.float32, -s_in, s_in), 'W1': jax.random.uniform(ks[3], (NUM_EXPERTS, D_MODEL, D_FF), jnp.float32, -s_in, s_in), 'b1': jax.random.uniform(ks[4], (NUM_EXPERTS, D_FF), jnp.float32, -s_in, s_in), 'W2': jax.random.uniform(ks[5], (NUM_EXPERTS, D_FF, D_MODEL), jnp.float32, -s_ff, s_ff), 'b2': jax.random.uniform(ks[6], (NUM_EXPERTS, D_MODEL), jnp.float32, -s_ff, s_ff)}
    _L3_ffn_in = _L3_ffn_setup()
    _d = {'L0_attn_x': _L0_attn_in['x'], 'L0_attn_wq': _L0_attn_in['wq'], 'L0_attn_bq': _L0_attn_in['bq'], 'L0_attn_wk': _L0_attn_in['wk'], 'L0_attn_bk': _L0_attn_in['bk'], 'L0_attn_wv': _L0_attn_in['wv'], 'L0_attn_bv': _L0_attn_in['bv'], 'L0_attn_wo': _L0_attn_in['wo'], 'L0_attn_bo': _L0_attn_in['bo'], 'L0_ffn_ln1_w': _L0_ffn_in['ln1_w'], 'L0_ffn_ln2_w': _L0_ffn_in['ln2_w'], 'L0_ffn_Wq': _L0_ffn_in['Wq'], 'L0_ffn_Wk': _L0_ffn_in['Wk'], 'L0_ffn_Wv': _L0_ffn_in['Wv'], 'L0_ffn_Wo': _L0_ffn_in['Wo'], 'L0_ffn_Wr': _L0_ffn_in['Wr'], 'L0_ffn_Wg': _L0_ffn_in['Wg'], 'L0_ffn_Wu': _L0_ffn_in['Wu'], 'L0_ffn_Wd': _L0_ffn_in['Wd'], 'L1_attn_Wq': _L1_attn_in['Wq'], 'L1_attn_Wk': _L1_attn_in['Wk'], 'L1_attn_Wv': _L1_attn_in['Wv'], 'L1_ffn_router_weight': _L1_ffn_in['router_weight'], 'L1_ffn_e_bias': _L1_ffn_in['e_bias'], 'L1_ffn_gate_w': _L1_ffn_in['gate_w'], 'L1_ffn_up_w': _L1_ffn_in['up_w'], 'L1_ffn_down_w': _L1_ffn_in['down_w'], 'L1_ffn_sh_gate_w': _L1_ffn_in['sh_gate_w'], 'L1_ffn_sh_up_w': _L1_ffn_in['sh_up_w'], 'L1_ffn_sh_down_w': _L1_ffn_in['sh_down_w'], 'L2_attn_W_in': _L2_attn_in['W_in'], 'L2_attn_b_in': _L2_attn_in['b_in'], 'L2_attn_k_dist_emb': _L2_attn_in['k_dist_emb'], 'L2_attn_v_dist_emb': _L2_attn_in['v_dist_emb'], 'L2_attn_W_out': _L2_attn_in['W_out'], 'L2_attn_b_out': _L2_attn_in['b_out'], 'L2_ffn_routing_token': _L2_ffn_in['routing_token'], 'L2_ffn_gamma_l': _L2_ffn_in['gamma_l'], 'L2_ffn_w1_l': _L2_ffn_in['w1_l'], 'L2_ffn_b1_l': _L2_ffn_in['b1_l'], 'L2_ffn_w2_l': _L2_ffn_in['w2_l'], 'L2_ffn_b2_l': _L2_ffn_in['b2_l'], 'L2_ffn_gamma_h': _L2_ffn_in['gamma_h'], 'L2_ffn_w1_h': _L2_ffn_in['w1_h'], 'L2_ffn_b1_h': _L2_ffn_in['b1_h'], 'L2_ffn_w2_h': _L2_ffn_in['w2_h'], 'L2_ffn_b2_h': _L2_ffn_in['b2_h'], 'L3_attn_Wqkv': _L3_attn_in['Wqkv'], 'L3_attn_Wout': _L3_attn_in['Wout'], 'L3_ffn_Wr': _L3_ffn_in['Wr'], 'L3_ffn_br': _L3_ffn_in['br'], 'L3_ffn_W1': _L3_ffn_in['W1'], 'L3_ffn_b1': _L3_ffn_in['b1'], 'L3_ffn_W2': _L3_ffn_in['W2'], 'L3_ffn_b2': _L3_ffn_in['b2']}
    _x0 = _d['L0_attn_x']
    _d['L0_attn_x'] = jax.random.normal(jax.random.fold_in(jax.random.key(seed), 1), (4, 1024, 128), dtype=_x0.dtype)
    del _x0
    return _d

def reference(L0_attn_x, L0_attn_wq, L0_attn_bq, L0_attn_wk, L0_attn_bk, L0_attn_wv, L0_attn_bv, L0_attn_wo, L0_attn_bo, L0_ffn_ln1_w, L0_ffn_ln2_w, L0_ffn_Wq, L0_ffn_Wk, L0_ffn_Wv, L0_ffn_Wo, L0_ffn_Wr, L0_ffn_Wg, L0_ffn_Wu, L0_ffn_Wd, L1_attn_Wq, L1_attn_Wk, L1_attn_Wv, L1_ffn_router_weight, L1_ffn_e_bias, L1_ffn_gate_w, L1_ffn_up_w, L1_ffn_down_w, L1_ffn_sh_gate_w, L1_ffn_sh_up_w, L1_ffn_sh_down_w, L2_attn_W_in, L2_attn_b_in, L2_attn_k_dist_emb, L2_attn_v_dist_emb, L2_attn_W_out, L2_attn_b_out, L2_ffn_routing_token, L2_ffn_gamma_l, L2_ffn_w1_l, L2_ffn_b1_l, L2_ffn_w2_l, L2_ffn_b2_l, L2_ffn_gamma_h, L2_ffn_w1_h, L2_ffn_b1_h, L2_ffn_w2_h, L2_ffn_b2_h, L3_attn_Wqkv, L3_attn_Wout, L3_ffn_Wr, L3_ffn_br, L3_ffn_W1, L3_ffn_b1, L3_ffn_W2, L3_ffn_b2):

    def _L0_attn_ref(x, wq, bq, wk, bk, wv, bv, wo, bo):
        import jax, jax.numpy as jnp
        import numpy as np
        NUM_HEADS = 16

        def _heads(t, B, N, H, hd):
            return t.reshape(B, N, H, hd).transpose(0, 2, 1, 3)
        B, N, D = x.shape
        H = NUM_HEADS
        hd = D // H
        q = _heads(x @ wq.T + bq, B, N, H, hd)
        k = _heads(x @ wk.T + bk, B, N, H, hd)
        v = _heads(x @ wv.T + bv, B, N, H, hd)
        q2 = jnp.sum(q * q, axis=-1)
        k2 = jnp.sum(k * k, axis=-1)
        qk = jnp.einsum('bhid,bhjd->bhij', q, k)
        d2 = jnp.maximum(q2[..., :, None] + k2[..., None, :] - 2.0 * qk, 1e-12)
        attn = jax.nn.softmax(-jnp.sqrt(d2), axis=-1)
        out = jnp.einsum('bhij,bhjd->bhid', attn, v)
        out = out.transpose(0, 2, 1, 3).reshape(B, N, D)
        return out @ wo.T + bo

    def _L0_ffn_ref(hidden_states, ln1_w, ln2_w, Wq, Wk, Wv, Wo, Wr, Wg, Wu, Wd):
        import jax, jax.numpy as jnp
        import numpy as np
        B, S, D = (2, 256, 128)
        H, HKV = (16, 4)
        HD = D // H
        F, E, K = (256, 8, 2)
        THETA = 10000.0
        EPS = 1e-05

        def _rmsnorm(x, w):
            return x * jax.lax.rsqrt(jnp.mean(x * x, axis=-1, keepdims=True) + EPS) * w

        def _rope_cos_sin(seq_len, head_dim, theta):
            inv_freq = 1.0 / theta ** (jnp.arange(0, head_dim, 2, dtype=jnp.float32) / head_dim)
            freqs = jnp.arange(seq_len, dtype=jnp.float32)[:, None] * inv_freq
            return (jnp.cos(freqs), jnp.sin(freqs))

        def _apply_rope(x, cos, sin):
            x1, x2 = jnp.split(x, 2, axis=-1)
            c = cos[None, :, None, :]
            s = sin[None, :, None, :]
            return jnp.concatenate([x1 * c - x2 * s, x2 * c + x1 * s], axis=-1)
        b, s, d = hidden_states.shape
        residual = hidden_states
        h = _rmsnorm(hidden_states, ln1_w)
        q = (h @ Wq).reshape(b, s, H, HD)
        k = (h @ Wk).reshape(b, s, HKV, HD)
        v = (h @ Wv).reshape(b, s, HKV, HD)
        cos, sin = _rope_cos_sin(s, HD, THETA)
        q = _apply_rope(q, cos, sin)
        k = _apply_rope(k, cos, sin)
        rep = H // HKV
        k = jnp.repeat(k, rep, axis=2)
        v = jnp.repeat(v, rep, axis=2)
        scores = jnp.einsum('bqhd,bkhd->bhqk', q, k) / np.sqrt(HD).astype(np.float32)
        causal = jnp.tril(jnp.ones((s, s), dtype=bool))
        scores = jnp.where(causal[None, None], scores, jnp.finfo(scores.dtype).min)
        attn = jax.nn.softmax(scores, axis=-1)
        ctx = jnp.einsum('bhqk,bkhd->bqhd', attn, v).reshape(b, s, H * HD)
        attn_out = ctx @ Wo
        h = jnp.clip(residual + attn_out, -100.0, 100.0)
        residual = h
        hn = _rmsnorm(h, ln2_w)
        flat = hn.reshape(b * s, d)
        logits = flat @ Wr
        probs = jax.nn.softmax(logits, axis=-1)
        topv, topi = jax.lax.top_k(probs, K)
        topv = topv / jnp.sum(topv, axis=-1, keepdims=True)
        w = jnp.sum(jax.nn.one_hot(topi, E, dtype=flat.dtype) * topv[..., None], axis=1)
        g = jnp.einsum('td,edf->etf', flat, Wg)
        u = jnp.einsum('td,edf->etf', flat, Wu)
        a = jax.nn.silu(g) * u
        o = jnp.einsum('etf,efd->etd', a, Wd)
        moe_out = jnp.einsum('te,etd->td', w, o).reshape(b, s, d)
        out = jnp.clip(residual + moe_out, -100.0, 100.0)
        return out

    def _L1_attn_ref(inputs, Wq, Wk, Wv):
        import jax, jax.numpy as jnp
        import numpy as np
        B, T, D = inputs.shape
        q = jnp.einsum('btd,ed->bte', inputs, Wq)
        k = jnp.einsum('btd,ed->bte', inputs, Wk)
        v = jnp.einsum('btd,ed->bte', inputs, Wv)
        scores = jnp.einsum('bqe,bke->bqk', q, k)
        causal = jnp.tril(jnp.ones((T, T), dtype=bool))
        scores = jnp.where(causal, scores, -jnp.inf)
        scale = jnp.asarray(1.0 / np.sqrt(D), dtype=scores.dtype)
        weights = jax.nn.softmax(scores * scale, axis=-1)
        return jnp.einsum('bqk,bke->bqe', weights, v)

    def _L1_ffn_ref(hidden_states, router_weight, e_bias, gate_w, up_w, down_w, sh_gate_w, sh_up_w, sh_down_w):
        import jax, jax.numpy as jnp
        import numpy as np
        B, S, H = (1, 256, 128)
        E, K = (16, 4)
        G, TG = (4, 2)
        I_MOE = 64
        N_SH = 2
        SCALE = 2.5

        def _mlp(x, gw, uw, dw):
            return jax.nn.silu(x @ gw.T) * (x @ uw.T) @ dw.T

        def _route(x2d, router_weight, e_bias):
            T = x2d.shape[0]
            scores = jax.nn.sigmoid(x2d @ router_weight.T)
            sc = scores + e_bias[None, :]
            group_scores = jnp.sum(jax.lax.top_k(sc.reshape(T, G, E // G), 2)[0], axis=-1)
            _, gidx = jax.lax.top_k(group_scores, TG)
            gmask = jnp.zeros((T, G), sc.dtype).at[jnp.arange(T)[:, None], gidx].set(1.0)
            smask = jnp.repeat(gmask, E // G, axis=1)
            masked = jnp.where(smask > 0, sc, 0.0)
            _, tidx = jax.lax.top_k(masked, K)
            tw = jnp.take_along_axis(scores, tidx, axis=1)
            tw = tw / (jnp.sum(tw, axis=-1, keepdims=True) + 1e-20)
            tw = tw * SCALE
            return (tidx, tw)

        def _moe_forward(hidden_states, router_weight, e_bias, gate_w, up_w, down_w, sh_gate_w, sh_up_w, sh_down_w):
            orig_shape = hidden_states.shape
            x = hidden_states.reshape(-1, H)
            T = x.shape[0]
            tidx, tw = _route(x, router_weight, e_bias)
            g = jnp.einsum('th,eih->tei', x, gate_w)
            u = jnp.einsum('th,eih->tei', x, up_w)
            h = jax.nn.silu(g) * u
            yo = jnp.einsum('tei,ehi->teh', h, down_w)
            combine = jnp.zeros((T, E), tw.dtype).at[jnp.arange(T)[:, None], tidx].add(tw)
            routed = jnp.einsum('te,teh->th', combine, yo)
            shared = _mlp(hidden_states.reshape(-1, H), sh_gate_w, sh_up_w, sh_down_w)
            return (routed + shared).reshape(orig_shape)
        return _moe_forward(hidden_states, router_weight, e_bias, gate_w, up_w, down_w, sh_gate_w, sh_up_w, sh_down_w)

    def _L2_attn_ref(inputs, W_in, b_in, k_dist_emb, v_dist_emb, W_out, b_out):
        import jax, jax.numpy as jnp
        import numpy as np
        EMBED_DIM = 128
        N_HEADS = 16
        KV_SIZE = 64
        CLIP_DIST = 10
        SLEN = 128
        BSZ = 8
        slen, bsz, _ = inputs.shape
        h, d = (N_HEADS, KV_SIZE)
        qkv = inputs @ W_in.T + b_in
        qkv = qkv.reshape(slen, bsz, 3, h, d).transpose(2, 1, 3, 0, 4)
        q, k, v = (qkv[0], qkv[1], qkv[2])
        q = q * d ** (-0.5)
        idx = jnp.arange(slen)
        dist = jnp.minimum(jnp.abs(idx[None, :] - idx[:, None]), CLIP_DIST)
        k_dist = k_dist_emb[dist]
        v_dist = v_dist_emb[dist]
        attn = jnp.einsum('bhsd,bhtd->bhst', q, k) + jnp.einsum('bhsd,std->bhst', q, k_dist)
        attn = jax.nn.softmax(attn, axis=-1)
        out = jnp.einsum('bhst,bhtd->bhsd', attn, v) + jnp.einsum('bhst,std->bhsd', attn, v_dist)
        out = out.transpose(2, 0, 1, 3).reshape(slen, bsz, h * d)
        return out @ W_out.T + b_out

    def _L2_ffn_ref(x, routing_token, gamma_l, w1_l, b1_l, w2_l, b2_l, gamma_h, w1_h, b1_h, w2_h, b2_h):
        import jax, jax.numpy as jnp
        import numpy as np
        NUM_HEAVY = 128
        N_ITERS = 50
        FETCH_K_RATIO = 9.0 / 8.0
        EPS = 1.0

        def rmsnorm(x, gamma):
            scale = gamma.shape[0] ** 0.5
            normed = x / jnp.maximum(jnp.linalg.norm(x, axis=-1, keepdims=True), 1e-12)
            return normed * scale * gamma

        def feedforward(x, gamma, w1, b1, w2, b2):
            h = rmsnorm(x, gamma)
            h = jax.nn.gelu(h @ w1.T + b1, approximate=False)
            return h @ w2.T + b2

        def coor_descent(s, n_iters, k, eps):
            logk = jnp.log(jnp.asarray(k, s.dtype))
            a0 = jnp.zeros_like(s[..., :1])
            b0 = -s

            def body(carry, _):
                a, b = carry
                a = eps * (logk - jax.nn.logsumexp((s + b) / eps, axis=-1, keepdims=True))
                b = -jax.nn.relu(s + a)
                return ((a, b), None)
            (a, b), _ = jax.lax.scan(body, (a0, b0), None, length=n_iters)
            return jnp.exp((s + a + b) / eps)
        b, n, dim = x.shape
        light_out = feedforward(x, gamma_l, w1_l, b1_l, w2_l, b2_l)
        s = jnp.einsum('bnd,d->bn', x, routing_token)
        effective_k = min(NUM_HEAVY * FETCH_K_RATIO, n)
        scores = coor_descent(s, N_ITERS, effective_k, EPS)
        selected_scores, selected_indices = jax.lax.top_k(scores, NUM_HEAVY)
        selected_scores = selected_scores + jax.lax.stop_gradient(1.0 - selected_scores)
        routed = jnp.take_along_axis(x, selected_indices[..., None], axis=1)
        routed_out = feedforward(routed, gamma_h, w1_h, b1_h, w2_h, b2_h)
        routed_out = routed_out * selected_scores[..., None]
        batch_range = jnp.arange(b)[:, None]
        heavy_out = jnp.zeros_like(x).at[batch_range, selected_indices].set(routed_out)
        return light_out + heavy_out

    def _L3_attn_ref(x, Wqkv, Wout):
        import jax, jax.numpy as jnp
        import numpy as np
        B, T, D, H = (4, 256, 128, 16)
        HEAD_DIM = D // H
        LOCAL_WINDOW = 64

        def _rotate_half(t):
            t1, t2 = jnp.split(t, 2, axis=-1)
            return jnp.concatenate([-t2, t1], axis=-1)

        def _apply_rope(q, k):
            Tq, d = (q.shape[2], q.shape[3])
            half = d // 2
            theta = 1.0 / 10000.0 ** (jnp.arange(half, dtype=jnp.float32) / half)
            pos = jnp.arange(Tq, dtype=jnp.float32)
            freqs = pos[:, None] * theta[None, :]
            freqs = jnp.concatenate([freqs, freqs], axis=-1)
            cos = jnp.cos(freqs)[None, None]
            sin = jnp.sin(freqs)[None, None]
            q = q * cos + _rotate_half(q) * sin
            k = k * cos + _rotate_half(k) * sin
            return (q, k)
        Bx, Tx, C = x.shape
        h, d, w = (H, HEAD_DIM, LOCAL_WINDOW)
        qkv = x @ Wqkv
        q, k, v = jnp.split(qkv, 3, axis=-1)
        q = q.reshape(Bx, Tx, h, d).transpose(0, 2, 1, 3)
        k = k.reshape(Bx, Tx, h, d).transpose(0, 2, 1, 3)
        v = v.reshape(Bx, Tx, h, d).transpose(0, 2, 1, 3)
        q, k = _apply_rope(q, k)
        idx = jnp.arange(Tx)
        dist = idx[None, :] - idx[:, None]
        allowed = (dist <= 0) & (dist >= -(w - 1))
        scores = jnp.einsum('bhqd,bhkd->bhqk', q, k) / jnp.sqrt(jnp.float32(d))
        scores = jnp.where(allowed[None, None], scores, -jnp.inf)
        weights = jax.nn.softmax(scores, axis=-1)
        out = jnp.einsum('bhqk,bhkd->bhqd', weights, v)
        out = out.transpose(0, 2, 1, 3).reshape(Bx, Tx, C)
        return out @ Wout

    def _L3_ffn_ref(x, Wr, br, W1, b1, W2, b2):
        import jax, jax.numpy as jnp
        import numpy as np
        D_MODEL = 128
        D_FF = 512
        NUM_EXPERTS = 8
        B, N = (16, 128)
        scores = jnp.einsum('bh,he->be', x.mean(axis=1), Wr) + br
        top1 = jnp.argmax(scores, axis=-1)
        w1 = W1[top1]
        c1 = b1[top1]
        w2 = W2[top1]
        c2 = b2[top1]
        h = jax.nn.relu(jnp.einsum('bnh,bhf->bnf', x, w1) + c1[:, None, :])
        out = jnp.einsum('bnf,bfh->bnh', h, w2) + c2[:, None, :]
        return out
    x = L0_attn_x
    x = _layernorm(x + _L0_attn_ref(x, L0_attn_wq, L0_attn_bq, L0_attn_wk, L0_attn_bk, L0_attn_wv, L0_attn_bv, L0_attn_wo, L0_attn_bo), axis=-1)
    x = _layernorm(x + _L0_ffn_ref(x, L0_ffn_ln1_w, L0_ffn_ln2_w, L0_ffn_Wq, L0_ffn_Wk, L0_ffn_Wv, L0_ffn_Wo, L0_ffn_Wr, L0_ffn_Wg, L0_ffn_Wu, L0_ffn_Wd), axis=-1)
    x = _layernorm(x + _L1_attn_ref(x, L1_attn_Wq, L1_attn_Wk, L1_attn_Wv), axis=-1)
    x = _layernorm(x + _L1_ffn_ref(x, L1_ffn_router_weight, L1_ffn_e_bias, L1_ffn_gate_w, L1_ffn_up_w, L1_ffn_down_w, L1_ffn_sh_gate_w, L1_ffn_sh_up_w, L1_ffn_sh_down_w), axis=-1)
    x = _layernorm(x + _L2_attn_ref(x, L2_attn_W_in, L2_attn_b_in, L2_attn_k_dist_emb, L2_attn_v_dist_emb, L2_attn_W_out, L2_attn_b_out), axis=-1)
    x = _layernorm(x + _L2_ffn_ref(x, L2_ffn_routing_token, L2_ffn_gamma_l, L2_ffn_w1_l, L2_ffn_b1_l, L2_ffn_w2_l, L2_ffn_b2_l, L2_ffn_gamma_h, L2_ffn_w1_h, L2_ffn_b1_h, L2_ffn_w2_h, L2_ffn_b2_h), axis=-1)
    x = _layernorm(x + _L3_attn_ref(x, L3_attn_Wqkv, L3_attn_Wout), axis=-1)
    x = _layernorm(x + _L3_ffn_ref(x, L3_ffn_Wr, L3_ffn_br, L3_ffn_W1, L3_ffn_b1, L3_ffn_W2, L3_ffn_b2), axis=-1)
    return x

_drawn_inputs = setup_inputs


def setup_inputs(seed=0):
    import zlib

    import numpy as np

    out = dict(_drawn_inputs(seed))
    spreads = {'L1_ffn_e_bias': (0.0, 0.8),
     'L2_attn_b_in': (0.0, 0.1),
     'L2_attn_b_out': (0.0, 0.1),
     'L2_ffn_gamma_l': (1.0, 0.2),
     'L2_ffn_gamma_h': (1.0, 0.6)}
    factors = {'L0_attn_wq': 8.0,
     'L0_attn_bq': 8.0,
     'L0_attn_wk': 8.0,
     'L0_attn_bk': 8.0,
     'L0_attn_wv': 8.0,
     'L0_attn_bv': 7.227,
     'L0_attn_wo': 7.194,
     'L0_ffn_ln1_w': 8.0,
     'L0_ffn_ln2_w': 8.0,
     'L0_ffn_Wq': 8.0,
     'L0_ffn_Wk': 8.0,
     'L0_ffn_Wv': 8.0,
     'L0_ffn_Wo': 8.0,
     'L0_ffn_Wr': 8.0,
     'L0_ffn_Wg': 8.0,
     'L0_ffn_Wu': 8.0,
     'L0_ffn_Wd': 8.0,
     'L1_ffn_router_weight': 8.0,
     'L1_ffn_gate_w': 8.0,
     'L1_ffn_up_w': 7.352,
     'L1_ffn_down_w': 8.0,
     'L1_ffn_sh_gate_w': 7.716,
     'L1_ffn_sh_up_w': 7.57,
     'L1_ffn_sh_down_w': 8.0,
     'L2_attn_k_dist_emb': 42.275,
     'L2_attn_v_dist_emb': 8.0,
     'L2_ffn_b1_l': 3.382,
     'L2_ffn_b1_h': 8.0,
     'L2_ffn_b2_h': 6.608,
     'L3_attn_Wqkv': 4.65,
     'L3_attn_Wout': 4.734,
     'L3_ffn_b1': 2.766}
    for name, (base, spread) in spreads.items():
        noise = np.random.default_rng([zlib.crc32(name.encode()), seed]).standard_normal(out[name].shape)
        drawn = base * np.exp(spread * noise) if base else spread * noise
        out[name] = jnp.asarray(drawn.astype(out[name].dtype))
    for name, factor in factors.items():
        out[name] = (out[name] * factor).astype(out[name].dtype)
    return out
```

```python
import math
from contextlib import ExitStack

import concourse.bass as bass
from concourse import mybir

F32 = mybir.dt.float32
BF16 = mybir.dt.bfloat16
U32 = mybir.dt.uint32
ALU = mybir.AluOpType
ACT = mybir.ActivationFunctionType
AX = mybir.AxisListType

D = 128
SEQS, SEQ = 4, 1024
TILES = SEQS * SEQ // 128
QT = SEQ // 128
CHUNKS = TILES // 4
H, HD = 16, 8
SLOT = 64
PAIRS = 8
EPS = 1e-5
K_HEAVY = 128
K_EFF = 144.0


def columns(sizes):
    table, at = {}, 0
    for name, n in sizes:
        table[name] = (at, at + n)
        at += n
    return table, at


CF, CF_N = columns([("ident", 128), ("cos", 64), ("sin", 64), ("lt16", 256), ("lt8", 64), ("lt4", 16),
                    ("ones", 128), ("eps", 1), ("mean", 1), ("mhalf", 4), ("selb", 512)])
CB, CB_N = columns([("ident", 128), ("causal", 128), ("causalT", 128), ("behind", 64), ("behindT", 64),
                    ("winc", 128), ("wincT", 128), ("sel8", 1024), ("sel16", 1024), ("before", 128), ("ones", 128)])


def constants():
    import numpy as np

    f = np.zeros((128, CF_N), np.float32)
    b = np.zeros((128, CB_N), np.float32)
    p = np.arange(128)

    def put(m, table, name, rows, value):
        lo, hi = table[name]
        m[rows, lo:hi] = value

    every = slice(None)
    put(f, CF, "ident", every, np.eye(128))
    inv = (np.float32(1.0) / np.float32(10000.0) ** (np.arange(4, dtype=np.float32) / np.float32(4))).astype(np.float32)
    cos = np.zeros((128, 8, 8), np.float32)
    sin = np.zeros((128, 8, 8), np.float32)
    for t in range(8):
        ang = ((p + 128 * t).astype(np.float32)[:, None] * inv).astype(np.float32)
        cos[:, t, 0:4] = cos[:, t, 4:8] = np.cos(ang)
        sin[:, t, 0:4] = -np.sin(ang)
        sin[:, t, 4:8] = np.sin(ang)
    put(f, CF, "cos", every, cos.reshape(128, 64))
    put(f, CF, "sin", every, sin.reshape(128, 64))
    for n in (16, 8, 4):
        lt = (np.arange(n)[None, :] < np.arange(n)[:, None]).astype(np.float32)
        put(f, CF, f"lt{n}", every, lt.reshape(1, n * n))
    put(f, CF, "ones", every, 1.0)
    put(f, CF, "eps", every, EPS)
    put(f, CF, "mean", every, 1.0 / SEQ)
    put(f, CF, "mhalf", every, -0.5)
    put(f, CF, "selb", slice(0, 4), np.repeat(np.eye(4), 128, axis=1))

    neg = -1e30
    q, k = np.meshgrid(p, p, indexing="ij")
    causal = np.where(k <= q, 0.0, neg)
    window = np.where((k <= q) & (q - k <= 63), 0.0, neg)
    behind = np.where(q + 128 - k <= 63, 0.0, neg)
    put(b, CB, "ident", every, np.eye(128))
    put(b, CB, "causal", every, causal)
    put(b, CB, "causalT", every, causal.T)
    put(b, CB, "behind", every, behind[:, 64:])
    put(b, CB, "behindT", every, behind.T[:, :64])
    put(b, CB, "winc", every, window)
    put(b, CB, "wincT", every, window.T)
    sel8 = np.zeros((24, 8, 128), np.float32)
    sel16 = np.zeros((48, 8, 128), np.float32)
    for part in range(3):
        for e in range(8):
            sel8[part * 8 + e, e, :] = 1
            sel16[part * 16 + 2 * e, e, 0:64] = 1
            sel16[part * 16 + 2 * e + 1, e, 64:128] = 1
    put(b, CB, "sel8", slice(0, 24), sel8.reshape(24, 1024))
    put(b, CB, "sel16", slice(0, 48), sel16.reshape(48, 1024))
    put(b, CB, "before", every, p[None, :] < p[:, None])
    put(b, CB, "ones", every, 1.0)
    return f, b


def program(nc, a, out):
    ctx = ExitStack()
    with ctx:
        def sb(name, shape, dt=F32):
            return ctx.enter_context(nc.sbuf_tensor(name, shape, dt))

        sems = {}

        def S(name):
            if name not in sems:
                sems[name] = ctx.enter_context(nc.semaphore(name))
            return sems[name]

        V, P, T, A = nc.vector, nc.gpsimd, nc.tensor, nc.scalar

        ps = ctx.enter_context(nc.psum_tensor("ps", [128, 8, 512], F32))
        cf = sb("cf", [128, CF_N])
        cb = sb("cb", [128, CB_N], BF16)

        def F(name, rows=128):
            return cf[0:rows, CF[name][0]:CF[name][1]]

        def B(name, rows=128):
            return cb[0:rows, CB[name][0]:CB[name][1]]

        ident, identb = F("ident"), B("ident")
        ones_row = F("ones", 1)

        def bank(i):
            return ps[:, i, :]

        def bank_bf(i):
            return ps[:, i, :].bitcast(BF16)

        def flat(ap):
            return ap.rearrange("p t d -> p (t d)")

        x = sb("x", [128, TILES, D])
        xT = sb("xT", [128, TILES * 128])
        y = sb("y", [128, 2, 4, D])
        stats = sb("stats", [128, 2, 4, 6])
        mv = sb("mv", [128, 2, 4, 2])
        ve = sb("ve", [128, 2, 4])
        rs = sb("rs", [128, 2, 4])

        w1T = sb("w1T", [128, 4, 128])
        w3T = w1T[:, 0:3, :]
        brow = sb("brow", [1, 512])
        b1 = brow[:]
        fb2 = brow[:, 0:256].rearrange("p (a n) -> p a n", a=2)
        b8b2 = brow[:, 256:512].rearrange("p (a n) -> p a n", a=2)
        w2 = sb("w2", [128, 192])
        w2o = sb("w2o", [128, 128])
        ln12 = sb("ln12", [128, 2])
        w2r = sb("w2r", [128, 8])
        w2x = sb("w2x", [128, 6144])
        w2g = w2x[:, 0:2048].rearrange("p (e f) -> p e f", e=8)
        w2u = w2x[:, 2048:4096].rearrange("p (e f) -> p e f", e=8)
        w2d = w2x[:, 4096:6144].rearrange("p (e f) -> p e f", e=16)
        w5n = w2x[:, 0:3072].rearrange("p (a b) -> p a b", a=24)
        w5on = w2x[:, 3072:4096].rearrange("p (a b) -> p a b", a=8)
        w6x = w2x[:, 4096:6144].rearrange("p (a b) -> p a b", b=128)
        f1hn, f2hn, f1hT, f2hT = w6x[:, 0:4, :], w6x[:, 4:8, :], w6x[:, 8:12, :], w6x[:, 12:16, :]
        w8a = w2x[:, 0:1024].rearrange("p (b n) -> p b n", b=2)
        w8b = w2x[:, 1024:2048].rearrange("p (b c n) -> p b c n", b=2, c=4)
        w3 = sb("w3", [128, 3, 128])
        w4r = sb("w4r", [16, 128])
        w4rT = sb("w4rT", [128, 16])
        ebias = sb("ebias", [128, 16])
        kdb = sb("kdb", [128, 8])
        vdb = sb("vdb", [128, 128])
        b5q = sb("b5q", [128, 8])
        qk5 = sb("qk5", [128, 64])
        rb5 = sb("rb5", [1, 64])
        vw5 = sb("vw5", [64, 128])
        b5o = sb("b5o", [1, 128])
        rt = sb("rt", [128, 4, 4])
        gam = sb("gam", [128, 2])
        f1ln = sb("f1ln", [64, 128])
        f1lT = sb("f1lT", [128, 64])
        f2ln = sb("f2ln", [128, 64])
        f2lT = sb("f2lT", [64, 128])
        fb1l = sb("fb1l", [64, 1])
        fb1h = sb("fb1h", [128, 4])
        w7 = sb("w7", [128, 384])
        w7o = sb("w7o", [128, 128])
        w8r = sb("w8r", [128, 8])
        b8r = sb("b8r", [1, 8])
        b8b1 = sb("b8b1", [128, 2, 4])

        heads = sb("heads", [128, 4, 64, HD])
        qf, kf, qr, kr = heads[:, 0], heads[:, 1], heads[:, 2], heads[:, 3]
        parts = sb("parts", [128, 6, 64, HD], BF16)
        qp, kp = parts[:, 0:3], parts[:, 3:6]
        stacks = sb("stacks", [128, 2, 64, SLOT], BF16)
        qstack, kstack = stacks[:, 0], stacks[:, 1]
        turned = sb("turned", [128, 2, PAIRS, SEQ], BF16)
        qT, kT = turned[:, 0], turned[:, 1]
        norm2 = sb("norm2", [128, 2, 64])
        norm2r = sb("norm2r", [128, 2, 64])
        norm2p = sb("norm2p", [128, 2, 3, 64], BF16)
        v1 = sb("v1", [128, QT, H, HD + 1])
        v1g = sb("v1g", [128, QT, 4, HD + 1])
        nm = sb("nm", [128, 64])
        nmr = sb("nmr", [128, 64])
        m2 = sb("m2", [128, 16])
        orec = sb("orec", [128, 4, H])
        on = sb("on", [128, 4, D])
        oT = sb("oT", [128, 512])
        pTr = sb("pTr", [128, 2, QT, 128])
        obuf = sb("obuf", [128, 2, 512])
        w1 = pTr[:, 0, 0:4, :]
        hf = heads[:].rearrange("p a n d -> p (a n d)")
        sf = stacks[:].rearrange("p a n s -> p (a n s)").bitcast(F32)
        q3T, k3T = sf[:, 0:1024], sf[:, 1024:2048]
        v3 = sf[:, 2048:3072].rearrange("p (t d) -> p t d", t=QT)
        tf = turned[:].rearrange("p a b c -> p (a b c)").bitcast(F32)
        w4n = tf[:, 0:3456].rearrange("p (a b) -> p a b", a=27)
        w4T = tf[:, 3456:6912].rearrange("p (a b) -> p a b", a=27)
        w5T = tf[:, 0:3072]
        w5oT = tf[:, 3072:4096].rearrange("p (a b) -> p a b", a=8)
        b5row = parts[0:3].rearrange("p a n d -> p (a n d)")

        big = sb("big", [128, 8192])
        b5f = big[0:1, 0:3072]
        b5p = big[0:1, 3072:7680].bitcast(BF16).rearrange("p (a n) -> p a n", a=3)
        RING = 8
        cb32 = big[:, 0:CB_N]
        ring = big[:].rearrange("p (r k) -> p r k", r=RING)
        pT2 = big[:, 0:3072].rearrange("p (u k q) -> p u k q", u=3, k=2)
        hx = big[:, 3072:3584].rearrange("p (t d) -> p t d", t=4)
        h1 = big[:, 3584:4096].rearrange("p (t d) -> p t d", t=4)
        hT = big[:, 4096:4608]
        hT2 = hT
        junk = big[:, 4608:5120].rearrange("p (t d) -> p t d", t=4)
        rot = big[:, 4608:5632].rearrange("p (a n d) -> p a n d", a=2, d=HD)
        gt, eq = big[:, 0:1024], big[:, 1024:2048]
        sil = big[:, 0:1536].rearrange("p (a n) -> p a n", a=3)
        t1 = big[:, 1536:3072].rearrange("p (a n) -> p a n", a=3)
        act = big[:, 4608:6144].rearrange("p (a n) -> p a n", a=3)
        cbs = big[:, 6144:7168].rearrange("p (a n) -> p a n", a=2)
        lg = sb("lg", [128, 4, 16])
        lgm = sb("lgm", [128, 4])
        lge = sb("lge", [128, 4, 16])
        rk = sb("rk", [128, 64])
        msk = sb("msk", [128, 64])
        cw = sb("cw", [128, 4, 16])
        cwr = sb("cwr", [128, 4, 16])
        csum = sb("csum", [128, 4])
        crec = sb("crec", [128, 4])
        ssq = sb("ssq", [128, 4])
        cpart = sb("cpart", [128, 4, 48], BF16)
        cT = sb("cT", [48, 512], BF16)
        top8 = sb("top8", [1, 4, 8])
        top_idx = sb("top_idx", [1, 4, 8], U32)
        sc8 = sb("sc8", [1, 4, 8])

        block = ctx.enter_context(nc.Block())

        @block.sync
        def _(sp):
            loaded = {}

            def load(dst, src, name):
                sp.dma_start(dst, src).then_inc(S(name), 16)
                loaded[name] = loaded.get(name, 0) + 16

            def column(v):
                return v.rearrange("(p o) -> p o", o=1)

            def row(v):
                return v.rearrange("(o d) -> o d", o=1)

            xin = a["L0_attn_x"].rearrange("b (q p) d -> p (b q) d", p=128)
            load(cf[:], a["const_f"], "ld_cf")
            load(x[:, 0:8, :], xin[:, 0:8, :], "ld_x0")
            for i, w in enumerate(("wq", "wk", "wv", "wo")):
                load(w1[:, i, :], a[f"L0_attn_{w}"], "ld_w1")
            for i, w in enumerate(("bq", "bk", "bv", "bo")):
                load(b1[:, 128 * i:128 * (i + 1)], row(a[f"L0_attn_{w}"]), "ld_w1")
            load(cb32, a["const_b"], "ld_cb")
            for b in range(1, 4):
                load(x[:, 8 * b:8 * b + 8, :], xin[:, 8 * b:8 * b + 8, :], f"ld_x{b}")
            wq = a["L0_ffn_Wq"].rearrange("k (g p r d) -> k g p r d", g=2, p=2, r=4)
            for g in range(2):
                for p in range(2):
                    dst = w2[:, 64 * g:64 * g + 64].rearrange("k (r p d) -> k r p d", r=4, p=2)[:, :, p, :]
                    load(dst, wq[:, g, p], "ld_w2")
            load(w2[:, 128:160], a["L0_ffn_Wk"], "ld_w2")
            load(w2[:, 160:192], a["L0_ffn_Wv"], "ld_w2")
            load(w2o[:], a["L0_ffn_Wo"], "ld_w2")
            load(ln12[:, 0:1], column(a["L0_ffn_ln1_w"]), "ld_w2")
            load(ln12[:, 1:2], column(a["L0_ffn_ln2_w"]), "ld_w2")
            load(w2r[:], a["L0_ffn_Wr"], "ld_w2")
            for i, w in enumerate(("Wq", "Wk", "Wv")):
                load(w3[:, i, :], a[f"L1_attn_{w}"], "ld_w3")
            load(w4r[:], a["L1_ffn_router_weight"], "ld_w4r")
            load(ebias[:], row(a["L1_ffn_e_bias"]).to_broadcast([128, 16]), "ld_w4r")
            sp.wait_ge(S("const_zero"), 1)
            for half in range(2):
                rows = slice(64 * half, 64 * half + 64)
                for r in range(4):
                    load(kdb[rows, 4 * half + r:4 * half + r + 1], column(a["L2_attn_k_dist_emb"][r, :]), "ld_w5s")
                    at = 60 + 4 * half + r
                    load(vdb[rows, at:at + 1], column(a["L2_attn_v_dist_emb"][r, :]), "ld_w5s")
            for c in range(8):
                load(b5q[:, c:c + 1], column(a["L2_attn_b_in"][128 * c:128 * c + 128]), "ld_w5s")
            load(b5o[:], row(a["L2_attn_b_out"]), "ld_w5s")
            for r in range(4):
                load(rt[:, r, r:r + 1], column(a["L2_ffn_routing_token"]), "ld_w6")
            for i, g in enumerate(("l", "h")):
                load(gam[:, i:i + 1], column(a[f"L2_ffn_gamma_{g}"]), "ld_w6")
            load(f1ln[:], a["L2_ffn_w1_l"], "ld_w6")
            load(f2ln[:], a["L2_ffn_w2_l"], "ld_w6")
            load(fb1l[:], column(a["L2_ffn_b1_l"]), "ld_w6")
            for c in range(4):
                load(fb1h[:, c:c + 1], column(a["L2_ffn_b1_h"][128 * c:128 * c + 128]), "ld_w6")
            load(w7[:], a["L3_attn_Wqkv"], "ld_w7")
            load(w7o[:], a["L3_attn_Wout"], "ld_w7")
            load(w8r[:], a["L3_ffn_Wr"], "ld_w8r")
            load(b8r[:], row(a["L3_ffn_br"]), "ld_w8r")
            sp.wait_ge(S("l1_pT_ps"), 2 * SEQS * QT * H)
            load(w2g, a["L0_ffn_Wg"].rearrange("e d f -> d e f"), "ld_w2x")
            load(w2u, a["L0_ffn_Wu"].rearrange("e d f -> d e f"), "ld_w2x")
            for j in range(2):
                load(w2d.rearrange("f (e j) d -> f e j d", j=2)[:, :, j, :],
                     a["L0_ffn_Wd"].rearrange("e (j f) d -> f e j d", f=128)[:, :, j, :], "ld_w2x")
            sp.wait_ge(S("ln_x"), 4 * 16)
            for i, g in enumerate(("l", "h")):
                load(fb2[:, i, :], row(a[f"L2_ffn_b2_{g}"]), "ld_w6h")
            load(w4n[:, 0:8, :], a["L1_ffn_gate_w"].rearrange("(g e) i h -> (e i) g h", e=2), "ld_w4")
            load(w4n[:, 8, :], a["L1_ffn_sh_gate_w"], "ld_w4")
            load(w4n[:, 9:17, :], a["L1_ffn_up_w"].rearrange("(g e) i h -> (e i) g h", e=2), "ld_w4")
            load(w4n[:, 17, :], a["L1_ffn_sh_up_w"], "ld_w4")
            for e2 in range(2):
                load(w4n[:, 18:26, 64 * e2:64 * e2 + 64],
                     a["L1_ffn_down_w"].rearrange("(g e) h i -> h g e i", e=2)[:, :, e2, :], "ld_w4")
            load(w4n[:, 26, :], a["L1_ffn_sh_down_w"], "ld_w4")
            for i in range(3):
                load(w5n[:, 8 * i:8 * i + 8, :],
                     a["L2_attn_W_in"][1024 * i:1024 * i + 1024, :].rearrange("(c p) d -> p c d", p=128), "ld_w5")
            load(w5on, a["L2_attn_W_out"].rearrange("o (c p) -> o c p", p=128), "ld_w5")
            load(f1hn, a["L2_ffn_w1_h"].rearrange("(c p) d -> p c d", p=128), "ld_w6h")
            load(f2hn, a["L2_ffn_w2_h"].rearrange("o (c p) -> o c p", p=128), "ld_w6h")
            sp.wait_ge(S("ln_x"), 4 * 32)
            load(b5f, row(a["L2_attn_b_in"]), "ld_b5")
            sp.wait_ge(S("l5_b5p"), 1)
            for j in range(3):
                load(b5row[j:j + 1, :], b5p[:, j, :], "ld_b5row")
            sp.wait_ge(S("l8_top"), 4)
            for b in range(SEQS):
                if b >= 2:
                    sp.wait_ge(S("ln_x"), 4 * (7 * CHUNKS + 2 * (b - 1)))
                chosen = sp.value_load(top_idx[0:1, b, 0:1], min_val=0, max_val=7)
                one = bass.ds(chosen, 1)
                load(w8a[:, b % 2, :], a["L3_ffn_W1"][one].rearrange("e p n -> (e p) n"), f"ld_w8e{b}")
                for k in range(4):
                    load(b8b1[:, b % 2, k:k + 1],
                         a["L3_ffn_b1"][one][:, 128 * k:128 * k + 128].rearrange("e (p o) -> (e p) o", o=1),
                         f"ld_w8e{b}")
                load(w8b[:, b % 2, :, :], a["L3_ffn_W2"][one].rearrange("e (c p) n -> p (e c) n", p=128),
                     f"ld_w8e{b}")
                load(b8b2[:, b % 2, :], a["L3_ffn_b2"][one], f"ld_w8e{b}")
            o_dram = out.rearrange("b (q p) d -> p (b q) d", p=128)
            for c in range(CHUNKS):
                sp.wait_ge(S("ln_x"), 4 * (7 * CHUNKS + c + 1))
                sp.dma_start(o_dram[:, 4 * c:4 * c + 4, :], x[:, 4 * c:4 * c + 4, :]).then_inc(S("stored"), 16)
            sp.wait_ge(S("stored"), 16 * CHUNKS)
            for name, count in loaded.items():
                sp.wait_ge(S(name), count)

        class Chain:

            def __init__(self, eng, sem):
                self.eng, self.sem, self.n = eng, sem, 0

            def __call__(self, ins):
                ins.then_inc(self.sem, 1)
                self.n += 1

            def wait(self):
                self.eng.wait_ge(self.sem, self.n)

        def chunk_tiles(n, c):
            return range(c, 32, 8) if n == 5 else range(4 * c, 4 * c + 4)

        def xs(n, c):
            return x[:, c:32:8, :] if n == 5 else x[:, 4 * c:4 * c + 4, :]

        def xTs(n, c):
            if n == 5:
                return xT[:].rearrange("p (s q t) -> p s q t", s=4, q=8)[:, :, c, :]
            return xT[:, 512 * c:512 * c + 512].rearrange("p (s t) -> p s t", s=4)

        def ln_vector(e, step, n, c):
            k, h = (n - 1) * CHUNKS + c, c % 2
            step.wait()
            for t in range(4):
                step(V.bn_stats(stats[:, h, t, :], y[:, h, t, :]))
            step.wait()
            for t in range(4):
                V.bn_aggr(mv[:, h, t, :], stats[:, h, t, :]).then_inc(S("ln_var"), 1)
            e.wait_ge(S("ln_rs"), k + 1)
            for t, tile in enumerate(chunk_tiles(n, c)):
                V.tensor_scalar(x[:, tile, :], y[:, h, t, :], mv[:, h, t, 0:1], rs[:, h, t:t + 1],
                                ALU.subtract, ALU.mult).then_inc(S("ln_x"), 1)

        def ln_gpsimd(e, step, n, c):
            k, h = (n - 1) * CHUNKS + c, c % 2
            e.wait_ge(S("ln_var"), 4 * (k + 1))
            step(P.tensor_scalar(ve[:, h, :], mv[:, h, :, 1], EPS, None, ALU.add))
            step.wait()
            P.tensor_tensor(rs[:, h, :], ve[:, h, :], F("mhalf"), ALU.pow).then_inc(S("ln_rs"), 1)

        def xT_tensor(e, n, c, b):
            k = (n - 1) * CHUNKS + c
            e.wait_ge(S("ln_x"), 4 * (k + 1))
            for t, tile in enumerate(chunk_tiles(n, c)):
                mm = T.transpose(ps[:, b, 128 * t:128 * (t + 1)], x[:, tile, :], ident)
            mm.then_inc(S("xT_ps"), 1)

        def xT_scalar(e, n, c, b):
            k = (n - 1) * CHUNKS + c
            e.wait_ge(S("xT_ps"), k + 1 + CHUNKS)
            A.activation(xTs(n, c), bank(b).rearrange("p (s t) -> p s t", s=4), ACT.Copy).then_inc(S("xT"), 1)

        def x0T_tensor(e, c, b):
            e.wait_ge(S(f"ld_x{c // 2}"), 16)
            for t in range(4):
                mm = T.transpose(ps[:, b, 128 * t:128 * (t + 1)], x[:, 4 * c + t, :], ident)
            mm.then_inc(S("xT_ps"), 1)

        def x0T_scalar(e, c, b):
            e.wait_ge(S("xT_ps"), c + 1)
            A.activation(xT[:, 512 * c:512 * c + 512], bank(b), ACT.Copy).then_inc(S("xT"), 1)

        def xT_ready(n, c):
            return (n - 1) * CHUNKS + c + 1

        def split_parts(step, eng, src, parts, res, n, name=None):
            step(eng.tensor_copy(parts[:, 0, 0:n, :], src[:, 0:n, :]))
            step.wait()
            step(eng.tensor_tensor(res[:, 0:n, :], src[:, 0:n, :], parts[:, 0, 0:n, :], ALU.subtract))
            step.wait()
            step(eng.tensor_copy(parts[:, 1, 0:n, :], res[:, 0:n, :]))
            step.wait()
            last = eng.tensor_tensor(parts[:, 2, 0:n, :], res[:, 0:n, :], parts[:, 1, 0:n, :], ALU.subtract)
            if name:
                last.then_inc(S(name), 1)
            else:
                step(last)

        Q_SLOTS = [(0, 0, 3, 1), (1, 3, 2, 1), (2, 5, 1, 1)]
        K_SLOTS = [(0, 0, 2, 3), (0, 5, 1, 1), (1, 1, 2, 3), (2, 2, 1, 1)]

        def fill_slots(step, eng, parts, stack, n, slots):
            step.wait()
            for part, first, count, stride in slots:
                src = parts[:, part, 0:n, :]
                if count == 1:
                    step(eng.tensor_copy(stack[:, 0:n, 8 * first:8 * first + 8], src))
                else:
                    dst = stack[:, 0:n, 0:48].rearrange("p n (s d) -> p n s d", d=8)
                    dst = dst[:, :, first:first + stride * (count - 1) + 1:stride, :]
                    step(eng.tensor_copy(dst, src.unsqueeze(2).to_broadcast([128, n, count, 8])))

        def fill_keys_scalar(e, n, name):
            for part, first, count, stride in K_SLOTS:
                src = kp[:, part, 0:n, :]
                if count == 1:
                    dst = kstack[:, 0:n, 8 * first:8 * first + 8]
                else:
                    dst = kstack[:, 0:n, 0:48].rearrange("p n (s d) -> p n s d", d=8)
                    dst = dst[:, :, first:first + stride * (count - 1) + 1:stride, :]
                    src = src.unsqueeze(2).to_broadcast([128, n, count, 8])
                A.activation(dst, src, ACT.Copy).then_inc(S(name), 1)

        def stack_transposes(e, stack, heads, name, i, b):
            groups = heads // 4
            for g in range(groups):
                if g or i:
                    e.wait_ge(S(f"{name}_sb"), groups * i + g)
                for pair in range(2):
                    for t in range(4):
                        h = t * heads + 4 * g + 2 * pair
                        col = 512 * pair + 128 * t
                        mm = T.transpose(bank_bf(b)[:, col:col + 128],
                                         stack[:, h:h + 2, :].rearrange("p h s -> p (h s)"), identb)
                mm.then_inc(S(f"{name}_ps"), 1)

        def stack_evac(e, copy, dst, heads, name, i, b, half):
            groups = heads // 4
            for g in range(groups):
                e.wait_ge(S(f"{name}_ps"), groups * i + g + 1)
                copy(dst[:, 2 * g:2 * g + 2, 512 * half:512 * half + 512],
                     bank_bf(b).rearrange("p (a b) -> p a b", a=2)).then_inc(S(f"{name}_sb"), 1)

        def act_copy(o, i):
            return A.activation(o, i, ACT.Copy)

        def narrow_name(n, what):
            return f"l1_{what}" if n == 1 else f"nr_{what}"

        def narrow_chunk(n, c):
            return c + CHUNKS if n == 7 else c

        def finish_tensor(e, n, c, wo, bias, bt, bo):
            e.wait_ge(S(narrow_name(n, "on")), 4 * (narrow_chunk(n, c) + 1))
            for t in range(4):
                mm = T.transpose(ps[:, bt, 128 * t:128 * (t + 1)], on[:, t, :], ident)
            mm.then_inc(S(narrow_name(n, "oT_ps")), 1)
            e.wait_ge(S(narrow_name(n, "oT")), narrow_chunk(n, c) + 1)
            for t in range(4):
                dst = ps[:, bo, 128 * t:128 * (t + 1)]
                mm = T.matmul(dst, oT[:, 128 * t:128 * (t + 1)], wo, start=True, stop=bias is None)
                if bias is not None:
                    mm = T.matmul(dst, ones_row, bias, start=False, stop=True)
            mm.then_inc(S(narrow_name(n, "out")), 1)

        def finish_scalar(e, n, c, bt):
            e.wait_ge(S(narrow_name(n, "oT_ps")), narrow_chunk(n, c) + 1)
            A.activation(oT[:], bank(bt), ACT.Copy).then_inc(S(narrow_name(n, "oT")), 1)

        def normalise_vector(e, step, n, t, o):
            step(V.reciprocal(orec[:, t, :], o[:, :, 8]))
            step.wait()
            V.tensor_tensor(on[:, t, :].rearrange("p (h d) -> p h d", h=H), o[:, :, 0:8],
                            orec[:, t, :].unsqueeze(2).to_broadcast([128, H, 8]), ALU.mult)\
                .then_inc(S(narrow_name(n, "on")), 1)

        def residual_vector(e, step, n, c, b):
            V_y = flat(y[:, c % 2])
            if n == 5:
                step(V.tensor_tensor(y[:, c % 2], bank(b).rearrange("p (t d) -> p t d", t=4), xs(n, c), ALU.add))
            else:
                step(V.tensor_tensor(V_y, bank(b), flat(xs(n, c)), ALU.add))

        BATCH = 4
        ROWS = QT * H
        FINISH = ROWS // 2 + 2 * BATCH - 1

        RING1 = 8

        def ring1(i):
            place = i % RING1
            return ring[:, place, :] if place < RING else w2x[:, 1024 * (place - RING):1024 * (place - RING + 1)]

        def row_of(r):
            return r // H, (r % H) // 2, r % 2

        def l1_tensor(e):
            e.wait_ge(S("ld_cf"), 16)
            e.wait_ge(S("ld_w1"), 128)
            for i in range(4):
                mm = T.transpose(ps[:, 7, 128 * i:128 * (i + 1)], w1[:, i, :], ident)
            mm.then_inc(S("wT_ps"), 1)
            for c in range(2):
                x0T_tensor(e, c, 4 + c)

            def prep(c):
                e.wait_ge(S("xT"), xT_ready(1, c))
                e.wait_ge(S("wT"), 1)
                if c >= 1:
                    e.wait_ge(S("l1_qkv_sb"), 3 * c)
                if c % 2 == 0 and c:
                    e.wait_ge(S("l1_clamped"), ROWS * (c // 2))
                for t in range(4):
                    T.matmul(ps[:, t, 0:384], xT[:, 512 * c + 128 * t:512 * c + 128 * (t + 1)],
                             flat(w1T[:, 0:3, :]), start=True, stop=False)
                    mm = T.matmul(ps[:, t, 0:384], ones_row, b1[:, 0:384], start=False, stop=True)
                mm.then_inc(S("l1_qkv"), 1)
                e.wait_ge(S("cb_ready"), 1)
                e.wait_ge(S("l1_kstack"), 5 * (c + 1))
                if c % 2 == 0 and c:
                    e.wait_ge(S("l1_pT_sb"), 2 * ROWS * (c // 2))
                if c == 0:
                    e.wait_ge(S("xT"), 2)
                stack_transposes(e, kstack, H, "l1_kT", c, 4)
                e.wait_ge(S("l1_qstack"), c + 1)
                stack_transposes(e, qstack, H, "l1_qT", c, 5)

            def scores(b, r):
                qt, pair, p = row_of(r)
                i = ROWS * b + r
                if r >= 2:
                    e.wait_ge(S("l1_clamped"), i - 1)
                rows = slice(64 * p, 64 * p + 64)
                for half in range(2):
                    mm = T.matmul(bank(2 * p + half), qT[rows, pair, 128 * qt:128 * qt + 128],
                                  kT[rows, pair, 512 * half:512 * half + 512], start=True, stop=True)
                mm.then_inc(S("l1_d2"), 1)

            def turn(b, r):
                i = ROWS * b + r
                e.wait_ge(S("l1_prob"), i + 1)
                for half in range(2):
                    if i:
                        e.wait_ge(S("l1_pT_sb"), 2 * i - 1 + half)
                    for k in range(4):
                        kt = 4 * half + k
                        mm = T.transpose(ps[:, 4 + half, 128 * k:128 * k + 128],
                                         ring1(i)[:, 128 * kt:128 * kt + 128], ident)
                    mm.then_inc(S("l1_pT_ps"), 1)

            def values(b, r):
                qt, pair, p = row_of(r)
                i = ROWS * b + r
                e.wait_ge(S("l1_pT_sb"), 2 * (i + 1))
                if r % H == 0 and i:
                    e.wait_ge(S("ob"), i // H)
                h = 2 * pair + p
                dst = ps[32 * (h % 4):32 * (h % 4) + HD + 1, 6, 128 * (h // 4):128 * (h // 4) + 128]
                for kt in range(QT):
                    mm = T.matmul(dst, v1[:, kt, h, :], pTr[:, i % 2, kt, :], start=kt == 0, stop=kt == QT - 1)
                mm.then_inc(S("l1_pv"), 1)

            def turn_outputs(tile):
                e.wait_ge(S("ob"), tile + 1)
                if tile:
                    e.wait_ge(S("l1_on"), tile)
                if tile % 4 == 0 and tile:
                    e.wait_ge(S("l1_y"), tile // 4)
                for g in range(4):
                    mm = T.transpose(ps[:, 7, 128 * g:128 * g + 128], obuf[:, 0, 128 * g:128 * g + 128], ident)
                mm.then_inc(S("ob_turned"), 1)

            for b in range(SEQS):
                prep(2 * b)
                prep(2 * b + 1)
                e.wait_ge(S("l1_kT_sb"), 8 * (b + 1))
                e.wait_ge(S("l1_qT_sb"), 8 * (b + 1))
                e.wait_ge(S("l1_qkv_sb"), 6 * (b + 1))
                for r in range(RING1):
                    scores(b, r)
                for r in range(ROWS + 1):
                    if r > H and r % H == 1:
                        turn_outputs(QT * b + r // H - 1)
                    if r < ROWS:
                        turn(b, r)
                    if r:
                        values(b, r - 1)
                    if r + RING1 < ROWS:
                        scores(b, r + RING1)
                    if r == FINISH:
                        finish_tensor(e, 1, 2 * b, w1T[:, 3, :], b1[:, 384:512], 7, 7)
                turn_outputs(QT * b + QT - 1)
                finish_tensor(e, 1, 2 * b + 1, w1T[:, 3, :], b1[:, 384:512], 7, 7)
                if b < SEQS - 1:
                    e.wait_ge(S("l1_y"), 2 * b + 2)
                    e.wait_ge(S("l1_pT_sb"), 2 * ROWS * (b + 1))
                    for c in range(2 * b + 2, 2 * b + 4):
                        x0T_tensor(e, c, 4 + c % 2)
            e.wait_ge(S("l1_pT_sb"), 2 * ROWS * SEQS)
            for c in range(CHUNKS):
                e.wait_ge(S("xT"), CHUNKS + c)
                xT_tensor(e, 1, c, 4)

        def l1_scalar(e):
            e.wait_ge(S("wT_ps"), 1)
            A.activation(flat(w1T[:]), bank(7), ACT.Copy).then_inc(S("wT"), 1)
            for c in range(2):
                x0T_scalar(e, c, 4 + c)
            view = "p (t h) d -> p t (h d)"
            for b in range(SEQS):
                for c in (2 * b, 2 * b + 1):
                    e.wait_ge(S("l1_qkv"), c + 1)
                    if c:
                        e.wait_ge(S("l1_kparts"), c)
                        e.wait_ge(S("l1_qstack"), c)
                    qkv = ps[:, 0:4, :]
                    A.activation(kf[:].rearrange(view, t=4), qkv[:, :, 128:256], ACT.Copy).then_inc(S("l1_qkv_sb"), 1)
                    A.activation(qf[:].rearrange(view, t=4), qkv[:, :, 0:128], ACT.Copy, scale=-2.0)\
                        .then_inc(S("l1_qkv_sb"), 1)
                    A.activation(v1[:, 4 * (c % 2):4 * (c % 2) + 4, :, 0:8],
                                 qkv[:, :, 256:384].rearrange("p t (h d) -> p t h d", d=8),
                                 ACT.Copy).then_inc(S("l1_qkv_sb"), 1)
                    e.wait_ge(S("l1_kparts"), c + 1)
                    if c:
                        e.wait_ge(S("l1_kT_ps"), 4 * c)
                    fill_keys_scalar(e, 64, "l1_kstack")
                    stack_evac(e, act_copy, kT, H, "l1_kT", c, 4, c % 2)
                for g in range(ROWS // BATCH):
                    i0 = ROWS * b + BATCH * g
                    for i in range(i0, i0 + BATCH):
                        e.wait_ge(S("l1_clamped"), i + 1)
                        A.activation(ring1(i), ring1(i), ACT.Sqrt).then_inc(S("l1_dist"), 1)
                    mins = m2[:, i0 % 16:i0 % 16 + BATCH]
                    A.activation(mins, mins, ACT.Sqrt).then_inc(S("l1_dist"), 1)
                    for i in range(i0, i0 + BATCH):
                        if i == i0:
                            e.wait_ge(S("l1_dist"), (BATCH + 1) * (i0 // BATCH + 1))
                        A.activation(ring1(i), ring1(i), ACT.Exp,
                                     bias=m2[:, i % 16:i % 16 + 1], scale=-1.0).then_inc(S("l1_prob"), 1)
                    if (g + 1) * BATCH == FINISH + 1:
                        finish_scalar(e, 1, 2 * b, 7)
                finish_scalar(e, 1, 2 * b + 1, 7)
                if b < SEQS - 1:
                    for c in range(2 * b + 2, 2 * b + 4):
                        x0T_scalar(e, c, 4 + c % 2)
            for c in range(CHUNKS):
                xT_scalar(e, 1, c, 4)

        def l1_gpsimd(e, step):
            step(P.memset(rt[:], 0.0))
            step(P.memset(kdb[:], 0.0))
            step(P.memset(v1[:, :, :, 8:9], 1.0))
            step(P.memset(v1g[:, :, :, 8:9], 1.0))
            step.wait()
            P.memset(vdb[:], 0.0).then_inc(S("const_zero"), 1)
            step(P.memset(kstack[:, :, 54:64], 0.0))
            step(P.memset(kstack[:, :, 48:51], 1.0))
            step(P.memset(qstack[:, :, 51:54], 1.0))
            step.wait()
            P.memset(qstack[:, :, 54:64], 0.0).then_inc(S("l1_consts"), 1)
            for c in range(CHUNKS):
                e.wait_ge(S("l1_norm2"), c + 1)
                if c:
                    e.wait_ge(S("l1_kT_ps"), 4 * c)
                step.wait()
                P.tensor_copy(kstack[:, :, 51:54], norm2p[:, 1, :, :].rearrange("p r n -> p n r"))\
                    .then_inc(S("l1_kstack"), 1)
                if c % 2:
                    ln_gpsimd(e, step, 1, c - 1)
                    ln_gpsimd(e, step, 1, c)

        def l1_vector(e, step):
            def prep(c):
                e.wait_ge(S("l1_qkv_sb"), 3 * c + 2)
                if c:
                    e.wait_ge(S("l1_qT_ps"), 4 * c)
                    e.wait_ge(S("l1_kstack"), 5 * c)
                split_parts(step, V, kf, kp, kr, 64, "l1_kparts")
                step.wait()
                if c >= 2:
                    e.wait_ge(S("ln_x"), 4 * (c - c % 2))
                sq = y[:].rearrange("p a t (n d) -> p a (t n) d", d=HD)
                for i, (src, sc) in enumerate(((qf, 0.25), (kf, 1.0))):
                    step(V.scalar_tensor_tensor(sq[:, i], src[:], sc, src[:], ALU.mult, ALU.mult))
                step.wait()
                step(V.tensor_reduce(norm2[:], sq, AX.X, ALU.add))
                step.wait()
                step(V.tensor_copy(norm2p[:, :, 0, :], norm2[:]))
                step.wait()
                step(V.tensor_tensor(norm2r[:], norm2[:], norm2p[:, :, 0, :], ALU.subtract))
                step.wait()
                step(V.tensor_copy(norm2p[:, :, 1, :], norm2r[:]))
                step.wait()
                V.tensor_tensor(norm2p[:, :, 2, :], norm2r[:], norm2p[:, :, 1, :], ALU.subtract)\
                    .then_inc(S("l1_norm2"), 1)
                split_parts(step, V, qf, qp, qr, 64)
                fill_slots(step, V, qp, qstack, 64, Q_SLOTS)
                step.wait()
                e.wait_ge(S("l1_norm2"), c + 1)
                e.wait_ge(S("l1_consts"), 1)
                V.tensor_copy(qstack[:, :, 48:51], norm2p[:, 0, :, :].rearrange("p r n -> p n r"))\
                    .then_inc(S("l1_qstack"), 1)
                stack_evac(e, V.tensor_copy, qT, H, "l1_qT", c, 5, c % 2)

            def clamp(i):
                p = i % 2
                e.wait_ge(S("l1_d2"), i + 1)
                if i >= RING1:
                    e.wait_ge(S("l1_pT_ps"), 2 * (i - RING1 + 1))
                V.tensor_scalar(ring1(i), ps[:, 2 * p:2 * p + 2, :].rearrange("p a b -> p (a b)"),
                                1e-12, None, ALU.max, ALU.min, accum_out=m2[:, i % 16:i % 16 + 1])\
                    .then_inc(S("l1_clamped"), 1)

            def evac(i):
                for half in range(2):
                    e.wait_ge(S("l1_pT_ps"), 2 * i + half + 1)
                    if i >= 2:
                        e.wait_ge(S("l1_pv"), i - 1)
                    V.tensor_copy(pTr[:, i % 2, 4 * half:4 * half + 4, :].rearrange("p k q -> p (k q)"),
                                  bank(4 + half)).then_inc(S("l1_pT_sb"), 1)

            def take_outputs(t):
                e.wait_ge(S("l1_pv"), H * (t + 1))
                if t:
                    e.wait_ge(S("ob_turned"), t)
                V.tensor_copy(obuf[:, 0, :], bank(6)).then_inc(S("ob"), 1)

            def tile_done(t):
                e.wait_ge(S("ob_turned"), t + 1)
                if t % 4 == 0 and t:
                    e.wait_ge(S("l1_oT_ps"), t // 4)
                normalise_vector(e, step, 1, t % 4, bank(7).rearrange("p (h d) -> p h d", h=H))

            def chunk_done(c):
                e.wait_ge(S("l1_out"), c + 1)
                V.tensor_tensor(flat(y[:, c % 2]), bank(7), flat(xs(1, c)), ALU.add).then_inc(S("l1_y"), 1)
                e.wait_ge(S("l1_y"), c + 1)

            e.wait_ge(S("ld_cb"), 16)
            V.tensor_copy(cb[:], cb32).then_inc(S("cb_ready"), 1)
            step(V.memset(bank(6), 0.0))
            for b in range(SEQS):
                prep(2 * b)
                prep(2 * b + 1)
                base = ROWS * b
                for r in range(RING1):
                    clamp(base + r)
                for r in range(ROWS):
                    evac(base + r)
                    if r and r % H == 0:
                        take_outputs(QT * b + r // H - 1)
                    if r > H and r % H == 1:
                        tile_done(QT * b + r // H - 1)
                    if r + RING1 < ROWS:
                        clamp(base + r + RING1)
                    if r == FINISH + 1:
                        chunk_done(2 * b)
                take_outputs(QT * b + QT - 1)
                tile_done(QT * b + QT - 1)
                chunk_done(2 * b + 1)
                for c in (2 * b, 2 * b + 1):
                    ln_vector(e, step, 1, c)

        def after_chunk(e, n, c):
            e.wait_ge(S("ln_x"), 4 * ((n - 1) * CHUNKS + c))

        def after_turn(e, n, c):
            e.wait_ge(S("xT"), CHUNKS + (n - 1) * CHUNKS + c)

        def rms_vector(e, step, src, dst, name, c, factor=1.0):
            step.wait()
            for t in range(4):
                V.scalar_tensor_tensor(junk[:, t, :], src[:, t, :], 1.0, src[:, t, :], ALU.mult, ALU.mult,
                                       accum_out=ssq[:, t:t + 1]).then_inc(S(f"{name}_ss"), 1)
            e.wait_ge(S(f"{name}_r"), c + 1)
            for t in range(4):
                V.tensor_scalar(dst[:, t, :], src[:, t, :], crec[:, t:t + 1], factor, ALU.mult, ALU.mult)\
                    .then_inc(S(f"{name}_x"), 1)

        def rms_gpsimd(e, step, name, c, scale=1.0 / D, op=ALU.add, floor=EPS):
            e.wait_ge(S(f"{name}_ss"), 4 * (c + 1))
            step(P.tensor_scalar(csum[:], ssq[:], scale, floor, ALU.mult, op))
            step.wait()
            P.tensor_tensor(crec[:], csum[:], F("mhalf"), ALU.pow).then_inc(S(f"{name}_r"), 1)

        def turn_tensor(e, src, name, c, b):
            e.wait_ge(S(f"{name}_x"), 4 * (c + 1))
            for t in range(4):
                mm = T.transpose(ps[:, b, 128 * t:128 * (t + 1)], src[:, t, :], ident)
            mm.then_inc(S(f"{name}_T_ps"), 1)

        def rank_vector(step, src, n, E, k):
            g4 = gt[:, 0:n * E * E].rearrange("p (n e j) -> p n e j", n=n, e=E)
            q4 = eq[:, 0:n * E * E].rearrange("p (n e j) -> p n e j", n=n, e=E)
            by_j = src.unsqueeze(2).to_broadcast([128, n, E, E])
            by_e = src.unsqueeze(3).to_broadcast([128, n, E, E])
            step.wait()
            step(V.tensor_tensor(g4, by_j, by_e, ALU.is_gt))
            step(V.tensor_tensor(q4, by_j, by_e, ALU.is_equal))
            step.wait()
            q3 = eq[:, 0:n * E * E].rearrange("p (n f) -> p n f", n=n)
            step(V.tensor_tensor(q3, q3, F(f"lt{E}").unsqueeze(1).to_broadcast([128, n, E * E]), ALU.mult))
            step.wait()
            step(V.tensor_tensor(g4, g4, q4, ALU.add))
            step.wait()
            step(V.tensor_reduce(rk[:, 0:n * E].rearrange("p (n e) -> p n e", n=n), g4, AX.X, ALU.add))
            step.wait()
            step(V.tensor_scalar(msk[:, 0:n * E], rk[:, 0:n * E], float(k), None, ALU.is_lt))
            step.wait()

        def weights_vector(e, step, E, scale, tiny):
            c3 = cw[:, :, 0:E]
            part = cpart[:, :, 0:3 * E].rearrange("p t (a e) -> p t a e", a=3)
            step(V.tensor_reduce(csum[:], c3, AX.X, ALU.add))
            step.wait()
            if tiny:
                step(V.tensor_scalar(csum[:], csum[:], tiny, None, ALU.add))
                step.wait()
            step(V.reciprocal(crec[:], csum[:]))
            step.wait()
            step(V.tensor_tensor(c3, c3, crec[:].unsqueeze(2).to_broadcast([128, 4, E]), ALU.mult))
            step.wait()
            if scale != 1.0:
                step(V.tensor_scalar(c3, c3, scale, None, ALU.mult))
                step.wait()
            step(V.tensor_copy(part[:, :, 0, :], c3))
            step.wait()
            step(V.tensor_tensor(cwr[:, :, 0:E], c3, part[:, :, 0, :], ALU.subtract))
            step.wait()
            step(V.tensor_copy(part[:, :, 1, :], cwr[:, :, 0:E]))
            step.wait()
            V.tensor_tensor(part[:, :, 2, :], cwr[:, :, 0:E], part[:, :, 1, :], ALU.subtract)\
                .then_inc(S("ex_cpart"), 1)

        class Experts:
            def __init__(self, n, units, E, sel, weight_of, gate, up, down):
                self.n, self.units, self.E, self.sel, self.weight_of = n, units, E, sel, weight_of
                self.gate, self.up, self.down = gate, up, down
                self.chunk0, self.unit0, self.new0 = (CHUNKS, 16 * CHUNKS, 8 * CHUNKS) if n == 4 else (0, 0, 0)
                self.new = [u for u in range(units)
                            if weight_of(u) is not None and (u == 0 or weight_of(u - 1) != weight_of(u))]

            def last_unit(self, w):
                return max(u for u in range(self.units) if self.weight_of(u) == w)

        def experts_tensor(e, x_, c, xin):
            base, wbase, E3 = x_.unit0 + x_.units * c, x_.new0 + len(x_.new) * c, 3 * x_.E
            e.wait_ge(S("ex_cpart"), x_.chunk0 + c + 1)
            for t in range(4):
                tr = T.transpose(bank_bf(4)[0:E3, 128 * t:128 * (t + 1)], cpart[:, t, 0:E3], identb)
            tr.then_inc(S("ex_cT_ps"), 1)
            e.wait_ge(S("ex_cT"), x_.chunk0 + c + 1)

            def down(u):
                e.wait_ge(S("ex_a"), base + u + 1)
                for t in range(4):
                    mm = T.matmul(ps[:, 6, 128 * t:128 * (t + 1)], act[:, u % 3, 128 * t:128 * (t + 1)],
                                  x_.down(u), start=u == 0 and t == 0, stop=u == x_.units - 1,
                                  skip_group_check=True)
                mm.then_inc(S("ex_down"), 1)

            for u in range(x_.units):
                w = x_.weight_of(u)
                if u in x_.new:
                    if w >= 2:
                        e.wait_ge(S("ex_cb"), wbase + w - 1)
                    T.matmul(bank(4 + w % 2), B(x_.sel, E3)[:, 128 * w:128 * (w + 1)],
                             cT[0:E3, :], start=True, stop=True).then_inc(S("ex_cb_ps"), 1)
                if u >= 2:
                    e.wait_ge(S("ex_sil"), base + u - 1)
                T.matmul(bank(u % 2), x_.gate(u), xin, start=True, stop=True).then_inc(S("ex_g"), 1)
                if u >= 2:
                    e.wait_ge(S("ex_a"), base + u - 1)
                T.matmul(bank(2 + u % 2), x_.up(u), xin, start=True, stop=True).then_inc(S("ex_u"), 1)
                if u >= 2:
                    down(u - 2)
            down(x_.units - 2)
            down(x_.units - 1)

        def experts_scalar(e, x_, c):
            base, wbase, E3 = x_.unit0 + x_.units * c, x_.new0 + len(x_.new) * c, 3 * x_.E
            e.wait_ge(S("ex_cT_ps"), x_.chunk0 + c + 1)
            A.activation(cT[0:E3, :], bank_bf(4)[0:E3, 0:512], ACT.Copy).then_inc(S("ex_cT"), 1)
            for u in range(x_.units):
                w = x_.weight_of(u)
                if u in x_.new:
                    e.wait_ge(S("ex_cb_ps"), wbase + w + 1)
                    if w >= 2:
                        e.wait_ge(S("ex_t1"), base + x_.last_unit(w - 2) + 1)
                    A.activation(cbs[:, w % 2, :], bank(4 + w % 2), ACT.Copy).then_inc(S("ex_cb"), 1)
                e.wait_ge(S("ex_g"), base + u + 1)
                if u >= 3:
                    e.wait_ge(S("ex_t1"), base + u - 2)
                A.activation(sil[:, u % 3, :], bank(u % 2), ACT.Silu).then_inc(S("ex_sil"), 1)

        def experts_gpsimd(e, x_, c):
            base, wbase = x_.unit0 + x_.units * c, x_.new0 + len(x_.new) * c
            for u in range(x_.units):
                w = x_.weight_of(u)
                e.wait_ge(S("ex_sil"), base + u + 1)
                if u >= 3:
                    e.wait_ge(S("ex_a"), base + u - 2)
                if w is not None:
                    e.wait_ge(S("ex_cb"), wbase + w + 1)
                    P.tensor_tensor(t1[:, u % 3, :], sil[:, u % 3, :], cbs[:, w % 2, :], ALU.mult)\
                        .then_inc(S("ex_t1"), 1)
                else:
                    P.tensor_copy(t1[:, u % 3, :], sil[:, u % 3, :]).then_inc(S("ex_t1"), 1)

        def experts_vector(e, x_, c):
            base = x_.unit0 + x_.units * c
            for u in range(x_.units):
                e.wait_ge(S("ex_u"), base + u + 1)
                e.wait_ge(S("ex_t1"), base + u + 1)
                if u >= 3:
                    e.wait_ge(S("ex_down"), base + u - 2)
                V.tensor_tensor(act[:, u % 3, :], bank(2 + u % 2), t1[:, u % 3, :], ALU.mult)\
                    .then_inc(S("ex_a"), 1)

        class Narrow:
            def __init__(self, n, kv, values, head):
                self.n = n
                self.kv = kv
                self.values = values
                self.head = head
                self.units = 4 * PAIRS if n == 2 else H

            def groups(self, half):
                if self.n == 7:
                    return [None]
                g = [[(2 * i, 0, 0, 512), (2 * i + 1, 1, 0, 512)] for i in range(2 * half)]
                return g + [[(4 * half + i, 0, 128 * i, 512 - 128 * i)] for i in range(4)]

            def unit_base(self, c):
                return self.units * c + (4 * PAIRS * CHUNKS if self.n == 7 else 0)

            def group_base(self, c):
                before = l2n.group_base(CHUNKS) if self.n == 7 else 0
                return before + H * sum(len(self.groups(d % 2)) for d in range(c))

            def four_base(self, c):
                return TILES + 4 * narrow_chunk(self.n, c)

            def key_turn(self, c):
                return c + 2 if self.n == 7 else c

        l2n = Narrow(2, 4, v1g, lambda j, p: (8 * (j // 4) + 4 * p + j % 4, j // 4, 2 * (j // 4) + p))
        l7n = Narrow(7, H, v1, lambda j, p: (2 * j + p, j, 2 * j + p))

        def parity_rows(p):
            return slice(64 * p, 64 * p + 64)

        def narrow_first_tensor(e, a_, c):
            n, half = a_.n, c % 2
            base = a_.unit_base(c)
            for u in range(a_.units):
                if u >= 2:
                    e.wait_ge(S("nr_max"), base + u - 1)
                if n == 2:
                    t, j = u // PAIRS, u % PAIRS
                    q0 = 512 * half + 128 * t
                    width = q0 + 128
                    for p in range(2):
                        rows, b0 = parity_rows(p), 4 * (u % 2) + 2 * p
                        kj = a_.head(j, p)[1]
                        db, dcol = b0 + q0 // 512, q0 % 512
                        if q0 >= 512:
                            T.matmul(bank(b0), qT[rows, j, q0:q0 + 128], kT[rows, kj, 0:512], start=True, stop=True)
                        T.matmul(ps[:, db, dcol:dcol + 128], identb, B("causal"), start=True, stop=False,
                                 skip_group_check=True)
                        mm = T.matmul(ps[:, db, 0:dcol + 128], qT[rows, j, q0:q0 + 128],
                                      kT[rows, kj, width - dcol - 128:width], start=False, stop=True,
                                      skip_group_check=True)
                else:
                    j, p = u // 2, u % 2
                    rows = parity_rows(p)
                    for t in range(4):
                        b, at, q0 = 2 * (u % 4) + t // 2, 192 * (t % 2), 512 * half + 128 * t
                        first = q0 == 0
                        T.matmul(ps[:, b, at:at + 128], identb, B("winc"), start=t % 2 == 0, stop=False,
                                 skip_group_check=True)
                        T.matmul(ps[:, b, at + 128:at + 192], identb, B("winc")[:, 64:128] if first else B("behind"),
                                 start=False, stop=False, skip_group_check=True)
                        T.matmul(ps[:, b, at:at + 128], qT[rows, j, q0:q0 + 128], kT[rows, j, q0:q0 + 128],
                                 start=False, stop=True, skip_group_check=True)
                        k0 = q0 + 64 if first else q0 - 64
                        mm = T.matmul(ps[:, b, at + 128:at + 192], qT[rows, j, q0:q0 + 128], kT[rows, j, k0:k0 + 64],
                                      start=False, stop=True, skip_group_check=True)
                mm.then_inc(S("nr_s"), 1)

        def narrow_first_vector(e, step, a_, c):
            n, half, base = a_.n, c % 2, a_.unit_base(c)
            nm4 = nm[:].rearrange("p (t h) -> p t h", t=4)
            for u in range(a_.units):
                e.wait_ge(S("nr_s"), base + u + 1)
                if n == 2:
                    t, j = u // PAIRS, u % PAIRS
                    width = 512 * half + 128 * t + 128
                    s = ps[:, 4 * (u % 2):4 * (u % 2) + 4, :].rearrange("p (a b) k -> p a (b k)", a=2)[:, :, 0:width]
                    V.tensor_reduce(nm4[:, t, 2 * j:2 * j + 2], s, AX.X, ALU.max, negate=True)\
                        .then_inc(S("nr_max"), 1)
                else:
                    b = 2 * (u % 4)
                    s = ps[:, b:b + 2, 0:384].rearrange("p b (t k) -> p b t k", t=2)
                    V.tensor_reduce(nm4[:, :, u].rearrange("p (b t) -> p b t", b=2), s, AX.X, ALU.max, negate=True)\
                        .then_inc(S("nr_max"), 1)
            e.wait_ge(S("nr_max"), base + a_.units)
            step(V.tensor_copy(qstack[:, :, 48], nm[:]))
            step.wait()
            step(V.tensor_tensor(nmr[:], nm[:], qstack[:, :, 48], ALU.subtract))
            step.wait()
            step(V.tensor_copy(qstack[:, :, 49], nmr[:]))
            step.wait()
            V.tensor_tensor(qstack[:, :, 50], nmr[:], qstack[:, :, 49], ALU.subtract)\
                .then_inc(S("nr_mstack"), 1)

        def narrow_second_tensor(e, a_, c):
            n, half = a_.n, c % 2
            base = a_.group_base(c)
            work = [(h, g) for h in range(H) for g in a_.groups(half)]
            per_head = len(a_.groups(half))

            def scores(i):
                (u, g), b0 = work[i], 2 * (i % 2)
                j, p = u // 2, u % 2
                rows, kj = parity_rows(p), a_.head(j, p)[1]
                if i >= 2:
                    e.wait_ge(S("nr_prob"), base + i - 1)
                if g is None:
                    for t in range(4):
                        b, at, q0 = b0 + t // 2, 192 * (t % 2), 512 * half + 128 * t
                        T.matmul(ps[:, b, at:at + 128], identb, B("wincT"), start=t % 2 == 0, stop=False,
                                 skip_group_check=True)
                        T.matmul(ps[:, b, at + 128:at + 192], identb, B("behindT"), start=False, stop=q0 == 0,
                                 skip_group_check=True)
                        mm = T.matmul(ps[:, b, at:at + 128], kT[rows, j, q0:q0 + 128], qT[rows, j, q0:q0 + 128],
                                      start=False, stop=True, skip_group_check=True)
                        if q0:
                            mm = T.matmul(ps[:, b, at + 128:at + 192], kT[rows, j, q0 - 128:q0],
                                          qT[rows, j, q0:q0 + 64], start=False, stop=True, skip_group_check=True)
                else:
                    for kt, k, q0, width in g:
                        q = 512 * half + q0
                        diag = kt >= 4 * half
                        if diag:
                            T.matmul(ps[:, b0 + k, 0:128], identb, B("causalT"), start=True, stop=False,
                                     skip_group_check=True)
                        mm = T.matmul(ps[:, b0 + k, 0:width], kT[rows, kj, 128 * kt:128 * kt + 128],
                                      qT[rows, j, q:q + width], start=not diag, stop=True, skip_group_check=True)
                mm.then_inc(S("nr_sT"), 1)

            def values(i):
                (u, g), slot = work[i], i % 3
                _, _, vh = a_.head(u // 2, u % 2)
                e.wait_ge(S("nr_prob"), base + i + 1)
                if i % (4 * per_head) == 0 and u >= 8:
                    e.wait_ge(S("ob"), a_.four_base(c) + u // 4 - 1)
                first, b = 32 * (u % 4), 6 + u // 4 % 2

                def region(lo, n):
                    return ps[first:first + HD + 1, b, lo:lo + n]

                if g is None:
                    for t in range(4):
                        at, q0, tile = 192 * (t % 2), 512 * half + 128 * t, 4 * half + t
                        pt = pT2[:, slot, t // 2, :]
                        mm = T.matmul(region(128 * t, 128), a_.values[:, tile, vh, :], pt[:, at:at + 128],
                                      start=True, stop=not q0, skip_group_check=True)
                        if q0:
                            mm = T.matmul(region(128 * t, 64), a_.values[:, tile - 1, vh, :],
                                          pt[:, at + 128:at + 192], start=False, stop=True, skip_group_check=True)
                else:
                    for kt, k, q0, width in g:
                        mm = T.matmul(region(q0, width), a_.values[:, kt, vh, :], pT2[:, slot, k, 0:width],
                                      start=kt == 0, stop=kt == 4 * half + 3, skip_group_check=True)
                mm.then_inc(S("nr_pv"), 1)

            def turn_outputs(four):
                e.wait_ge(S("ob"), a_.four_base(c) + four + 1)
                if four:
                    e.wait_ge(S("nr_on"), a_.four_base(c) - 32 + four)
                for t in range(4):
                    mm = T.transpose(ps[:, 4, 128 * t:128 * t + 128], obuf[:, four % 2, 128 * t:128 * t + 128], ident)
                mm.then_inc(S("ob_turned"), 1)

            ends = {4 * per_head * (f + 1) + 3: f for f in range(3)}
            for i in range(len(work) + 2):
                if i < len(work):
                    scores(i)
                if i >= 2:
                    values(i - 2)
                if i in ends:
                    turn_outputs(ends[i])
            turn_outputs(3)

        def narrow_second_scalar(e, a_, c):
            n, half = a_.n, c % 2
            base = a_.group_base(c)
            work = [g for h in range(H) for g in a_.groups(half)]
            for i, g in enumerate(work):
                e.wait_ge(S("nr_sT"), base + i + 1)
                if i >= 3:
                    e.wait_ge(S("nr_pv"), base + i - 2)
                banks = 2 if g is None or len(g) == 2 else 1
                width = 384 if g is None else g[0][3]
                b0 = 2 * (i % 2)
                A.activation(pT2[:, i % 3, 0:banks, 0:width], ps[:, b0:b0 + banks, 0:width],
                             ACT.Exp, scale=float(HD) ** -0.5).then_inc(S("nr_prob"), 1)

        def narrow_rope_vector(step, src, dst, heads_, tmp, half):
            n = 4 * heads_
            s3 = src[:, 0:n, :].rearrange("p (t h) d -> p t h d", t=4)
            d3 = dst[:, 0:n, :].rearrange("p (t h) d -> p t h d", t=4)
            t3 = tmp[:, 0:n, :].rearrange("p (t h) d -> p t h d", t=4)

            def table(name):
                tab = F(name).rearrange("p (t d) -> p t d", t=8)[:, 4 * half:4 * half + 4, :]
                return tab.unsqueeze(2).to_broadcast([128, 4, heads_, 8])

            cos, sin = table("cos"), table("sin")
            step(V.tensor_tensor(d3, s3, cos, ALU.mult))
            step(V.tensor_tensor(t3[:, :, :, 0:4], s3[:, :, :, 4:8], sin[:, :, :, 0:4], ALU.mult))
            step(V.tensor_tensor(t3[:, :, :, 4:8], s3[:, :, :, 0:4], sin[:, :, :, 4:8], ALU.mult))
            step.wait()
            step(V.tensor_tensor(dst[:, 0:n, :], dst[:, 0:n, :], tmp[:, 0:n, :], ALU.add))

        def narrow_stacks_vector(e, step, a_, c):
            n, half = a_.n, c % 2
            nk = 4 * a_.kv
            step.wait()
            e.wait_ge(S("nr_qk_sb"), 3 * (narrow_chunk(n, c) + 1))
            narrow_rope_vector(step, kf, kr, a_.kv, rot[:, 1], half)
            step.wait()
            split_parts(step, V, kr, kp, kf, nk, "nr_kparts")
            narrow_rope_vector(step, qf, qr, H, rot[:, 0], half)
            step.wait()
            split_parts(step, V, qr, qp, qf, 64)
            fill_slots(step, V, qp, qstack, 64, Q_SLOTS)
            step.wait()
            V.memset(qstack[:, :, 48:51], 0.0).then_inc(S("nr_qstack"), 1)
            stack_evac(e, V.tensor_copy, qT, H, "nr_qT", narrow_chunk(n, c), 7, half)

        def narrow_gpsimd(e, step, a_, c, kst):
            n, nk = a_.n, 4 * a_.kv
            if c == 0:
                step(P.memset(kst[:, 0:nk, 48:51], 1.0))
                step.wait()
                step(P.memset(kst[:, 0:nk, 51:64], 0.0))
                if n == 7:
                    step(P.memset(qstack[:, :, 51:64], 0.0))
                step.wait()
                P.memset(v1[:, :, :, 8:9], 1.0).then_inc(S("nr_consts"), 1)

        def narrow_tensor(e, a_, c, kst):
            n = a_.n
            e.wait_ge(S("nr_consts"), 2 if n == 7 else 1)
            e.wait_ge(S("nr_kstack"), 4 * (narrow_chunk(n, c) + 1))
            stack_transposes(e, kst, a_.kv, "nr_kT", a_.key_turn(c), 6)
            e.wait_ge(S("nr_qstack"), narrow_chunk(n, c) + 1)
            stack_transposes(e, qstack, H, "nr_qT", narrow_chunk(n, c), 7)
            e.wait_ge(S("nr_kT_sb"), a_.kv // 4 * (a_.key_turn(c) + 1))
            e.wait_ge(S("nr_qT_sb"), 4 * (narrow_chunk(n, c) + 1))
            narrow_first_tensor(e, a_, c)
            e.wait_ge(S("nr_mstack"), narrow_chunk(n, c) + 1)
            stack_transposes(e, qstack, H, "nr_mT", narrow_chunk(n, c), 7)
            e.wait_ge(S("nr_mT_sb"), 4 * (narrow_chunk(n, c) + 1))
            narrow_second_tensor(e, a_, c)

        def narrow_vector(e, step, a_, c):
            n, half = a_.n, c % 2
            narrow_stacks_vector(e, step, a_, c)
            narrow_first_vector(e, step, a_, c)
            stack_evac(e, V.tensor_copy, qT, H, "nr_mT", narrow_chunk(n, c), 7, half)
            per_head = len(a_.groups(half))
            for four in range(4):
                done = a_.four_base(c) + four
                e.wait_ge(S("nr_pv"), a_.group_base(c) + 4 * per_head * (four + 1))
                if four >= 2:
                    e.wait_ge(S("ob_turned"), done - 1)
                V.tensor_copy(obuf[:, four % 2, :], bank(6 + four % 2)).then_inc(S("ob"), 1)
                e.wait_ge(S("ob_turned"), done + 1)
                o = bank(4).rearrange("p (t h d) -> p t h d", t=4, h=4)
                rec = orec[:, :, 4 * four:4 * four + 4]
                step(V.reciprocal(rec, o[:, :, :, 8]))
                step.wait()
                for p in range(2):
                    first = a_.head(2 * four, p)[0]
                    stride = a_.head(2 * four + 1, p)[0] - first
                    dst = on[:].rearrange("p t (h d) -> p t h d", h=H)[:, :, first:first + stride + 1:stride, :]
                    ins = V.tensor_tensor(dst, o[:, :, p::2, 0:8],
                                          rec[:, :, p::2].unsqueeze(3).to_broadcast([128, 4, 2, 8]), ALU.mult)
                    if p:
                        ins.then_inc(S("nr_on"), 1)
                    else:
                        step(ins)

        kstack_g = kstack[:, 0:16, :]
        l2x = Experts(2, 16, 8, "sel8", lambda u: u // 2,
                      lambda u: w2g[:, u // 2, 128 * (u % 2):128 * (u % 2) + 128],
                      lambda u: w2u[:, u // 2, 128 * (u % 2):128 * (u % 2) + 128],
                      lambda u: w2d[:, u, :])

        def l2_tensor(e):
            e.wait_ge(S("ld_w2"), 16 * 10)
            for c in range(CHUNKS):
                after_turn(e, 2, c)
                turn_tensor(e, hx, "rms", 2 * c, 0)
                e.wait_ge(S("l2_hT"), c + 1)
                for t in range(4):
                    mm = T.matmul(ps[:, 1 + t // 2, 192 * (t % 2):192 * (t % 2) + 192],
                                  hT[:, 128 * t:128 * (t + 1)], w2[:], start=True, stop=True)
                mm.then_inc(S("l2_qkv"), 1)
                narrow_tensor(e, l2n, c, kstack_g)
                finish_tensor(e, 2, c, w2o[:], None, 0, 1)
                turn_tensor(e, hx, "rms", 2 * c + 1, 0)
                e.wait_ge(S("l2_hT2"), c + 1)
                for t in range(4):
                    mm = T.matmul(ps[:, 7, 8 * t:8 * t + 8], hT2[:, 128 * t:128 * (t + 1)], w2r[:],
                                  start=True, stop=True)
                mm.then_inc(S("l2_logit"), 1)
                e.wait_ge(S("ld_w2x"), 64)
                experts_tensor(e, l2x, c, hT2)
                xT_tensor(e, 2, c, 7)

        def l2_scalar(e):
            e.wait_ge(S("ld_w2"), 16 * 10)
            for c in range(CHUNKS):
                after_chunk(e, 2, c)
                e.wait_ge(S("rms_T_ps"), 2 * c + 1)
                A.activation(hT[:], bank(0), ACT.Copy, scale=ln12[:, 0:1]).then_inc(S("l2_hT"), 1)
                e.wait_ge(S("l2_qkv"), c + 1)
                qkv = ps[:, 1:3, 0:384].rearrange("p b (t n) -> p b t n", t=2)
                A.activation(kf[:, 0:16, :].rearrange("p (b t h) d -> p b t (h d)", b=2, t=2),
                             qkv[:, :, :, 128:160], ACT.Copy).then_inc(S("nr_qk_sb"), 1)
                A.activation(qf[:].rearrange("p (b t h) d -> p b t (h d)", b=2, t=2),
                             qkv[:, :, :, 0:128], ACT.Copy).then_inc(S("nr_qk_sb"), 1)
                first = 4 * (c % 2)
                A.activation(v1g[:, first:first + 2, :, 0:8],
                             qkv[:, 0, :, 160:192].rearrange("p t (h d) -> p t h d", d=8),
                             ACT.Copy).then_inc(S("act_step"), 1)
                A.activation(v1g[:, first + 2:first + 4, :, 0:8],
                             qkv[:, 1, :, 160:192].rearrange("p t (h d) -> p t h d", d=8),
                             ACT.Copy).then_inc(S("nr_qk_sb"), 1)
                e.wait_ge(S("nr_kparts"), c + 1)
                fill_keys_scalar(e, 16, "nr_kstack")
                stack_evac(e, act_copy, kT, 4, "nr_kT", c, 6, c % 2)
                narrow_second_scalar(e, l2n, c)
                finish_scalar(e, 2, c, 0)
                e.wait_ge(S("rms_T_ps"), 2 * c + 2)
                A.activation(hT2[:], bank(0), ACT.Copy, scale=ln12[:, 1:2]).then_inc(S("l2_hT2"), 1)
                e.wait_ge(S("l2_shift"), c + 1)
                A.activation(lge[:, :, 0:8], lge[:, :, 0:8], ACT.Exp).then_inc(S("l2_exp"), 1)
                experts_scalar(e, l2x, c)
                xT_scalar(e, 2, c, 7)

        def l2_gpsimd(e, step):
            for c in range(CHUNKS):
                after_chunk(e, 2, c)
                rms_gpsimd(e, step, "rms", 2 * c)
                narrow_gpsimd(e, step, l2n, c, kstack_g)
                rms_gpsimd(e, step, "rms", 2 * c + 1)
                experts_gpsimd(e, l2x, c)
                ln_gpsimd(e, step, 2, c)

        def l2_vector(e, step):
            for c in range(CHUNKS):
                after_chunk(e, 2, c)
                rms_vector(e, step, xs(2, c), hx, "rms", 2 * c)
                narrow_vector(e, step, l2n, c)
                e.wait_ge(S("nr_out"), c + 1)
                h1f = flat(h1)
                step(V.tensor_tensor(h1f, bank(1), flat(xs(2, c)), ALU.add))
                step.wait()
                step(V.tensor_scalar(h1f, h1f, -100.0, 100.0, ALU.max, ALU.min))
                step.wait()
                rms_vector(e, step, h1, hx, "rms", 2 * c + 1)
                e.wait_ge(S("l2_logit"), c + 1)
                l3 = lg[:, :, 0:8]
                step(V.tensor_copy(l3, ps[:, 7, 0:32].rearrange("p (t e) -> p t e", t=4)))
                step.wait()
                step(V.tensor_reduce(lgm[:], l3, AX.X, ALU.max))
                step.wait()
                V.tensor_tensor(lge[:, :, 0:8], l3, lgm[:].unsqueeze(2).to_broadcast([128, 4, 8]), ALU.subtract)\
                    .then_inc(S("l2_shift"), 1)
                rank_vector(step, l3, 4, 8, 2)
                e.wait_ge(S("l2_exp"), c + 1)
                step(V.tensor_tensor(cw[:, :, 0:8], lge[:, :, 0:8],
                                     msk[:, 0:32].rearrange("p (t e) -> p t e", t=4), ALU.mult))
                step.wait()
                weights_vector(e, step, 8, 1.0, 0.0)
                experts_vector(e, l2x, c)
                e.wait_ge(S("ex_down"), 16 * (c + 1))
                yf = flat(y[:, c % 2])
                step(V.tensor_tensor(yf, bank(6), h1f, ALU.add))
                step.wait()
                step(V.tensor_scalar(yf, yf, -100.0, 100.0, ALU.max, ALU.min))
                step.wait()
                step(V.tensor_tensor(yf, yf, flat(xs(2, c)), ALU.add))
                ln_vector(e, step, 2, c)

        SCALE3 = float(D) ** -0.5
        sum3 = norm2r[:].rearrange("p a n -> p (a n)")

        def l3_tensor(e):
            after_turn(e, 3, 0)
            e.wait_ge(S("ld_w3"), 48)
            for i in range(3):
                mm = T.transpose(ps[:, 7, 128 * i:128 * (i + 1)], w3[:, i, :], ident)
            mm.then_inc(S("wT_ps"), 1)
            e.wait_ge(S("wT"), 2)

            def scores(i):
                qt = i % QT
                width = 128 * (qt + 1)
                if i % QT < 2:
                    e.wait_ge(S("l3_qkv_sb"), 6 * (i // QT + 1))
                if i >= 2:
                    e.wait_ge(S("l3_prob"), i - 1)
                b0, db, dcol = 2 * (i % 2), qt // 4, 128 * (qt % 4)
                T.matmul(ps[:, b0 + db, dcol:dcol + 128], identb, B("causal"), start=True, stop=False,
                         skip_group_check=True)
                for half in range(db + 1):
                    w = min(512, width - 512 * half)
                    mm = T.matmul(ps[:, b0 + half, 0:w], q3T[:, 128 * qt:128 * qt + 128],
                                  k3T[:, 512 * half:512 * half + w], start=half != db, stop=True,
                                  skip_group_check=True)
                mm.then_inc(S("l3_s"), 1)

            def turn(i):
                e.wait_ge(S("l3_prob"), i + 1)
                if i:
                    e.wait_ge(S("l3_pT_sb"), i)
                for kt in range(i % QT + 1):
                    mm = T.transpose(ps[:, 4 + kt // 4, 128 * (kt % 4):128 * (kt % 4) + 128],
                                     ring[:, i % RING, 128 * kt:128 * kt + 128], ident)
                mm.then_inc(S("l3_pT_ps"), 1)

            def values(i):
                qt = i % QT
                e.wait_ge(S("l3_pT_sb"), i + 1)
                if i >= 2:
                    e.wait_ge(S("l3_y"), i - 1)
                for kt in range(qt + 1):
                    mm = T.matmul(ps[:, 6 + i % 2, 0:128], pTr[:, i % 2, kt, :], v3[:, kt, :],
                                  start=kt == 0, stop=kt == qt)
                mm.then_inc(S("l3_pv"), 1)

            for b in range(SEQS):
                if b:
                    after_turn(e, 3, 2 * b)
                    e.wait_ge(S("l3_pT_sb"), QT * b)
                for half in range(2):
                    src = xT[:, SEQ * b + 512 * half:SEQ * b + 512 * half + 512]
                    T.matmul(bank(half), w3T[:, 0, :], src, start=True, stop=True).then_inc(S("l3_qkv"), 1)
                for half in range(2):
                    src = xT[:, SEQ * b + 512 * half:SEQ * b + 512 * half + 512]
                    T.matmul(bank(2 + half), w3T[:, 1, :], src, start=True, stop=True).then_inc(S("l3_qkv"), 1)
                for half in range(2):
                    for t in range(4):
                        at = SEQ * b + 512 * half + 128 * t
                        mm = T.matmul(ps[:, 4 + half, 128 * t:128 * t + 128], xT[:, at:at + 128], w3T[:, 2, :],
                                      start=True, stop=True)
                    mm.then_inc(S("l3_qkv"), 1)
                scores(QT * b)
                for r in range(QT + 1):
                    if r + 1 < QT:
                        scores(QT * b + r + 1)
                    if r < QT:
                        turn(QT * b + r)
                    if r:
                        values(QT * b + r - 1)
                for c in (2 * b, 2 * b + 1):
                    after_turn(e, 3, c)
                    xT_tensor(e, 3, c, 0)

        def l3_scalar(e):
            e.wait_ge(S("wT_ps"), 2)
            A.activation(flat(w3T), ps[:, 7, 0:384], ACT.Copy).then_inc(S("wT"), 1)
            for b in range(SEQS):
                for i, dst in enumerate((q3T[:, 0:512], q3T[:, 512:1024], k3T[:, 0:512], k3T[:, 512:1024],
                                         flat(v3[:, 0:4, :]), flat(v3[:, 4:8, :]))):
                    e.wait_ge(S("l3_qkv"), 6 * b + i + 1)
                    A.activation(dst, bank(i), ACT.Copy).then_inc(S("l3_qkv_sb"), 1)
                for i in range(QT * b, QT * b + QT):
                    width = 128 * (i % QT + 1)
                    e.wait_ge(S("l3_max"), i + 1)
                    if i >= RING:
                        e.wait_ge(S("l3_pT_ps"), i - RING + 1)
                    b0 = 2 * (i % 2)
                    s = ps[:, b0:b0 + 2, :].rearrange("p a b -> p (a b)")[:, 0:width]
                    A.activation(ring[:, i % RING, 0:width], s, ACT.Exp, bias=nmr[:, i:i + 1], scale=SCALE3,
                                 accum_out=sum3[:, i:i + 1]).then_inc(S("l3_prob"), 1)
                for c in (2 * b, 2 * b + 1):
                    xT_scalar(e, 3, c, 0)

        def l3_gpsimd(e, step):
            for c in range(CHUNKS):
                ln_gpsimd(e, step, 3, c)

        def l3_vector(e, step):
            def row_max(i):
                width, b0 = 128 * (i % QT + 1), 2 * (i % 2)
                e.wait_ge(S("l3_s"), i + 1)
                s = ps[:, b0:b0 + 2, :].rearrange("p a b -> p (a b)")[:, 0:width]
                step(V.tensor_reduce(nm[:, i:i + 1], s, AX.X, ALU.max, negate=True))
                step.wait()
                V.tensor_scalar(nmr[:, i:i + 1], nm[:, i:i + 1], SCALE3, None, ALU.mult).then_inc(S("l3_max"), 1)

            def evac(i):
                e.wait_ge(S("l3_pT_ps"), i + 1)
                if i >= 2:
                    e.wait_ge(S("l3_pv"), i - 1)
                n = i % QT + 1
                src = ps[:, 4:6, :].rearrange("p a b -> p (a b)")[:, 0:128 * n]
                V.tensor_copy(pTr[:, i % 2, 0:n, :].rearrange("p k q -> p (k q)"), src).then_inc(S("l3_pT_sb"), 1)

            def output(i):
                t, c = i % 4, i // 4
                if t == 0:
                    after_chunk(e, 3, c)
                e.wait_ge(S("l3_pv"), i + 1)
                step(V.reciprocal(m2[:, i % 16:i % 16 + 1], sum3[:, i:i + 1]))
                step.wait()
                V.scalar_tensor_tensor(y[:, c % 2, t, :], ps[:, 6 + i % 2, 0:128], m2[:, i % 16:i % 16 + 1],
                                       x[:, 4 * c + t, :], ALU.mult, ALU.add).then_inc(S("l3_y"), 1)

            for b in range(SEQS):
                base = QT * b
                row_max(base)
                for r in range(QT + 1):
                    if r + 1 < QT:
                        row_max(base + r + 1)
                    if r < QT:
                        evac(base + r)
                    if r:
                        output(base + r - 1)
                        if r % 4 == 0:
                            c = 2 * b + r // 4 - 1
                            e.wait_ge(S("l3_y"), 4 * (c + 1))
                            ln_vector(e, step, 3, c)

        l4x = Experts(4, 9, 16, "sel16", lambda u: u if u < 8 else None,
                      lambda u: w4T[:, u, :], lambda u: w4T[:, 9 + u, :], lambda u: w4T[:, 18 + u, :])

        def l4_tensor(e):
            after_turn(e, 4, 0)
            e.wait_ge(S("ld_w4"), 16 * 7)
            for g in range(7):
                for i in range(4 * g, min(4 * g + 4, 27)):
                    mm = T.transpose(ps[:, g, 128 * (i % 4):128 * (i % 4) + 128], w4n[:, i, :], ident)
                mm.then_inc(S("wT_ps"), 1)
            e.wait_ge(S("ld_w4r"), 32)
            T.transpose(ps[:, 7, 0:16], w4r[:], F("ident", 16)[:, 0:16]).then_inc(S("wT_ps"), 1)
            e.wait_ge(S("wT"), 10)
            for c in range(CHUNKS):
                after_turn(e, 4, c)
                xin = xT[:, 512 * c:512 * c + 512]
                for t in range(4):
                    mm = T.matmul(ps[:, 7, 16 * t:16 * t + 16], xin[:, 128 * t:128 * t + 128], w4rT[:],
                                  start=True, stop=True)
                mm.then_inc(S("l4_logit"), 1)
                experts_tensor(e, l4x, c, xin)
                xT_tensor(e, 4, c, 7)

        def l4_scalar(e):
            for g in range(7):
                n = min(4, 27 - 4 * g)
                e.wait_ge(S("wT_ps"), g + 3)
                A.activation(flat(w4T[:, 4 * g:4 * g + n, :]), ps[:, g, 0:128 * n], ACT.Copy).then_inc(S("wT"), 1)
            e.wait_ge(S("wT_ps"), 10)
            A.activation(w4rT[:], ps[:, 7, 0:16], ACT.Copy).then_inc(S("wT"), 1)
            for c in range(CHUNKS):
                after_chunk(e, 4, c)
                e.wait_ge(S("l4_logit"), c + 1)
                A.activation(lg[:].rearrange("p t e -> p (t e)"), ps[:, 7, 0:64], ACT.Sigmoid)\
                    .then_inc(S("l4_sig"), 1)
                experts_scalar(e, l4x, c)
                xT_scalar(e, 4, c, 7)

        def l4_gpsimd(e, step):
            for c in range(CHUNKS):
                experts_gpsimd(e, l4x, c)
                ln_gpsimd(e, step, 4, c)

        def l4_vector(e, step):
            pairs = gt[:, 0:96].rearrange("p (g k) -> p g k", k=6)
            e.wait_ge(S("ld_w4r"), 32)
            for c in range(CHUNKS):
                after_chunk(e, 4, c)
                e.wait_ge(S("l4_sig"), c + 1)
                step(V.tensor_tensor(lge[:], lg[:], ebias[:].unsqueeze(1).to_broadcast([128, 4, 16]), ALU.add))
                step.wait()
                g4 = lge[:].rearrange("p t (g k) -> p (t g) k", g=4)
                step(V.tensor_tensor(pairs[:, :, 0:3], g4[:, :, 0:3], g4[:, :, 1:4], ALU.add))
                step(V.tensor_tensor(pairs[:, :, 3:5], g4[:, :, 0:2], g4[:, :, 2:4], ALU.add))
                step(V.tensor_tensor(pairs[:, :, 5:6], g4[:, :, 0:1], g4[:, :, 3:4], ALU.add))
                step.wait()
                step(V.tensor_reduce(cwr[:, :, 0:4].rearrange("p t g -> p t g"),
                                     pairs.rearrange("p (t g) k -> p t g k", t=4), AX.X, ALU.max))
                rank_vector(step, cwr[:, :, 0:4], 4, 4, 2)
                step(V.tensor_tensor(cw[:].rearrange("p t (g k) -> p (t g) k", g=4), g4,
                                     msk[:, 0:16].unsqueeze(2).to_broadcast([128, 16, 4]), ALU.mult))
                rank_vector(step, cw[:], 4, 16, 4)
                step(V.tensor_tensor(cw[:], lg[:], msk[:, 0:64].rearrange("p (t e) -> p t e", t=4), ALU.mult))
                step.wait()
                weights_vector(e, step, 16, 2.5, 1e-20)
                experts_vector(e, l4x, c)
                e.wait_ge(S("ex_down"), 16 * CHUNKS + 9 * (c + 1))
                residual_vector(e, step, 4, c, 6)
                ln_vector(e, step, 4, c)

        HD5 = 64
        q5 = big[:, 0:4096].rearrange("p (s n) -> p s n", s=4)
        k5 = big[:, 4096:8192].rearrange("p (s n) -> p s n", s=4)
        v5 = tf[:, 4096:8192].rearrange("p (s n) -> p s n", s=4)
        prod5 = sf[:, 0:2048].rearrange("p (a n) -> p a n", a=2)
        pv5 = sf[:, 2048:4096].rearrange("p (a n) -> p a n", a=2)
        ctxT = hf[:, 0:1024]
        small5 = pTr[:].rearrange("p a k q -> p (a k q)")
        sc5 = small5[:, 0:256].rearrange("p (s t h) -> p s t h", s=4, t=4)
        qd5 = small5[:, 256:512].rearrange("p (s h r) -> p s h r", s=4, r=4)
        pj5 = small5[:, 512:768].rearrange("p (s h r) -> p s h r", s=4, r=4)
        mx5 = small5[:, 768:832].rearrange("p (s h) -> p s h", s=4)
        pjT = small5[0:64, 1024:1536]
        PAIRS5 = sorted(((s, t) for s in range(4) for t in range(4)), key=lambda st: (max(st), st))
        DVE5 = (2, 5, 8, 11, 13, 15)
        POOL5 = [i for i in range(16) if i not in DVE5]
        PROJ5 = [(part, s, half) for s in range(4) for part in (0, 1) for half in (0, 1)] + \
                [(2, s, half) for s in range(4) for half in (0, 1)]

        def by_offset(v, off):
            lo, hi = max(0, -off), min(4, 4 - off)
            st = v.rearrange("p s t h -> p (s t) h")
            first = 5 * lo + off
            return st[:, first:first + 5 * (hi - lo - 1) + 1:5, :], lo, hi

        def l5_tensor(e):
            after_turn(e, 5, 0)
            e.wait_ge(S("ld_w5"), 16 * 4)
            e.wait_ge(S("ld_w5s"), 16 * 25)
            for g in range(8):
                for i in range(4):
                    src = w5n[:, 4 * g + i, :] if g < 6 else w5on[:, 4 * (g - 6) + i, :]
                    mm = T.transpose(ps[:, g, 128 * i:128 * (i + 1)], src, ident)
                mm.then_inc(S("wT_ps"), 1)
            e.wait_ge(S("wT"), 18)
            for i in range(8):
                T.matmul(ps[:, 0, 8 * i:8 * i + 8], w5n[:, i, :], kdb[:], start=True, stop=True)
                T.matmul(ps[0:1, 1, 8 * i:8 * i + 8], b5q[:, i:i + 1], kdb[:], start=True, stop=True)
                mm = T.matmul(ps[0:64, 2, 0:128], vdb[:, 60 - 8 * i:124 - 8 * i], w5oT[:, i, :],
                              start=i == 0, stop=i == 7)
            mm.then_inc(S("l5_fold_ps"), 1)
            e.wait_ge(S("l5_fold"), 3)
            e.wait_ge(S("ld_b5row"), 48)
            for c in range(CHUNKS):
                after_turn(e, 5, c)
                for i in range(24):
                    part, s, half = PROJ5[i]
                    if i >= 4:
                        e.wait_ge(S("l5_qkv_sb"), 24 * c + i - 3)
                    tok = SEQ * s + 128 * c
                    cols = slice(1024 * part + 512 * half, 1024 * part + 512 * half + 512)
                    T.matmul(bank(i % 4), xT[:, tok:tok + 128], w5T[:, cols], start=True, stop=False)
                    T.matmul(bank(i % 4), B("ones", 3), b5row[0:3, cols], start=False, stop=True)\
                        .then_inc(S("l5_qkv"), 1)
                for s in range(4):
                    tok = SEQ * s + 128 * c
                    T.matmul(ps[:, 6, 64 * s:64 * s + 64], xT[:, tok:tok + 128], qk5[:], start=True, stop=False)
                    mm = T.matmul(ps[:, 6, 64 * s:64 * s + 64], ones_row, rb5[:], start=False, stop=True)
                mm.then_inc(S("l5_qd_ps"), 1)
                e.wait_ge(S("l5_pj"), c + 1)
                for s in range(4):
                    mm = T.transpose(ps[0:64, 4, 128 * s:128 * s + 128], pj5[:, s].rearrange("p h r -> p (h r)"), ident)
                mm.then_inc(S("l5_pjT_ps"), 1)
                e.wait_ge(S("l5_qkv_sb"), 24 * (c + 1))
                e.wait_ge(S("l5_pjT"), c + 1)

                def project(s):
                    e.wait_ge(S("l5_ctxT"), 4 * c + s + 1)
                    dst = ps[:, 5, 128 * s:128 * s + 128]
                    for i in range(8):
                        T.matmul(dst, ctxT[:, 128 * i:128 * i + 128], w5oT[:, i, :], start=i == 0, stop=False)
                    T.matmul(dst, pjT[:, 128 * s:128 * s + 128], vw5[:], start=False, stop=False)
                    T.matmul(dst, ones_row, b5o[:], start=False, stop=True).then_inc(S("l5_out"), 1)

                for s in range(4):
                    if s >= 2:
                        e.wait_ge(S("l5_ctxT"), 4 * c + s - 1)
                    for t in range(4):
                        j = 3 * s + t
                        if t == 3:
                            e.wait_ge(S("l5_pv_pool"), 4 * c + s + 1)
                            src = prod5[:, s % 2, :]
                        else:
                            e.wait_ge(S("l5_pv"), 12 * c + j + 1)
                            src = pv5[:, j % 2, :]
                        for k in range(8):
                            mm = T.matmul(ps[:, 2 * (s % 2) + k // 4, 128 * (k % 4):128 * (k % 4) + 128],
                                          src[:, 128 * k:128 * k + 128], ident, is_transpose=True,
                                          start=t == 0 and k % 4 == 0, stop=t == 3, skip_group_check=True)
                        mm.then_inc(S("l5_ctx"), 1)
                    if s:
                        project(s - 1)
                project(3)
                xT_tensor(e, 5, c, 7)

        def l5_scalar(e):
            after_chunk(e, 5, 0)
            for g in range(8):
                e.wait_ge(S("wT_ps"), g + 11)
                dst = w5T[:, 512 * g:512 * g + 512] if g < 6 else flat(w5oT[:, 4 * (g - 6):4 * (g - 6) + 4, :])
                A.activation(dst, bank(g), ACT.Copy).then_inc(S("wT"), 1)
            e.wait_ge(S("l5_fold_ps"), 1)
            A.activation(qk5[:], ps[:, 0, 0:64], ACT.Copy).then_inc(S("l5_fold"), 1)
            A.activation(rb5[:], ps[0:1, 1, 0:64], ACT.Copy).then_inc(S("l5_fold"), 1)
            A.activation(vw5[:], ps[0:64, 2, 0:128], ACT.Copy).then_inc(S("l5_fold"), 1)
            for c in range(CHUNKS):
                after_chunk(e, 5, c)
                if c == 0:
                    e.wait_ge(S("ld_b5row"), 48)
                for i in range(24):
                    part, s, half = PROJ5[i]
                    e.wait_ge(S("l5_qkv"), 24 * c + i + 1)
                    A.activation((q5, k5, v5)[part][:, s, 512 * half:512 * half + 512], bank(i % 4), ACT.Copy,
                                 scale=HD5 ** -0.5 if part == 0 else 1.0).then_inc(S("l5_qkv_sb"), 1)
                e.wait_ge(S("l5_qd_ps"), c + 1)
                A.activation(qd5.rearrange("p s h r -> p (s h r)"), ps[:, 6, 0:256], ACT.Copy, scale=HD5 ** -0.5)\
                    .then_inc(S("l5_qd"), 1)
                e.wait_ge(S("l5_shift"), c + 1)
                A.activation(sc5, sc5, ACT.Exp).then_inc(S("l5_exp"), 1)
                e.wait_ge(S("l5_pjT_ps"), c + 1)
                A.activation(pjT, ps[0:64, 4, :], ACT.Copy).then_inc(S("l5_pjT"), 1)
                for s in range(4):
                    e.wait_ge(S("l5_ctx"), 16 * c + 4 * s + 4)
                    if s:
                        e.wait_ge(S("l5_out"), 4 * c + s)
                    b = 2 * (s % 2)
                    A.activation(ctxT, ps[:, b:b + 2, :].rearrange("p a b -> p (a b)"), ACT.Copy)\
                        .then_inc(S("l5_ctxT"), 1)
                xT_scalar(e, 5, c, 7)

        def l5_gpsimd(e, step):
            for c in range(CHUNKS):
                after_chunk(e, 5, c)
                for j, i in enumerate(POOL5):
                    s, t = PAIRS5[i]
                    e.wait_ge(S("l5_qkv_sb"), 24 * c + 4 * max(s, t) + 4)
                    if j >= 2:
                        e.wait_ge(S("l5_dots"), 10 * c + j - 1)
                    P.tensor_tensor(prod5[:, j % 2, :], q5[:, s, :], k5[:, t, :], ALU.mult).then_inc(S("l5_prod"), 1)
                e.wait_ge(S("l5_dots"), 10 * (c + 1))
                e.wait_ge(S("l5_pj"), c + 1)
                e.wait_ge(S("l5_qkv_sb"), 24 * (c + 1))
                for s in range(4):
                    if s >= 2:
                        e.wait_ge(S("l5_ctx"), 16 * c + 4 * s - 4)
                    P.tensor_tensor(prod5[:, s % 2, :].rearrange("p (h d) -> p h d", h=H),
                                    v5[:, 3, :].rearrange("p (h d) -> p h d", h=H),
                                    sc5[:, s, 3, :].unsqueeze(2).to_broadcast([128, H, HD5]), ALU.mult)\
                        .then_inc(S("l5_pv_pool"), 1)
                ln_gpsimd(e, step, 5, c)

        def l5_vector(e, step):
            after_chunk(e, 5, 0)
            e.wait_ge(S("ld_b5"), 16)
            step(V.tensor_copy(b5p[:, 0, :], b5f))
            step.wait()
            step(V.tensor_tensor(b5f, b5f, b5p[:, 0, :], ALU.subtract))
            step.wait()
            step(V.tensor_copy(b5p[:, 1, :], b5f))
            step.wait()
            V.tensor_tensor(b5p[:, 2, :], b5f, b5p[:, 1, :], ALU.subtract).then_inc(S("l5_b5p"), 1)
            for c in range(CHUNKS):
                after_chunk(e, 5, c)
                step(V.memset(pj5, 0.0))
                for i, (s, t) in enumerate(PAIRS5):
                    if i in DVE5:
                        step.wait()
                        e.wait_ge(S("l5_qkv_sb"), 24 * c + 4 * max(s, t) + 4)
                        step(V.tensor_tensor(pv5[:, 0, :], q5[:, s, :], k5[:, t, :], ALU.mult))
                        step.wait()
                        step(V.tensor_reduce(sc5[:, s, t, :], pv5[:, 0, :].rearrange("p (h d) -> p h d", h=H),
                                             AX.X, ALU.add))
                        continue
                    j = POOL5.index(i)
                    e.wait_ge(S("l5_prod"), 10 * c + j + 1)
                    V.tensor_reduce(sc5[:, s, t, :], prod5[:, j % 2, :].rearrange("p (h d) -> p h d", h=H),
                                    AX.X, ALU.add).then_inc(S("l5_dots"), 1)
                step.wait()
                e.wait_ge(S("l5_dots"), 10 * (c + 1))
                e.wait_ge(S("l5_qd"), c + 1)
                for off in range(-3, 4):
                    v, lo, hi = by_offset(sc5, off)
                    step(V.tensor_tensor(v, v, qd5[:, lo:hi, :, abs(off)], ALU.add))
                step.wait()
                by_t = sc5.rearrange("p s t h -> p s h t")
                step(V.tensor_reduce(mx5, by_t, AX.X, ALU.max))
                step.wait()
                V.tensor_tensor(sc5, sc5, mx5.unsqueeze(2).to_broadcast([128, 4, 4, H]), ALU.subtract)\
                    .then_inc(S("l5_shift"), 1)
                e.wait_ge(S("l5_exp"), c + 1)
                step(V.tensor_reduce(mx5, by_t, AX.X, ALU.add))
                step.wait()
                step(V.reciprocal(mx5, mx5))
                step.wait()
                step(V.tensor_tensor(sc5, sc5, mx5.unsqueeze(2).to_broadcast([128, 4, 4, H]), ALU.mult))
                step.wait()
                for off in (0, 1, 2, 3, -1, -2, -3):
                    v, lo, hi = by_offset(sc5, off)
                    dst = pj5[:, lo:hi, :, abs(off)]
                    if off == -1:
                        step.wait()
                    ins = V.tensor_tensor(dst, dst, v, ALU.add)
                    if off == -3:
                        ins.then_inc(S("l5_pj"), 1)
                    else:
                        step(ins)
                e.wait_ge(S("l5_qkv_sb"), 24 * (c + 1))
                for j in range(12):
                    s, t = j // 3, j % 3
                    if j >= 2:
                        e.wait_ge(S("l5_ctx"), 16 * c + 4 * ((j - 2) // 3) + (j - 2) % 3 + 1)
                    V.tensor_tensor(pv5[:, j % 2, :].rearrange("p (h d) -> p h d", h=H),
                                    v5[:, t, :].rearrange("p (h d) -> p h d", h=H),
                                    sc5[:, s, t, :].unsqueeze(2).to_broadcast([128, H, HD5]), ALU.mult)\
                        .then_inc(S("l5_pv"), 1)
                e.wait_ge(S("l5_out"), 4 * (c + 1))
                residual_vector(e, step, 5, c, 5)
                ln_vector(e, step, 5, c)

        PHASES = (13, 12, 12, 12)
        CAP = 60.0
        small6 = small5
        row6 = sf[0:4, :]
        s6, E6, junk6, kinv6 = row6[:, 0:1024], row6[:, 1024:2048], row6[:, 2048:3072], row6[:, 3072:4096]
        z6 = hf[0:4, 0:1024]
        col6 = small6[0:4, 0:16]
        smax6, L6, ctr6, tmp6, lnu6 = (col6[:, i:i + 1] for i in range(5))
        u6 = col6[:, 8:10]
        zcol, count6 = small6[:, 16:20], small6[:, 32:48]
        G6, e6, rank6 = small6[:, 64:68], small6[:, 68:72], small6[:, 72:76]
        zrow = big[:, 0:1024]
        zjunk = big[:, 1024:2048]
        hl6, hh6 = big[:, 2048:2560], big[:, 2560:3072]
        gl6 = big[0:64, 5120:5632]
        gh6 = big[:, 5632:7680].rearrange("p (k n) -> p k n", k=4)
        LOG_N_OVER_K = math.log(SEQ / K_EFF)

        def l6_tensor(e):
            after_turn(e, 6, 0)
            e.wait_ge(S("ld_w6"), 16 * 13)
            e.wait_ge(S("ld_w6h"), 16 * 4)
            for i in range(4):
                T.transpose(ps[:, 0, 128 * i:128 * i + 128], f1hn[:, i, :], ident)
                T.transpose(ps[:, 1, 128 * i:128 * i + 128], f2hn[:, i, :], ident)
            T.transpose(ps[:, 2, 0:64], f1ln[:], F("ident", 64)[:, 0:64])
            T.transpose(ps[0:64, 3, 0:128], f2ln[:], ident).then_inc(S("wT_ps"), 1)
            for half in range(2):
                for b in range(4):
                    at = SEQ * b + 512 * half
                    mm = T.matmul(ps[0:4, 4 + half, :], rt[:, b, :], xT[:, at:at + 512], start=b == 0, stop=b == 3)
            mm.then_inc(S("l6_s_ps"), 1)
            e.wait_ge(S("wT"), 22)
            e.wait_ge(S("l6_z"), 1)
            for c in range(CHUNKS):
                b = c // 2
                after_turn(e, 6, c)
                for half in range(2):
                    mm = T.matmul(bank(half), F("selb", 4)[:, 128 * b:128 * b + 128], z6[:, 512 * half:512 * half + 512],
                                  start=True, stop=True)
                mm.then_inc(S("l6_zrow_ps"), 1)
                turn_tensor(e, hx, "rms", 16 + c, 2)
                e.wait_ge(S("l6_h"), 2 * (c + 1))
                T.matmul(ps[0:64, 3, :], f1lT[:], hl6, start=True, stop=True).then_inc(S("l6_up"), 1)
                for k in range(4):
                    if k >= 1:
                        e.wait_ge(S("l6_gelu"), 5 * c + k)
                    T.matmul(bank(2 + k % 2), f1hT[:, k, :], hh6, start=True, stop=True).then_inc(S("l6_up"), 1)
                e.wait_ge(S("l6_gelu"), 5 * (c + 1))
                for t in range(4):
                    cols = slice(128 * t, 128 * t + 128)
                    T.matmul(ps[:, 4, cols], gl6[:, cols], f2lT[:], start=True, stop=False)
                    T.matmul(ps[:, 4, cols], ones_row, fb2[:, 0, :], start=False, stop=True)
                for t in range(4):
                    cols = slice(128 * t, 128 * t + 128)
                    for k in range(4):
                        T.matmul(ps[:, 5, cols], gh6[:, k, cols], f2hT[:, k, :], start=k == 0, stop=False)
                    mm = T.matmul(ps[:, 5, cols], ones_row, fb2[:, 1, :], start=False, stop=True)
                mm.then_inc(S("l6_out"), 1)
                xT_tensor(e, 6, c, 7)

        def l6_scalar(e):
            e.wait_ge(S("wT_ps"), 19)
            A.activation(flat(f1hT), bank(0), ACT.Copy).then_inc(S("wT"), 1)
            A.activation(flat(f2hT), bank(1), ACT.Copy).then_inc(S("wT"), 1)
            A.activation(f1lT[:], ps[:, 2, 0:64], ACT.Copy).then_inc(S("wT"), 1)
            A.activation(f2lT[:], ps[0:64, 3, 0:128], ACT.Copy).then_inc(S("wT"), 1)
            for p in range(len(PHASES)):
                e.wait_ge(S("l6_centred"), p + 1)
                A.activation(E6, E6, ACT.Exp).then_inc(S("l6_exp"), 1)
                A.activation(u6[:, 0:1], tmp6, ACT.Exp).then_inc(S("l6_exp"), 1)
                e.wait_ge(S("l6_stepped"), p + 1)
                A.activation(lnu6, u6[:, PHASES[p] % 2:PHASES[p] % 2 + 1], ACT.Ln).then_inc(S("l6_ln"), 1)
            for c in range(CHUNKS):
                after_chunk(e, 6, c)
                e.wait_ge(S("l6_zrow_ps"), c + 1)
                A.activation(zrow, ps[:, 0:2, :].rearrange("p a b -> p (a b)"), ACT.Copy).then_inc(S("l6_zrow"), 1)
                e.wait_ge(S("l6_zcol"), 4 * (c + 1))
                A.activation(e6, zcol, ACT.Exp).then_inc(S("l6_e"), 1)
                e.wait_ge(S("rms_T_ps"), 17 + c)
                A.activation(hl6, bank(2), ACT.Copy, scale=gam[:, 0:1]).then_inc(S("l6_h"), 1)
                A.activation(hh6, bank(2), ACT.Copy, scale=gam[:, 1:2]).then_inc(S("l6_h"), 1)
                e.wait_ge(S("l6_up"), 5 * c + 1)
                A.activation(gl6, ps[0:64, 3, :], ACT.Gelu, bias=fb1l[:]).then_inc(S("l6_gelu"), 1)
                for k in range(4):
                    e.wait_ge(S("l6_up"), 5 * c + k + 2)
                    A.activation(gh6[:, k, :], bank(2 + k % 2), ACT.Gelu, bias=fb1h[:, k:k + 1])\
                        .then_inc(S("l6_gelu"), 1)
                xT_scalar(e, 6, c, 7)

        def l6_gpsimd(e, step):
            after_chunk(e, 6, 0)
            P.memset(kinv6, 1.0 / K_EFF).then_inc(S("l6_kinv"), 1)
            for c in range(CHUNKS):
                after_chunk(e, 6, c)
                rms_gpsimd(e, step, "rms", 16 + c, 1.0, ALU.max, 1e-24)
                ln_gpsimd(e, step, 6, c)

        def l6_vector(e, step):
            e.wait_ge(S("l6_s_ps"), 1)
            after_chunk(e, 6, 0)
            step(V.tensor_copy(s6, ps[0:4, 4:6, :].rearrange("p a b -> p (a b)")))
            step(V.memset(L6, LOG_N_OVER_K))
            step.wait()
            step(V.tensor_reduce(smax6, s6, AX.X, ALU.max))
            step.wait()
            e.wait_ge(S("l6_kinv"), 1)
            for p, n in enumerate(PHASES):
                step(V.tensor_tensor(ctr6, L6, smax6, ALU.min))
                step.wait()
                step(V.tensor_scalar(tmp6, L6, ctr6, CAP, ALU.subtract, ALU.min))
                step.wait()
                V.tensor_scalar(E6, s6, ctr6, CAP, ALU.subtract, ALU.min).then_inc(S("l6_centred"), 1)
                e.wait_ge(S("l6_exp"), 2 * (p + 1))
                for i in range(n):
                    ins = V.scalar_tensor_tensor(junk6, E6, u6[:, i % 2:i % 2 + 1], kinv6, ALU.min, ALU.mult,
                                                 accum_out=u6[:, (i + 1) % 2:(i + 1) % 2 + 1])
                    if i == n - 1:
                        ins.then_inc(S("l6_stepped"), 1)
                    else:
                        step(ins)
                        step.wait()
                e.wait_ge(S("l6_ln"), p + 1)
                step(V.tensor_tensor(L6, ctr6, lnu6, ALU.add))
                step.wait()
            V.tensor_scalar(z6, s6, L6, 0.0, ALU.subtract, ALU.min).then_inc(S("l6_z"), 1)

            for c in range(CHUNKS):
                half = c % 2
                after_chunk(e, 6, c)
                rms_vector(e, step, xs(6, c), hx, "rms", 16 + c, float(D) ** 0.5)
                e.wait_ge(S("l6_zrow"), c + 1)
                for t in range(4):
                    q = 128 * (4 * half + t)
                    step.wait()
                    V.scalar_tensor_tensor(zjunk[:, 0:128], zrow[:, q:q + 128], 1.0, ident, ALU.mult, ALU.mult,
                                           accum_out=zcol[:, t:t + 1]).then_inc(S("l6_zcol"), 1)
                    e.wait_ge(S("l6_zcol"), 4 * c + t + 1)
                    z, cnt = zcol[:, t:t + 1], count6[:, 4 * t:4 * t + 4]
                    if q:
                        step(V.tensor_scalar(zjunk[:, 0:q], zrow[:, 0:q], z, None, ALU.is_ge, ALU.add,
                                             accum_out=cnt[:, 0:1]))
                    else:
                        step(V.memset(cnt[:, 0:1], 0.0))
                    if q + 128 < SEQ:
                        step.wait()
                        step(V.tensor_scalar(zjunk[:, 0:SEQ - q - 128], zrow[:, q + 128:SEQ], z, None, ALU.is_gt,
                                             ALU.add, accum_out=cnt[:, 1:2]))
                    else:
                        step(V.memset(cnt[:, 1:2], 0.0))
                    step.wait()
                    step(V.tensor_scalar(zjunk[:, 0:128], zrow[:, q:q + 128], z, None, ALU.is_gt, ALU.add,
                                         accum_out=cnt[:, 2:3]))
                    step.wait()
                    step(V.scalar_tensor_tensor(zjunk[:, 0:128], zrow[:, q:q + 128], z, B("before"),
                                                ALU.is_equal, ALU.mult, accum_out=cnt[:, 3:4]))
                step.wait()
                step(V.tensor_reduce(rank6, count6.rearrange("p (t k) -> p t k", t=4), AX.X, ALU.add))
                step.wait()
                e.wait_ge(S("l6_e"), c + 1)
                step(V.tensor_scalar(G6, e6, -1.0, 1.0, ALU.mult, ALU.add))
                step(V.tensor_scalar(rank6, rank6, float(K_HEAVY), None, ALU.is_lt))
                step.wait()
                step(V.tensor_tensor(G6, G6, e6, ALU.add))
                step.wait()
                step(V.tensor_tensor(G6, G6, rank6, ALU.mult))
                e.wait_ge(S("l6_out"), c + 1)
                step(V.tensor_tensor(flat(y[:, half]), bank(4), flat(xs(6, c)), ALU.add))
                step.wait()
                for t in range(4):
                    step(V.scalar_tensor_tensor(y[:, half, t, :], ps[:, 5, 128 * t:128 * t + 128], G6[:, t:t + 1],
                                                y[:, half, t, :], ALU.mult, ALU.add))
                ln_vector(e, step, 6, c)

        def l7_tensor(e):
            e.wait_ge(S("ld_w7"), 32)
            for c in range(CHUNKS):
                after_turn(e, 7, c)
                for t in range(4):
                    mm = T.matmul(ps[:, 1 + t, 0:384], xT[:, 512 * c + 128 * t:512 * c + 128 * (t + 1)], w7[:],
                                  start=True, stop=True)
                mm.then_inc(S("l7_qkv"), 1)
                narrow_tensor(e, l7n, c, kstack)
                finish_tensor(e, 7, c, w7o[:], None, 0, 1)
                xT_tensor(e, 7, c, 7)

        def l7_scalar(e):
            view = "p (t h) d -> p t (h d)"
            for c in range(CHUNKS):
                after_chunk(e, 7, c)
                e.wait_ge(S("l7_qkv"), c + 1)
                qkv = ps[:, 1:5, :]
                A.activation(kf[:].rearrange(view, t=4), qkv[:, :, 128:256], ACT.Copy).then_inc(S("nr_qk_sb"), 1)
                A.activation(qf[:].rearrange(view, t=4), qkv[:, :, 0:128], ACT.Copy).then_inc(S("nr_qk_sb"), 1)
                A.activation(v1[:, 4 * (c % 2):4 * (c % 2) + 4, :, 0:8],
                             qkv[:, :, 256:384].rearrange("p t (h d) -> p t h d", d=8),
                             ACT.Copy).then_inc(S("nr_qk_sb"), 1)
                e.wait_ge(S("nr_kparts"), CHUNKS + c + 1)
                fill_keys_scalar(e, 64, "nr_kstack")
                stack_evac(e, act_copy, kT, H, "nr_kT", c + 2, 6, c % 2)
                narrow_second_scalar(e, l7n, c)
                finish_scalar(e, 7, c, 0)
                xT_scalar(e, 7, c, 7)

        def l7_gpsimd(e, step):
            for c in range(CHUNKS):
                after_chunk(e, 7, c)
                narrow_gpsimd(e, step, l7n, c, kstack)
                ln_gpsimd(e, step, 7, c)

        def l7_vector(e, step):
            for c in range(CHUNKS):
                after_chunk(e, 7, c)
                narrow_vector(e, step, l7n, c)
                e.wait_ge(S("nr_out"), CHUNKS + c + 1)
                residual_vector(e, step, 7, c, 1)
                ln_vector(e, step, 7, c)

        mean8 = small5[:, 0:4]
        r8 = big[:, 0:2048].rearrange("p (k n) -> p k n", k=4)

        def l8_tensor(e):
            after_turn(e, 8, 0)
            for b in range(SEQS):
                for t in range(QT):
                    mm = T.matmul(ps[:, 0, b:b + 1], x[:, QT * b + t, :], F("mean"), start=t == 0, stop=t == QT - 1)
            mm.then_inc(S("l8_mean_ps"), 1)
            e.wait_ge(S("l8_mean"), 1)
            e.wait_ge(S("ld_w8r"), 32)
            for b in range(SEQS):
                T.matmul(ps[0:1, 1, 8 * b:8 * b + 8], mean8[:, b:b + 1], w8r[:], start=True, stop=False)
                mm = T.matmul(ps[0:1, 1, 8 * b:8 * b + 8], ones_row[:, 0:1], b8r[:], start=False, stop=True)
            mm.then_inc(S("l8_scores"), 1)
            for c in range(CHUNKS):
                b = c // 2
                e.wait_ge(S(f"ld_w8e{b}"), 16 * 7)
                after_chunk(e, 8, c)
                for k in range(4):
                    T.matmul(bank(k), w8a[:, b % 2, 128 * k:128 * k + 128], xT[:, 512 * c:512 * c + 512],
                             start=True, stop=True).then_inc(S("l8_up"), 1)
                e.wait_ge(S("l8_relu"), 4 * (c + 1))
                for t in range(4):
                    cols = slice(128 * t, 128 * t + 128)
                    for k in range(4):
                        T.matmul(ps[:, 4, cols], r8[:, k, cols], w8b[:, b % 2, k, :], start=k == 0, stop=False)
                    mm = T.matmul(ps[:, 4, cols], ones_row, b8b2[:, b % 2, :], start=False, stop=True)
                mm.then_inc(S("l8_out"), 1)

        def l8_scalar(e):
            for c in range(CHUNKS):
                b = c // 2
                after_chunk(e, 8, c)
                e.wait_ge(S(f"ld_w8e{b}"), 16 * 7)
                for k in range(4):
                    e.wait_ge(S("l8_up"), 4 * c + k + 1)
                    A.activation(r8[:, k, :], bank(k), ACT.Relu, bias=b8b1[:, b % 2, k:k + 1])\
                        .then_inc(S("l8_relu"), 1)

        def l8_gpsimd(e, step):
            for c in range(CHUNKS):
                ln_gpsimd(e, step, 8, c)

        def l8_vector(e, step):
            e.wait_ge(S("l8_mean_ps"), 1)
            V.tensor_copy(mean8, ps[:, 0, 0:4]).then_inc(S("l8_mean"), 1)
            e.wait_ge(S("l8_scores"), 1)
            step(V.tensor_copy(sc8[:], ps[0:1, 1, 0:32].rearrange("p (b e) -> p b e", b=4)))
            step.wait()
            for b in range(SEQS):
                step(V.max(top8[:, b, :], sc8[:, b, :]))
            step.wait()
            for b in range(SEQS):
                V.max_index(top_idx[:, b, :], top8[:, b, :], sc8[:, b, :]).then_inc(S("l8_top"), 1)
            for c in range(CHUNKS):
                after_chunk(e, 8, c)
                e.wait_ge(S("l8_out"), c + 1)
                residual_vector(e, step, 8, c, 4)
                ln_vector(e, step, 8, c)


        @block.tensor
        def _(e):
            l1_tensor(e)
            l2_tensor(e)
            l3_tensor(e)
            l4_tensor(e)
            l5_tensor(e)
            l6_tensor(e)
            l7_tensor(e)
            l8_tensor(e)

        @block.scalar
        def _(e):
            l1_scalar(e)
            l2_scalar(e)
            l3_scalar(e)
            l4_scalar(e)
            l5_scalar(e)
            l6_scalar(e)
            l7_scalar(e)
            l8_scalar(e)

        @block.gpsimd
        def _(e):
            step = Chain(e, S("pool_step"))
            l1_gpsimd(e, step)
            l2_gpsimd(e, step)
            l3_gpsimd(e, step)
            l4_gpsimd(e, step)
            l5_gpsimd(e, step)
            l6_gpsimd(e, step)
            l7_gpsimd(e, step)
            l8_gpsimd(e, step)

        @block.vector
        def _(e):
            step = Chain(e, S("dve_step"))
            l1_vector(e, step)
            l2_vector(e, step)
            l3_vector(e, step)
            l4_vector(e, step)
            l5_vector(e, step)
            l6_vector(e, step)
            l7_vector(e, step)
            l8_vector(e, step)


_OUTS = [((SEQS, SEQ, D), "float32")]


def kernel(**inputs):
    import numpy as _np
    import concourse.bacc as _bacc
    from concourse import mybir as _mybir
    from concourse.bass_utils import run_bass_kernel_spmd as _run

    nc = _bacc.Bacc("TRN2", target_bir_lowering=False, num_devices=1)
    const_f, const_b = constants()
    every = dict(inputs)
    every["const_f"], every["const_b"] = const_f, const_b
    arrays, args = {}, {}
    for name, value in every.items():
        v = _np.ascontiguousarray(value)
        arrays[f"in_{name}_dram"] = v
        args[name] = nc.dram_tensor(f"in_{name}_dram", v.shape, _mybir.dt.from_np(v.dtype), kind="ExternalInput").ap()
    shape, dtype = _OUTS[0]
    out = nc.dram_tensor("out_0_dram", shape, _mybir.dt.from_np(_np.dtype(dtype)), kind="ExternalOutput").ap()
    program(nc, args, out)
    r = _run(nc, [arrays], core_ids=[0])
    return r.results[0]["out_0_dram"]
```

```python
import math
from contextlib import ExitStack

import concourse.bass as bass
from concourse import mybir

F32 = mybir.dt.float32
BF16 = mybir.dt.bfloat16
U32 = mybir.dt.uint32
ALU = mybir.AluOpType
ACT = mybir.ActivationFunctionType
AX = mybir.AxisListType

D = 128
SEQS, SEQ = 4, 1024
TILES = SEQS * SEQ // 128
QT = SEQ // 128
CHUNKS = TILES // 4
H, HD = 16, 8
SLOT = 64
PAIRS = 8
EPS = 1e-5
K_HEAVY = 128
K_EFF = 144.0


def columns(sizes):
    table, at = {}, 0
    for name, n in sizes:
        table[name] = (at, at + n)
        at += n
    return table, at


CF, CF_N = columns([("ident", 128), ("cos", 64), ("sin", 64), ("lt16", 256), ("lt8", 64), ("lt4", 16),
                    ("ones", 128), ("eps", 1), ("mean", 1), ("mhalf", 4), ("selb", 512)])
CB, CB_N = columns([("ident", 128), ("causal", 128), ("causalT", 128), ("behind", 64), ("behindT", 64),
                    ("winc", 128), ("wincT", 128), ("sel8", 1024), ("sel16", 1024), ("before", 128), ("ones", 128)])


def constants():
    import numpy as np

    f = np.zeros((128, CF_N), np.float32)
    b = np.zeros((128, CB_N), np.float32)
    p = np.arange(128)

    def put(m, table, name, rows, value):
        lo, hi = table[name]
        m[rows, lo:hi] = value

    every = slice(None)
    put(f, CF, "ident", every, np.eye(128))
    inv = (np.float32(1.0) / np.float32(10000.0) ** (np.arange(4, dtype=np.float32) / np.float32(4))).astype(np.float32)
    cos = np.zeros((128, 8, 8), np.float32)
    sin = np.zeros((128, 8, 8), np.float32)
    for t in range(8):
        ang = ((p + 128 * t).astype(np.float32)[:, None] * inv).astype(np.float32)
        cos[:, t, 0:4] = cos[:, t, 4:8] = np.cos(ang)
        sin[:, t, 0:4] = -np.sin(ang)
        sin[:, t, 4:8] = np.sin(ang)
    put(f, CF, "cos", every, cos.reshape(128, 64))
    put(f, CF, "sin", every, sin.reshape(128, 64))
    for n in (16, 8, 4):
        lt = (np.arange(n)[None, :] < np.arange(n)[:, None]).astype(np.float32)
        put(f, CF, f"lt{n}", every, lt.reshape(1, n * n))
    put(f, CF, "ones", every, 1.0)
    put(f, CF, "eps", every, EPS)
    put(f, CF, "mean", every, 1.0 / SEQ)
    put(f, CF, "mhalf", every, -0.5)
    put(f, CF, "selb", slice(0, 4), np.repeat(np.eye(4), 128, axis=1))

    neg = -1e30
    q, k = np.meshgrid(p, p, indexing="ij")
    causal = np.where(k <= q, 0.0, neg)
    window = np.where((k <= q) & (q - k <= 63), 0.0, neg)
    behind = np.where(q + 128 - k <= 63, 0.0, neg)
    put(b, CB, "ident", every, np.eye(128))
    put(b, CB, "causal", every, causal)
    put(b, CB, "causalT", every, causal.T)
    put(b, CB, "behind", every, behind[:, 64:])
    put(b, CB, "behindT", every, behind.T[:, :64])
    put(b, CB, "winc", every, window)
    put(b, CB, "wincT", every, window.T)
    sel8 = np.zeros((24, 8, 128), np.float32)
    sel16 = np.zeros((48, 8, 128), np.float32)
    for part in range(3):
        for e in range(8):
            sel8[part * 8 + e, e, :] = 1
            sel16[part * 16 + 2 * e, e, 0:64] = 1
            sel16[part * 16 + 2 * e + 1, e, 64:128] = 1
    put(b, CB, "sel8", slice(0, 24), sel8.reshape(24, 1024))
    put(b, CB, "sel16", slice(0, 48), sel16.reshape(48, 1024))
    put(b, CB, "before", every, p[None, :] < p[:, None])
    put(b, CB, "ones", every, 1.0)
    return f, b


def program(nc, a, out):
    ctx = ExitStack()
    with ctx:
        def sb(name, shape, dt=F32):
            return ctx.enter_context(nc.sbuf_tensor(name, shape, dt))

        sems = {}

        def S(name):
            if name not in sems:
                sems[name] = ctx.enter_context(nc.semaphore(name))
            return sems[name]

        V, P, T, A = nc.vector, nc.gpsimd, nc.tensor, nc.scalar

        ps = ctx.enter_context(nc.psum_tensor("ps", [128, 8, 512], F32))
        cf = sb("cf", [128, CF_N])
        cb = sb("cb", [128, CB_N], BF16)

        def F(name, rows=128):
            return cf[0:rows, CF[name][0]:CF[name][1]]

        def B(name, rows=128):
            return cb[0:rows, CB[name][0]:CB[name][1]]

        ident, identb = F("ident"), B("ident")
        ones_row = F("ones", 1)

        def bank(i):
            return ps[:, i, :]

        def bank_bf(i):
            return ps[:, i, :].bitcast(BF16)

        def flat(ap):
            return ap.rearrange("p t d -> p (t d)")

        x = sb("x", [128, TILES, D])
        xT = sb("xT", [128, TILES * 128])
        y = sb("y", [128, 2, 4, D])
        stats = sb("stats", [128, 2, 4, 6])
        mv = sb("mv", [128, 2, 4, 2])
        ve = sb("ve", [128, 2, 4])
        rs = sb("rs", [128, 2, 4])

        w1T = sb("w1T", [128, 4, 128])
        w3T = w1T[:, 0:3, :]
        brow = sb("brow", [1, 512])
        b1 = brow[:]
        fb2 = brow[:, 0:256].rearrange("p (a n) -> p a n", a=2)
        b8b2 = brow[:, 256:512].rearrange("p (a n) -> p a n", a=2)
        w2 = sb("w2", [128, 192])
        w2o = sb("w2o", [128, 128])
        ln12 = sb("ln12", [128, 2])
        w2r = sb("w2r", [128, 8])
        w2x = sb("w2x", [128, 6144])
        w2g = w2x[:, 0:2048].rearrange("p (e f) -> p e f", e=8)
        w2u = w2x[:, 2048:4096].rearrange("p (e f) -> p e f", e=8)
        w2d = w2x[:, 4096:6144].rearrange("p (e f) -> p e f", e=16)
        w5n = w2x[:, 0:3072].rearrange("p (a b) -> p a b", a=24)
        w5on = w2x[:, 3072:4096].rearrange("p (a b) -> p a b", a=8)
        w6x = w2x[:, 4096:6144].rearrange("p (a b) -> p a b", b=128)
        f1hn, f2hn, f1hT, f2hT = w6x[:, 0:4, :], w6x[:, 4:8, :], w6x[:, 8:12, :], w6x[:, 12:16, :]
        w8a = w2x[:, 0:1024].rearrange("p (b n) -> p b n", b=2)
        w8b = w2x[:, 1024:2048].rearrange("p (b c n) -> p b c n", b=2, c=4)
        w3 = sb("w3", [128, 3, 128])
        w4r = sb("w4r", [16, 128])
        w4rT = sb("w4rT", [128, 16])
        ebias = sb("ebias", [128, 16])
        kdb = sb("kdb", [128, 8])
        vdb = sb("vdb", [128, 128])
        b5q = sb("b5q", [128, 8])
        qk5 = sb("qk5", [128, 64])
        rb5 = sb("rb5", [1, 64])
        b5o = sb("b5o", [1, 128])
        rt = sb("rt", [128, 4, 4])
        gam = sb("gam", [128, 2])
        f1ln, f2lT = w2x[0:64, 2560:2688], w2x[0:64, 2688:2816]
        f1lT, f2ln = w2x[:, 2816:2880], w2x[:, 2880:2944]
        fb1l = sb("fb1l", [64, 1])
        fb1h = sb("fb1h", [128, 4])
        w7, w7o = w2x[:, 2048:2432], w2x[:, 2432:2560]
        w8r = sb("w8r", [128, 8])
        b8r = sb("b8r", [1, 8])
        b8b1 = sb("b8b1", [128, 2, 4])

        heads = sb("heads", [128, 4, 64, HD])
        qf, kf, qr, kr = heads[:, 0], heads[:, 1], heads[:, 2], heads[:, 3]
        parts = sb("parts", [128, 6, 64, HD], BF16)
        qp, kp = parts[:, 0:3], parts[:, 3:6]
        stacks = sb("stacks", [128, 2, 64, SLOT], BF16)
        qstack, kstack = stacks[:, 0], stacks[:, 1]
        turned = sb("turned", [128, 2, PAIRS, SEQ], BF16)
        qT, kT = turned[:, 0], turned[:, 1]
        norm2 = sb("norm2", [128, 2, 64])
        norm2r = sb("norm2r", [128, 2, 64])
        norm2p = sb("norm2p", [128, 2, 3, 64], BF16)
        values = sb("values", [128, 2, QT, H, HD + 1])
        values_g = sb("values_g", [128, 2, QT, 4, HD + 1])
        heads_v = values
        nm = sb("nm", [128, 64])
        nmr = sb("nmr", [128, 64])
        m2 = sb("m2", [128, 16])
        orec = sb("orec", [128, 4, H])
        on = sb("on", [128, 4, D])
        oT = sb("oT", [128, 512])
        pTr = sb("pTr", [128, 2, QT, 128])
        obuf = sb("obuf", [128, 2, 512])
        w1 = pTr[:, 0, 0:4, :]
        hf = heads[:].rearrange("p a n d -> p (a n d)")
        vw5 = hf[0:64, 1024:1152]
        sf = stacks[:].rearrange("p a n s -> p (a n s)").bitcast(F32)
        q3T, k3T = sf[:, 0:1024], sf[:, 1024:2048]
        v3 = sf[:, 2048:3072].rearrange("p (t d) -> p t d", t=QT)
        tf = turned[:].rearrange("p a b c -> p (a b c)").bitcast(F32)
        w4n = tf[:, 0:3456].rearrange("p (a b) -> p a b", a=27)
        w4T = tf[:, 3456:6912].rearrange("p (a b) -> p a b", a=27)
        w5T = tf[:, 0:3072]
        w5oT = tf[:, 3072:4096].rearrange("p (a b) -> p a b", a=8)
        b5row = parts[0:3].rearrange("p a n d -> p (a n d)")

        big = sb("big", [128, 8192])
        b5f = big[0:1, 0:3072]
        b5p = big[0:1, 3072:7680].bitcast(BF16).rearrange("p (a n) -> p a n", a=3)
        RING = 8
        cb32 = big[:, 0:CB_N]
        ring = big[:].rearrange("p (r k) -> p r k", r=RING)
        pT2 = big[:, 0:3072].rearrange("p (u k q) -> p u k q", u=3, k=2)
        hx = big[:, 3072:3584].rearrange("p (t d) -> p t d", t=4)
        h1 = big[:, 3584:4096].rearrange("p (t d) -> p t d", t=4)
        hT = big[:, 4096:4608]
        hT2 = hT
        hx1 = big[:, 7168:7680].rearrange("p (t d) -> p t d", t=4)
        junk = big[:, 4608:5120].rearrange("p (t d) -> p t d", t=4)
        rot = big[:, 4608:5632].rearrange("p (a n d) -> p a n d", a=2, d=HD)
        gt, eq = big[:, 3072:4096], big[:, 7168:8192]
        sil = big[:, 0:1536].rearrange("p (a n) -> p a n", a=3)
        t1 = big[:, 1536:3072].rearrange("p (a n) -> p a n", a=3)
        act = big[:, 4608:6144].rearrange("p (a n) -> p a n", a=3)
        cbs = big[:, 6144:7168].rearrange("p (a n) -> p a n", a=2)
        lg = sb("lg", [128, 4, 16])
        lgm = sb("lgm", [128, 4])
        lge = sb("lge", [128, 4, 16])
        rk = sb("rk", [128, 64])
        msk = sb("msk", [128, 64])
        cw = sb("cw", [128, 4, 16])
        cwr = sb("cwr", [128, 4, 16])
        csum = sb("csum", [128, 4])
        crec = sb("crec", [128, 4])
        ssq = sb("ssq", [128, 4])
        cpart = sb("cpart", [128, 4, 48], BF16)
        cT = sb("cT", [48, 512], BF16)
        top8 = sb("top8", [1, 4, 8])
        top_idx = sb("top_idx", [1, 4, 8], U32)
        sc8 = sb("sc8", [1, 4, 8])

        block = ctx.enter_context(nc.Block())

        @block.sync
        def _(sp):
            loaded = {}

            def load(dst, src, name):
                sp.dma_start(dst, src).then_inc(S(name), 16)
                loaded[name] = loaded.get(name, 0) + 16

            def column(v):
                return v.rearrange("(p o) -> p o", o=1)

            def row(v):
                return v.rearrange("(o d) -> o d", o=1)

            xin = a["L0_attn_x"].rearrange("b (q p) d -> p (b q) d", p=128)
            load(cf[:], a["const_f"], "ld_cf")
            load(x[:, 0:8, :], xin[:, 0:8, :], "ld_x0")
            for i, w in enumerate(("wq", "wk", "wv", "wo")):
                load(w1[:, i, :], a[f"L0_attn_{w}"], "ld_w1")
            for i, w in enumerate(("bq", "bk", "bv", "bo")):
                load(b1[:, 128 * i:128 * (i + 1)], row(a[f"L0_attn_{w}"]), "ld_w1")
            load(cb32, a["const_b"], "ld_cb")
            for b in range(1, 4):
                load(x[:, 8 * b:8 * b + 8, :], xin[:, 8 * b:8 * b + 8, :], f"ld_x{b}")
            wq = a["L0_ffn_Wq"].rearrange("k (g p r d) -> k g p r d", g=2, p=2, r=4)
            for g in range(2):
                for p in range(2):
                    dst = w2[:, 64 * g:64 * g + 64].rearrange("k (r p d) -> k r p d", r=4, p=2)[:, :, p, :]
                    load(dst, wq[:, g, p], "ld_w2")
            load(w2[:, 128:160], a["L0_ffn_Wk"], "ld_w2")
            load(w2[:, 160:192], a["L0_ffn_Wv"], "ld_w2")
            load(w2o[:], a["L0_ffn_Wo"], "ld_w2")
            load(ln12[:, 0:1], column(a["L0_ffn_ln1_w"]), "ld_w2")
            load(ln12[:, 1:2], column(a["L0_ffn_ln2_w"]), "ld_w2")
            load(w2r[:], a["L0_ffn_Wr"], "ld_w2")
            for i, w in enumerate(("Wq", "Wk", "Wv")):
                load(w3[:, i, :], a[f"L1_attn_{w}"], "ld_w3")
            load(w4r[:], a["L1_ffn_router_weight"], "ld_w4r")
            load(ebias[:], row(a["L1_ffn_e_bias"]).to_broadcast([128, 16]), "ld_w4r")
            sp.wait_ge(S("const_zero"), 1)
            for half in range(2):
                rows = slice(64 * half, 64 * half + 64)
                for r in range(4):
                    load(kdb[rows, 4 * half + r:4 * half + r + 1], column(a["L2_attn_k_dist_emb"][r, :]), "ld_w5s")
                    at = 60 + 4 * half + r
                    load(vdb[rows, at:at + 1], column(a["L2_attn_v_dist_emb"][r, :]), "ld_w5s")
            for c in range(8):
                load(b5q[:, c:c + 1], column(a["L2_attn_b_in"][128 * c:128 * c + 128]), "ld_w5s")
            load(b5o[:], row(a["L2_attn_b_out"]), "ld_w5s")
            for r in range(4):
                load(rt[:, r, r:r + 1], column(a["L2_ffn_routing_token"]), "ld_w6")
            for i, g in enumerate(("l", "h")):
                load(gam[:, i:i + 1], column(a[f"L2_ffn_gamma_{g}"]), "ld_w6")
            load(fb1l[:], column(a["L2_ffn_b1_l"]), "ld_w6")
            for c in range(4):
                load(fb1h[:, c:c + 1], column(a["L2_ffn_b1_h"][128 * c:128 * c + 128]), "ld_w6")
            load(w8r[:], a["L3_ffn_Wr"], "ld_w6")
            load(b8r[:], row(a["L3_ffn_br"]), "ld_w6")
            sp.wait_ge(S("l1_pT_ps"), 2 * SEQS * QT * H)
            load(w2g, a["L0_ffn_Wg"].rearrange("e d f -> d e f"), "ld_w2x")
            load(w2u, a["L0_ffn_Wu"].rearrange("e d f -> d e f"), "ld_w2x")
            for j in range(2):
                load(w2d.rearrange("f (e j) d -> f e j d", j=2)[:, :, j, :],
                     a["L0_ffn_Wd"].rearrange("e (j f) d -> f e j d", f=128)[:, :, j, :], "ld_w2x")
            sp.wait_ge(S("ln_x"), 4 * 16)
            for i, g in enumerate(("l", "h")):
                load(fb2[:, i, :], row(a[f"L2_ffn_b2_{g}"]), "ld_w6h")
            load(w4n[:, 0:8, :], a["L1_ffn_gate_w"].rearrange("(g e) i h -> (e i) g h", e=2), "ld_w4")
            load(w4n[:, 8, :], a["L1_ffn_sh_gate_w"], "ld_w4")
            load(w4n[:, 9:17, :], a["L1_ffn_up_w"].rearrange("(g e) i h -> (e i) g h", e=2), "ld_w4")
            load(w4n[:, 17, :], a["L1_ffn_sh_up_w"], "ld_w4")
            for e2 in range(2):
                load(w4n[:, 18:26, 64 * e2:64 * e2 + 64],
                     a["L1_ffn_down_w"].rearrange("(g e) h i -> h g e i", e=2)[:, :, e2, :], "ld_w4")
            load(w4n[:, 26, :], a["L1_ffn_sh_down_w"], "ld_w4")
            for i in range(3):
                load(w5n[:, 8 * i:8 * i + 8, :],
                     a["L2_attn_W_in"][1024 * i:1024 * i + 1024, :].rearrange("(c p) d -> p c d", p=128), "ld_w5")
            load(w5on, a["L2_attn_W_out"].rearrange("o (c p) -> o c p", p=128), "ld_w5")
            load(f1hn, a["L2_ffn_w1_h"].rearrange("(c p) d -> p c d", p=128), "ld_w6h")
            load(f2hn, a["L2_ffn_w2_h"].rearrange("o (c p) -> o c p", p=128), "ld_w6h")
            sp.wait_ge(S("ln_x"), 4 * 32)
            load(b5f, row(a["L2_attn_b_in"]), "ld_b5")
            sp.wait_ge(S("l5_b5p"), 1)
            for j in range(3):
                load(b5row[j:j + 1, :], b5p[:, j, :], "ld_b5row")
            sp.wait_ge(S("ln_x"), 4 * 40)
            load(f1ln, a["L2_ffn_w1_l"], "ld_w6h")
            load(f2ln, a["L2_ffn_w2_l"], "ld_w6h")
            load(w7, a["L3_attn_Wqkv"], "ld_w7")
            load(w7o, a["L3_attn_Wout"], "ld_w7")
            sp.wait_ge(S("l8_top"), 4)
            for b in range(SEQS):
                if b >= 2:
                    sp.wait_ge(S("ln_x"), 4 * (7 * CHUNKS + 2 * (b - 1)))
                chosen = sp.value_load(top_idx[0:1, b, 0:1], min_val=0, max_val=7)
                one = bass.ds(chosen, 1)
                load(w8a[:, b % 2, :], a["L3_ffn_W1"][one].rearrange("e p n -> (e p) n"), f"ld_w8e{b}")
                for k in range(4):
                    load(b8b1[:, b % 2, k:k + 1],
                         a["L3_ffn_b1"][one][:, 128 * k:128 * k + 128].rearrange("e (p o) -> (e p) o", o=1),
                         f"ld_w8e{b}")
                load(w8b[:, b % 2, :, :], a["L3_ffn_W2"][one].rearrange("e (c p) n -> p (e c) n", p=128),
                     f"ld_w8e{b}")
                load(b8b2[:, b % 2, :], a["L3_ffn_b2"][one], f"ld_w8e{b}")
            o_dram = out.rearrange("b (q p) d -> p (b q) d", p=128)
            for c in range(CHUNKS):
                sp.wait_ge(S("ln_x"), 4 * (7 * CHUNKS + c + 1))
                sp.dma_start(o_dram[:, 4 * c:4 * c + 4, :], x[:, 4 * c:4 * c + 4, :]).then_inc(S("stored"), 16)
            sp.wait_ge(S("stored"), 16 * CHUNKS)
            for name, count in loaded.items():
                sp.wait_ge(S(name), count)

        class Chain:

            def __init__(self, eng, sem):
                self.eng, self.sem, self.n = eng, sem, 0

            def __call__(self, ins):
                ins.then_inc(self.sem, 1)
                self.n += 1

            def wait(self):
                self.eng.wait_ge(self.sem, self.n)

        def chunk_tiles(n, c):
            return range(c, 32, 8) if n == 5 else range(4 * c, 4 * c + 4)

        def xs(n, c):
            return x[:, c:32:8, :] if n == 5 else x[:, 4 * c:4 * c + 4, :]

        def xTs(n, c):
            if n == 5:
                return xT[:].rearrange("p (s q t) -> p s q t", s=4, q=8)[:, :, c, :]
            return xT[:, 512 * c:512 * c + 512].rearrange("p (s t) -> p s t", s=4)

        def ln_vector(e, step, n, c):
            k, h = (n - 1) * CHUNKS + c, c % 2
            step.wait()
            for t in range(4):
                step(V.bn_stats(stats[:, h, t, :], y[:, h, t, :]))
            step.wait()
            for t in range(4):
                V.bn_aggr(mv[:, h, t, :], stats[:, h, t, :]).then_inc(S("ln_var"), 1)
            e.wait_ge(S("ln_rs"), k + 1)
            for t, tile in enumerate(chunk_tiles(n, c)):
                V.tensor_scalar(x[:, tile, :], y[:, h, t, :], mv[:, h, t, 0:1], rs[:, h, t:t + 1],
                                ALU.subtract, ALU.mult).then_inc(S("ln_x"), 1)

        def ln_gpsimd(e, step, n, c):
            k, h = (n - 1) * CHUNKS + c, c % 2
            e.wait_ge(S("ln_var"), 4 * (k + 1))
            step(P.tensor_scalar(ve[:, h, :], mv[:, h, :, 1], EPS, None, ALU.add))
            step.wait()
            P.tensor_tensor(rs[:, h, :], ve[:, h, :], F("mhalf"), ALU.pow).then_inc(S("ln_rs"), 1)

        def xT_tensor(e, n, c, b):
            k = (n - 1) * CHUNKS + c
            e.wait_ge(S("ln_x"), 4 * (k + 1))
            for t, tile in enumerate(chunk_tiles(n, c)):
                mm = T.transpose(ps[:, b, 128 * t:128 * (t + 1)], x[:, tile, :], ident)
            mm.then_inc(S("xT_ps"), 1)

        def xT_scalar(e, n, c, b):
            k = (n - 1) * CHUNKS + c
            e.wait_ge(S("xT_ps"), k + 1 + CHUNKS)
            A.activation(xTs(n, c), bank(b).rearrange("p (s t) -> p s t", s=4), ACT.Copy).then_inc(S("xT"), 1)

        def x0T_tensor(e, c, b):
            e.wait_ge(S(f"ld_x{c // 2}"), 16)
            for t in range(4):
                mm = T.transpose(ps[:, b, 128 * t:128 * (t + 1)], x[:, 4 * c + t, :], ident)
            mm.then_inc(S("xT_ps"), 1)

        def x0T_scalar(e, c, b):
            e.wait_ge(S("xT_ps"), c + 1)
            A.activation(xT[:, 512 * c:512 * c + 512], bank(b), ACT.Copy).then_inc(S("xT"), 1)

        def xT_ready(n, c):
            return (n - 1) * CHUNKS + c + 1

        def split_parts(step, eng, src, parts, res, n, name=None):
            step(eng.tensor_copy(parts[:, 0, 0:n, :], src[:, 0:n, :]))
            step.wait()
            step(eng.tensor_tensor(res[:, 0:n, :], src[:, 0:n, :], parts[:, 0, 0:n, :], ALU.subtract))
            step.wait()
            step(eng.tensor_copy(parts[:, 1, 0:n, :], res[:, 0:n, :]))
            step.wait()
            last = eng.tensor_tensor(parts[:, 2, 0:n, :], res[:, 0:n, :], parts[:, 1, 0:n, :], ALU.subtract)
            if name:
                last.then_inc(S(name), 1)
            else:
                step(last)

        Q_SLOTS = [(0, 0, 3, 1), (1, 3, 2, 1), (2, 5, 1, 1)]
        K_SLOTS = [(0, 0, 2, 3), (0, 5, 1, 1), (1, 1, 2, 3), (2, 2, 1, 1)]

        def fill_slots(step, eng, parts, stack, n, slots):
            step.wait()
            for part, first, count, stride in slots:
                src = parts[:, part, 0:n, :]
                if count == 1:
                    step(eng.tensor_copy(stack[:, 0:n, 8 * first:8 * first + 8], src))
                else:
                    dst = stack[:, 0:n, 0:48].rearrange("p n (s d) -> p n s d", d=8)
                    dst = dst[:, :, first:first + stride * (count - 1) + 1:stride, :]
                    step(eng.tensor_copy(dst, src.unsqueeze(2).to_broadcast([128, n, count, 8])))

        def fill_keys_scalar(e, n, name):
            for part, first, count, stride in K_SLOTS:
                src = kp[:, part, 0:n, :]
                if count == 1:
                    dst = kstack[:, 0:n, 8 * first:8 * first + 8]
                else:
                    dst = kstack[:, 0:n, 0:48].rearrange("p n (s d) -> p n s d", d=8)
                    dst = dst[:, :, first:first + stride * (count - 1) + 1:stride, :]
                    src = src.unsqueeze(2).to_broadcast([128, n, count, 8])
                A.activation(dst, src, ACT.Copy).then_inc(S(name), 1)

        def stack_transposes(stack, heads, name, g, b):
            for pair in range(2):
                for t in range(4):
                    h = t * heads + 4 * g + 2 * pair
                    col = 512 * pair + 128 * t
                    mm = T.transpose(bank_bf(b)[:, col:col + 128],
                                     stack[:, h:h + 2, :].rearrange("p h s -> p (h s)"), identb)
            mm.then_inc(S(f"{name}_ps"), 1)

        def turn_stacks(e, kv, k_name, k_chunk, bk, q_name, q_chunk, bq):
            for g in range(4):
                if g < kv // 4:
                    if g or k_chunk:
                        e.wait_ge(S(f"{k_name}_sb"), kv // 4 * k_chunk + g)
                    stack_transposes(kstack, kv, k_name, g, bk)
                if g or q_chunk:
                    e.wait_ge(S(f"{q_name}_sb"), 4 * q_chunk + g)
                stack_transposes(qstack, H, q_name, g, bq)

        def stack_evac(e, copy, dst, heads, name, i, b, half):
            groups = heads // 4
            for g in range(groups):
                e.wait_ge(S(f"{name}_ps"), groups * i + g + 1)
                copy(dst[:, 2 * g:2 * g + 2, 512 * half:512 * half + 512],
                     bank_bf(b).rearrange("p (a b) -> p a b", a=2)).then_inc(S(f"{name}_sb"), 1)

        def act_copy(o, i):
            return A.activation(o, i, ACT.Copy)

        def narrow_name(n, what):
            return f"l1_{what}" if n == 1 else f"nr_{what}"

        def narrow_chunk(n, c):
            return c + CHUNKS if n == 7 else c

        def finish_tensor(e, n, c, wo, bias, bt, bo):
            e.wait_ge(S(narrow_name(n, "on")), 4 * (narrow_chunk(n, c) + 1))
            for t in range(4):
                mm = T.transpose(ps[:, bt, 128 * t:128 * (t + 1)], on[:, t, :], ident)
            mm.then_inc(S(narrow_name(n, "oT_ps")), 1)
            e.wait_ge(S(narrow_name(n, "oT")), narrow_chunk(n, c) + 1)
            for t in range(4):
                dst = ps[:, bo, 128 * t:128 * (t + 1)]
                mm = T.matmul(dst, oT[:, 128 * t:128 * (t + 1)], wo, start=True, stop=bias is None)
                if bias is not None:
                    mm = T.matmul(dst, ones_row, bias, start=False, stop=True)
            mm.then_inc(S(narrow_name(n, "out")), 1)

        def finish_scalar(e, n, c, bt):
            e.wait_ge(S(narrow_name(n, "oT_ps")), narrow_chunk(n, c) + 1)
            A.activation(oT[:], bank(bt), ACT.Copy).then_inc(S(narrow_name(n, "oT")), 1)

        def normalise_vector(e, step, n, t, o):
            step(V.reciprocal(orec[:, t, :], o[:, :, 8]))
            step.wait()
            V.tensor_tensor(on[:, t, :].rearrange("p (h d) -> p h d", h=H), o[:, :, 0:8],
                            orec[:, t, :].unsqueeze(2).to_broadcast([128, H, 8]), ALU.mult)\
                .then_inc(S(narrow_name(n, "on")), 1)

        def residual_vector(e, step, n, c, b):
            V_y = flat(y[:, c % 2])
            if c >= 2:
                after_chunk(e, n, c - 1)
            if n == 5:
                step(V.tensor_tensor(y[:, c % 2], bank(b).rearrange("p (t d) -> p t d", t=4), xs(n, c), ALU.add))
            else:
                step(V.tensor_tensor(V_y, bank(b), flat(xs(n, c)), ALU.add))

        BATCH = 4
        ROWS = QT * H
        FINISH = ROWS // 2 + 2 * BATCH - 1

        RING1 = 10

        def ring1(i):
            place = i % RING1
            return ring[:, place, :] if place < RING else w2x[:, 1024 * (place - RING):1024 * (place - RING + 1)]

        def row_of(r):
            return r // H, (r % H) // 2, r % 2

        def l1_tensor(e):
            e.wait_ge(S("ld_cf"), 16)
            e.wait_ge(S("ld_w1"), 128)
            for i in range(4):
                mm = T.transpose(ps[:, 7, 128 * i:128 * (i + 1)], w1[:, i, :], ident)
            mm.then_inc(S("wT_ps"), 1)
            for c in range(2):
                x0T_tensor(e, c, 4 + c)

            def project(c):
                e.wait_ge(S("xT"), c + 2 - c % 2)
                e.wait_ge(S("wT"), 1)
                if c >= 1:
                    e.wait_ge(S("l1_qkv_sb"), 3 * c)
                if c % 2 == 0 and c:
                    e.wait_ge(S("l1_clamped"), ROWS * (c // 2))
                for t in range(4):
                    T.matmul(ps[:, t, 0:384], xT[:, 512 * c + 128 * t:512 * c + 128 * (t + 1)],
                             flat(w1T[:, 0:3, :]), start=True, stop=False)
                    mm = T.matmul(ps[:, t, 0:384], ones_row, b1[:, 0:384], start=False, stop=True)
                mm.then_inc(S("l1_qkv"), 1)

            def turn_operands(c):
                e.wait_ge(S("cb_ready"), 1)
                e.wait_ge(S("l1_kstack"), 5 * (c + 1))
                e.wait_ge(S("l1_qstack"), c + 1)
                if c % 2 == 0 and c:
                    e.wait_ge(S("l1_pT_sb"), 2 * ROWS * (c // 2))
                if c == 0:
                    e.wait_ge(S("xT"), 2)
                turn_stacks(e, H, "l1_kT", c, 4, "l1_qT", c, 5)

            def scores(b, r):
                qt, pair, p = row_of(r)
                i = ROWS * b + r
                if r >= 2:
                    e.wait_ge(S("l1_clamped"), i - 1)
                rows = slice(64 * p, 64 * p + 64)
                for half in range(2):
                    mm = T.matmul(bank(2 * p + half), qT[rows, pair, 128 * qt:128 * qt + 128],
                                  kT[rows, pair, 512 * half:512 * half + 512], start=True, stop=True)
                mm.then_inc(S("l1_d2"), 1)

            def turn(b, r):
                i = ROWS * b + r
                e.wait_ge(S("l1_prob"), i + 1)
                for half in range(2):
                    if i:
                        e.wait_ge(S("l1_pT_sb"), 2 * i - 1 + half)
                    for k in range(4):
                        kt = 4 * half + k
                        mm = T.transpose(ps[:, 4 + half, 128 * k:128 * k + 128],
                                         ring1(i)[:, 128 * kt:128 * kt + 128], ident)
                    mm.then_inc(S("l1_pT_ps"), 1)

            def values(b, r):
                qt, pair, p = row_of(r)
                i = ROWS * b + r
                e.wait_ge(S("l1_pT_sb"), 2 * (i + 1))
                if r % H == 0 and i:
                    e.wait_ge(S("ob"), i // H)
                h = 2 * pair + p
                dst = ps[32 * (h % 4):32 * (h % 4) + HD + 1, 6, 128 * (h // 4):128 * (h // 4) + 128]
                for kt in range(QT):
                    mm = T.matmul(dst, heads_v[:, b % 2, kt, h, :], pTr[:, i % 2, kt, :], start=kt == 0, stop=kt == QT - 1)
                mm.then_inc(S("l1_pv"), 1)

            def turn_outputs(tile):
                e.wait_ge(S("ob"), tile + 1)
                if tile:
                    e.wait_ge(S("l1_on"), tile)
                if tile % 4 == 0 and tile:
                    e.wait_ge(S("l1_y"), tile // 4)
                for g in range(4):
                    mm = T.transpose(ps[:, 7, 128 * g:128 * g + 128], obuf[:, 0, 128 * g:128 * g + 128], ident)
                mm.then_inc(S("ob_turned"), 1)

            for b in range(SEQS):
                if b == 0:
                    project(0)
                turn_operands(2 * b)
                project(2 * b + 1)
                turn_operands(2 * b + 1)
                e.wait_ge(S("l1_kT_sb"), 8 * (b + 1))
                e.wait_ge(S("l1_qT_sb"), 8 * (b + 1))
                e.wait_ge(S("l1_qkv_sb"), 6 * (b + 1))
                for r in range(RING1):
                    scores(b, r)
                for r in range(ROWS + 1):
                    if r > H and r % H == 1:
                        turn_outputs(QT * b + r // H - 1)
                    if r < ROWS:
                        turn(b, r)
                    if r:
                        values(b, r - 1)
                    if r + RING1 < ROWS:
                        scores(b, r + RING1)
                    if r == FINISH:
                        finish_tensor(e, 1, 2 * b, w1T[:, 3, :], b1[:, 384:512], 7, 7)
                    if r == ROWS - BATCH and b < SEQS - 1:
                        e.wait_ge(S("l1_clamped"), ROWS * (b + 1))
                        for c in range(2 * b + 2, 2 * b + 4):
                            x0T_tensor(e, c, c % 2)
                if b < SEQS - 1:
                    project(2 * b + 2)
                turn_outputs(QT * b + QT - 1)
                finish_tensor(e, 1, 2 * b + 1, w1T[:, 3, :], b1[:, 384:512], 7, 7)
            e.wait_ge(S("l1_pT_sb"), 2 * ROWS * SEQS)
            for c in range(CHUNKS):
                e.wait_ge(S("xT"), CHUNKS + c)
                xT_tensor(e, 1, c, 4)

        def l1_scalar(e):
            e.wait_ge(S("wT_ps"), 1)
            A.activation(flat(w1T[:]), bank(7), ACT.Copy).then_inc(S("wT"), 1)
            for c in range(2):
                x0T_scalar(e, c, 4 + c)
            view = "p (t h) d -> p t (h d)"

            def take_projections(c):
                e.wait_ge(S("l1_qkv"), c + 1)
                if c:
                    e.wait_ge(S("l1_kparts"), c)
                    e.wait_ge(S("l1_qstack"), c)
                qkv = ps[:, 0:4, :]
                A.activation(kf[:].rearrange(view, t=4), qkv[:, :, 128:256], ACT.Copy).then_inc(S("l1_qkv_sb"), 1)
                A.activation(qf[:].rearrange(view, t=4), qkv[:, :, 0:128], ACT.Copy, scale=-2.0)\
                    .then_inc(S("l1_qkv_sb"), 1)
                A.activation(values[:, c // 2 % 2, 4 * (c % 2):4 * (c % 2) + 4, :, 0:8],
                             qkv[:, :, 256:384].rearrange("p t (h d) -> p t h d", d=8),
                             ACT.Copy).then_inc(S("l1_qkv_sb"), 1)

            def take_keys(c):
                e.wait_ge(S("l1_kparts"), c + 1)
                if c:
                    e.wait_ge(S("l1_kT_ps"), 4 * c)
                fill_keys_scalar(e, 64, "l1_kstack")
                stack_evac(e, act_copy, kT, H, "l1_kT", c, 4, c % 2)

            take_projections(0)
            for b in range(SEQS):
                take_keys(2 * b)
                take_projections(2 * b + 1)
                take_keys(2 * b + 1)
                for g in range(ROWS // BATCH):
                    i0 = ROWS * b + BATCH * g
                    for i in range(i0, i0 + BATCH):
                        e.wait_ge(S("l1_clamped"), i + 1)
                        A.activation(ring1(i), ring1(i), ACT.Sqrt).then_inc(S("l1_dist"), 1)
                    mins = m2[:, i0 % 16:i0 % 16 + BATCH]
                    A.activation(mins, mins, ACT.Sqrt).then_inc(S("l1_dist"), 1)
                    for i in range(i0, i0 + BATCH):
                        if i == i0:
                            e.wait_ge(S("l1_dist"), (BATCH + 1) * (i0 // BATCH + 1))
                        A.activation(ring1(i), ring1(i), ACT.Exp,
                                     bias=m2[:, i % 16:i % 16 + 1], scale=-1.0).then_inc(S("l1_prob"), 1)
                    if (g + 1) * BATCH == FINISH + 1:
                        finish_scalar(e, 1, 2 * b, 7)
                if b < SEQS - 1:
                    for c in range(2 * b + 2, 2 * b + 4):
                        x0T_scalar(e, c, c % 2)
                    take_projections(2 * b + 2)
                finish_scalar(e, 1, 2 * b + 1, 7)
            for c in range(CHUNKS):
                xT_scalar(e, 1, c, 4)

        def l1_gpsimd(e, step):
            step(P.memset(rt[:], 0.0))
            step(P.memset(kdb[:], 0.0))
            for b in range(2):
                step(P.memset(values[:, b, :, :, 8:9], 1.0))
                step(P.memset(values_g[:, b, :, :, 8:9], 1.0))
            step.wait()
            P.memset(vdb[:], 0.0).then_inc(S("const_zero"), 1)
            step(P.memset(kstack[:, :, 54:64], 0.0))
            step(P.memset(kstack[:, :, 48:51], 1.0))
            step(P.memset(qstack[:, :, 51:54], 1.0))
            step.wait()
            P.memset(qstack[:, :, 54:64], 0.0).then_inc(S("l1_consts"), 1)
            for c in range(CHUNKS):
                e.wait_ge(S("l1_norm2"), c + 1)
                if c:
                    e.wait_ge(S("l1_kT_ps"), 4 * c)
                step.wait()
                P.tensor_copy(kstack[:, :, 51:54], norm2p[:, 1, :, :].rearrange("p r n -> p n r"))\
                    .then_inc(S("l1_kstack"), 1)
                if c % 2 and c > 1:
                    ln_gpsimd(e, step, 1, c - 3)
                    ln_gpsimd(e, step, 1, c - 2)
            ln_gpsimd(e, step, 1, CHUNKS - 2)
            ln_gpsimd(e, step, 1, CHUNKS - 1)

        def l1_vector(e, step):
            def prep(c):
                e.wait_ge(S("l1_qkv_sb"), 3 * c + 2)
                if c:
                    e.wait_ge(S("l1_qT_ps"), 4 * c)
                    e.wait_ge(S("l1_kstack"), 5 * c)
                sq = heads[:, 2:4]
                step.wait()
                for i, (src, sc) in enumerate(((qf, 0.25), (kf, 1.0))):
                    step(V.scalar_tensor_tensor(sq[:, i], src[:], sc, src[:], ALU.mult, ALU.mult))
                step.wait()
                step(V.tensor_reduce(norm2[:], sq, AX.X, ALU.add))
                step.wait()
                split_parts(step, V, kf, kp, kr, 64, "l1_kparts")
                step(V.tensor_copy(norm2p[:, :, 0, :], norm2[:]))
                step.wait()
                step(V.tensor_tensor(norm2r[:], norm2[:], norm2p[:, :, 0, :], ALU.subtract))
                step.wait()
                step(V.tensor_copy(norm2p[:, :, 1, :], norm2r[:]))
                step.wait()
                V.tensor_tensor(norm2p[:, :, 2, :], norm2r[:], norm2p[:, :, 1, :], ALU.subtract)\
                    .then_inc(S("l1_norm2"), 1)
                split_parts(step, V, qf, qp, qr, 64)
                fill_slots(step, V, qp, qstack, 64, Q_SLOTS)
                step.wait()
                e.wait_ge(S("l1_norm2"), c + 1)
                e.wait_ge(S("l1_consts"), 1)
                V.tensor_copy(qstack[:, :, 48:51], norm2p[:, 0, :, :].rearrange("p r n -> p n r"))\
                    .then_inc(S("l1_qstack"), 1)
                stack_evac(e, V.tensor_copy, qT, H, "l1_qT", c, 5, c % 2)

            def clamp(i):
                p = i % 2
                e.wait_ge(S("l1_d2"), i + 1)
                if i >= RING1:
                    e.wait_ge(S("l1_pT_ps"), 2 * (i - RING1 + 1))
                V.tensor_scalar(ring1(i), ps[:, 2 * p:2 * p + 2, :].rearrange("p a b -> p (a b)"),
                                1e-12, None, ALU.max, ALU.min, accum_out=m2[:, i % 16:i % 16 + 1])\
                    .then_inc(S("l1_clamped"), 1)

            def evac(i):
                for half in range(2):
                    e.wait_ge(S("l1_pT_ps"), 2 * i + half + 1)
                    if i >= 2:
                        e.wait_ge(S("l1_pv"), i - 1)
                    V.tensor_copy(pTr[:, i % 2, 4 * half:4 * half + 4, :].rearrange("p k q -> p (k q)"),
                                  bank(4 + half)).then_inc(S("l1_pT_sb"), 1)

            def take_outputs(t):
                e.wait_ge(S("l1_pv"), H * (t + 1))
                if t:
                    e.wait_ge(S("ob_turned"), t)
                V.tensor_copy(obuf[:, 0, :], bank(6)).then_inc(S("ob"), 1)

            def tile_done(t):
                e.wait_ge(S("ob_turned"), t + 1)
                if t % 4 == 0 and t:
                    e.wait_ge(S("l1_oT_ps"), t // 4)
                normalise_vector(e, step, 1, t % 4, bank(7).rearrange("p (h d) -> p h d", h=H))

            def chunk_done(c):
                e.wait_ge(S("l1_out"), c + 1)
                if c >= 2:
                    after_chunk(e, 1, c - 1)
                V.tensor_tensor(flat(y[:, c % 2]), bank(7), flat(xs(1, c)), ALU.add).then_inc(S("l1_y"), 1)
                e.wait_ge(S("l1_y"), c + 1)

            e.wait_ge(S("ld_cb"), 16)
            V.tensor_copy(cb[:], cb32).then_inc(S("cb_ready"), 1)
            step(V.memset(bank(6), 0.0))
            for b in range(SEQS):
                prep(2 * b)
                prep(2 * b + 1)
                base = ROWS * b
                for r in range(RING1):
                    clamp(base + r)
                for r in range(ROWS):
                    evac(base + r)
                    if r and r % H == 0:
                        take_outputs(QT * b + r // H - 1)
                    if r > H and r % H == 1:
                        tile_done(QT * b + r // H - 1)
                    if r + RING1 < ROWS:
                        clamp(base + r + RING1)
                    if b and r in (H + 4, H + 10):
                        ln_vector(e, step, 1, 2 * b - 2 + (r > H + 4))
                    if r == FINISH + 1:
                        chunk_done(2 * b)
                take_outputs(QT * b + QT - 1)
                tile_done(QT * b + QT - 1)
                chunk_done(2 * b + 1)
            for c in (CHUNKS - 2, CHUNKS - 1):
                ln_vector(e, step, 1, c)

        def after_chunk(e, n, c):
            e.wait_ge(S("ln_x"), 4 * ((n - 1) * CHUNKS + c))

        def after_turn(e, n, c):
            e.wait_ge(S("xT"), CHUNKS + (n - 1) * CHUNKS + c)

        def rms_vector(e, step, src, dst, name, c, factor=1.0, scaled=None):
            step.wait()
            for t in range(4):
                V.scalar_tensor_tensor(junk[:, t, :], src[:, t, :], 1.0, src[:, t, :], ALU.mult, ALU.mult,
                                       accum_out=ssq[:, t:t + 1]).then_inc(S(f"{name}_ss"), 1)
            e.wait_ge(S(f"{name}_r"), c + 1)
            for t in range(4):
                V.tensor_scalar(dst[:, t, :], src[:, t, :], crec[:, t:t + 1], factor, ALU.mult, ALU.mult)\
                    .then_inc(S(scaled or f"{name}_x"), 1)

        def rms_gpsimd(e, step, name, c, scale=1.0 / D, op=ALU.add, floor=EPS):
            e.wait_ge(S(f"{name}_ss"), 4 * (c + 1))
            step(P.tensor_scalar(csum[:], ssq[:], scale, floor, ALU.mult, op))
            step.wait()
            P.tensor_tensor(crec[:], csum[:], F("mhalf"), ALU.pow).then_inc(S(f"{name}_r"), 1)

        def turn_tensor(e, src, name, c, b):
            e.wait_ge(S(f"{name}_x"), 4 * (c + 1))
            for t in range(4):
                mm = T.transpose(ps[:, b, 128 * t:128 * (t + 1)], src[:, t, :], ident)
            mm.then_inc(S(f"{name}_T_ps"), 1)

        def rank_vector(step, src, n, E, k):
            g4 = gt[:, 0:n * E * E].rearrange("p (n e j) -> p n e j", n=n, e=E)
            q4 = eq[:, 1024 - n * E * E:1024].rearrange("p (n e j) -> p n e j", n=n, e=E)
            by_j = src.unsqueeze(2).to_broadcast([128, n, E, E])
            by_e = src.unsqueeze(3).to_broadcast([128, n, E, E])
            step.wait()
            step(V.tensor_tensor(g4, by_j, by_e, ALU.is_gt))
            step(V.tensor_tensor(q4, by_j, by_e, ALU.is_equal))
            step.wait()
            q3 = eq[:, 1024 - n * E * E:1024].rearrange("p (n f) -> p n f", n=n)
            step(V.tensor_tensor(q3, q3, F(f"lt{E}").unsqueeze(1).to_broadcast([128, n, E * E]), ALU.mult))
            step.wait()
            step(V.tensor_tensor(g4, g4, q4, ALU.add))
            step.wait()
            step(V.tensor_reduce(rk[:, 0:n * E].rearrange("p (n e) -> p n e", n=n), g4, AX.X, ALU.add))
            step.wait()
            step(V.tensor_scalar(msk[:, 0:n * E], rk[:, 0:n * E], float(k), None, ALU.is_lt))
            step.wait()

        def weights_vector(e, step, E, scale, tiny):
            c3 = cw[:, :, 0:E]
            part = cpart[:, :, 0:3 * E].rearrange("p t (a e) -> p t a e", a=3)
            step(V.tensor_reduce(csum[:], c3, AX.X, ALU.add))
            step.wait()
            if tiny:
                step(V.tensor_scalar(csum[:], csum[:], tiny, None, ALU.add))
                step.wait()
            step(V.reciprocal(crec[:], csum[:]))
            step.wait()
            step(V.tensor_tensor(c3, c3, crec[:].unsqueeze(2).to_broadcast([128, 4, E]), ALU.mult))
            step.wait()
            if scale != 1.0:
                step(V.tensor_scalar(c3, c3, scale, None, ALU.mult))
                step.wait()
            step(V.tensor_copy(part[:, :, 0, :], c3))
            step.wait()
            step(V.tensor_tensor(cwr[:, :, 0:E], c3, part[:, :, 0, :], ALU.subtract))
            step.wait()
            step(V.tensor_copy(part[:, :, 1, :], cwr[:, :, 0:E]))
            step.wait()
            V.tensor_tensor(part[:, :, 2, :], cwr[:, :, 0:E], part[:, :, 1, :], ALU.subtract)\
                .then_inc(S("ex_cpart"), 1)

        class Experts:
            def __init__(self, n, units, E, sel, weight_of, gate, up, down):
                self.n, self.units, self.E, self.sel, self.weight_of = n, units, E, sel, weight_of
                self.gate, self.up, self.down = gate, up, down
                self.chunk0, self.unit0, self.new0 = (CHUNKS, 16 * CHUNKS, 8 * CHUNKS) if n == 4 else (0, 0, 0)
                self.new = [u for u in range(units)
                            if weight_of(u) is not None and (u == 0 or weight_of(u - 1) != weight_of(u))]

            def last_unit(self, w):
                return max(u for u in range(self.units) if self.weight_of(u) == w)

        def experts_tensor(e, x_, c, xin, between=None):
            base, wbase, E3 = x_.unit0 + x_.units * c, x_.new0 + len(x_.new) * c, 3 * x_.E
            e.wait_ge(S("ex_cpart"), x_.chunk0 + c + 1)
            for t in range(4):
                tr = T.transpose(bank_bf(4)[0:E3, 128 * t:128 * (t + 1)], cpart[:, t, 0:E3], identb)
            tr.then_inc(S("ex_cT_ps"), 1)
            e.wait_ge(S("ex_cT"), x_.chunk0 + c + 1)

            def down(u):
                e.wait_ge(S("ex_a"), base + u + 1)
                for t in range(4):
                    mm = T.matmul(ps[:, 6, 128 * t:128 * (t + 1)], act[:, u % 3, 128 * t:128 * (t + 1)],
                                  x_.down(u), start=u == 0 and t == 0, stop=u == x_.units - 1,
                                  skip_group_check=True)
                mm.then_inc(S("ex_down"), 1)

            for u in range(x_.units):
                if between:
                    between(u)
                w = x_.weight_of(u)
                if u in x_.new:
                    if w >= 2:
                        e.wait_ge(S("ex_cb"), wbase + w - 1)
                    T.matmul(bank(4 + w % 2), B(x_.sel, E3)[:, 128 * w:128 * (w + 1)],
                             cT[0:E3, :], start=True, stop=True).then_inc(S("ex_cb_ps"), 1)
                if u >= 2:
                    e.wait_ge(S("ex_sil"), base + u - 1)
                T.matmul(bank(u % 2), x_.gate(u), xin, start=True, stop=True).then_inc(S("ex_g"), 1)
                if u >= 2:
                    e.wait_ge(S("ex_a"), base + u - 1)
                T.matmul(bank(2 + u % 2), x_.up(u), xin, start=True, stop=True).then_inc(S("ex_u"), 1)
                if u >= 2:
                    down(u - 2)
            down(x_.units - 2)
            down(x_.units - 1)

        def experts_scalar(e, x_, c, between=None):
            base, wbase, E3 = x_.unit0 + x_.units * c, x_.new0 + len(x_.new) * c, 3 * x_.E
            e.wait_ge(S("ex_cT_ps"), x_.chunk0 + c + 1)
            A.activation(cT[0:E3, :], bank_bf(4)[0:E3, 0:512], ACT.Copy).then_inc(S("ex_cT"), 1)
            for u in range(x_.units):
                if between:
                    between(u)
                w = x_.weight_of(u)
                if u in x_.new:
                    e.wait_ge(S("ex_cb_ps"), wbase + w + 1)
                    if w >= 2:
                        e.wait_ge(S("ex_t1"), base + x_.last_unit(w - 2) + 1)
                    A.activation(cbs[:, w % 2, :], bank(4 + w % 2), ACT.Copy).then_inc(S("ex_cb"), 1)
                e.wait_ge(S("ex_g"), base + u + 1)
                if u >= 3:
                    e.wait_ge(S("ex_t1"), base + u - 2)
                A.activation(sil[:, u % 3, :], bank(u % 2), ACT.Silu).then_inc(S("ex_sil"), 1)

        def experts_gpsimd(e, x_, c, between=None):
            base, wbase = x_.unit0 + x_.units * c, x_.new0 + len(x_.new) * c
            for u in range(x_.units):
                if between:
                    between(u)
                w = x_.weight_of(u)
                e.wait_ge(S("ex_sil"), base + u + 1)
                if u >= 3:
                    e.wait_ge(S("ex_a"), base + u - 2)
                if w is not None:
                    e.wait_ge(S("ex_cb"), wbase + w + 1)
                    P.tensor_tensor(t1[:, u % 3, :], sil[:, u % 3, :], cbs[:, w % 2, :], ALU.mult)\
                        .then_inc(S("ex_t1"), 1)
                else:
                    P.tensor_copy(t1[:, u % 3, :], sil[:, u % 3, :]).then_inc(S("ex_t1"), 1)

        def experts_vector(e, x_, c, between=None):
            base = x_.unit0 + x_.units * c
            for u in range(x_.units):
                if between:
                    between(u)
                e.wait_ge(S("ex_u"), base + u + 1)
                e.wait_ge(S("ex_t1"), base + u + 1)
                if u >= 3:
                    e.wait_ge(S("ex_down"), base + u - 2)
                V.tensor_tensor(act[:, u % 3, :], bank(2 + u % 2), t1[:, u % 3, :], ALU.mult)\
                    .then_inc(S("ex_a"), 1)

        class Narrow:
            def __init__(self, n, kv, values, head):
                self.n = n
                self.kv = kv
                self.values = values
                self.head = head
                self.units = 4 * PAIRS if n == 2 else H

            def groups(self, half):
                if self.n == 7:
                    return [None]
                g = [[(2 * i, 0, 0, 512), (2 * i + 1, 1, 0, 512)] for i in range(2 * half)]
                return g + [[(4 * half + i, 0, 128 * i, 512 - 128 * i)] for i in range(4)]

            def unit_base(self, c):
                return self.units * c + (4 * PAIRS * CHUNKS if self.n == 7 else 0)

            def group_base(self, c):
                before = l2n.group_base(CHUNKS) if self.n == 7 else 0
                return before + H * sum(len(self.groups(d % 2)) for d in range(c))

            def four_base(self, c):
                return TILES + 4 * narrow_chunk(self.n, c)

            def key_turn(self, c):
                return c + 2 if self.n == 7 else c

        l2n = Narrow(2, 4, values_g, lambda j, p: (8 * (j // 4) + 4 * p + j % 4, j // 4, 2 * (j // 4) + p))
        l7n = Narrow(7, H, values, lambda j, p: (2 * j + p, j, 2 * j + p))

        def parity_rows(p):
            return slice(64 * p, 64 * p + 64)

        def narrow_first_tensor(e, a_, c):
            n, half = a_.n, c % 2
            base = a_.unit_base(c)
            for u in range(a_.units):
                if u >= 2:
                    e.wait_ge(S("nr_max"), base + u - 1)
                if n == 2:
                    t, j = u // PAIRS, u % PAIRS
                    q0 = 512 * half + 128 * t
                    width = q0 + 128
                    for p in range(2):
                        rows, b0 = parity_rows(p), 4 * (u % 2) + 2 * p
                        kj = a_.head(j, p)[1]
                        db, dcol = b0 + q0 // 512, q0 % 512
                        if q0 >= 512:
                            T.matmul(bank(b0), qT[rows, j, q0:q0 + 128], kT[rows, kj, 0:512], start=True, stop=True)
                        T.matmul(ps[:, db, dcol:dcol + 128], identb, B("causal"), start=True, stop=False,
                                 skip_group_check=True)
                        mm = T.matmul(ps[:, db, 0:dcol + 128], qT[rows, j, q0:q0 + 128],
                                      kT[rows, kj, width - dcol - 128:width], start=False, stop=True,
                                      skip_group_check=True)
                else:
                    j, p = u // 2, u % 2
                    rows = parity_rows(p)
                    for t in range(4):
                        b, at, q0 = 2 * (u % 4) + t // 2, 192 * (t % 2), 512 * half + 128 * t
                        first = q0 == 0
                        T.matmul(ps[:, b, at:at + 128], identb, B("winc"), start=t % 2 == 0, stop=False,
                                 skip_group_check=True)
                        T.matmul(ps[:, b, at + 128:at + 192], identb, B("winc")[:, 64:128] if first else B("behind"),
                                 start=False, stop=False, skip_group_check=True)
                        T.matmul(ps[:, b, at:at + 128], qT[rows, j, q0:q0 + 128], kT[rows, j, q0:q0 + 128],
                                 start=False, stop=True, skip_group_check=True)
                        k0 = q0 + 64 if first else q0 - 64
                        mm = T.matmul(ps[:, b, at + 128:at + 192], qT[rows, j, q0:q0 + 128], kT[rows, j, k0:k0 + 64],
                                      start=False, stop=True, skip_group_check=True)
                mm.then_inc(S("nr_s"), 1)

        def narrow_first_vector(e, step, a_, c):
            n, half, base = a_.n, c % 2, a_.unit_base(c)
            nm4 = nm[:].rearrange("p (t h) -> p t h", t=4)
            for u in range(a_.units):
                e.wait_ge(S("nr_s"), base + u + 1)
                if n == 2:
                    t, j = u // PAIRS, u % PAIRS
                    width = 512 * half + 128 * t + 128
                    s = ps[:, 4 * (u % 2):4 * (u % 2) + 4, :].rearrange("p (a b) k -> p a (b k)", a=2)[:, :, 0:width]
                    V.tensor_reduce(nm4[:, t, 2 * j:2 * j + 2], s, AX.X, ALU.max, negate=True)\
                        .then_inc(S("nr_max"), 1)
                else:
                    b = 2 * (u % 4)
                    s = ps[:, b:b + 2, 0:384].rearrange("p b (t k) -> p b t k", t=2)
                    V.tensor_reduce(nm4[:, :, u].rearrange("p (b t) -> p b t", b=2), s, AX.X, ALU.max, negate=True)\
                        .then_inc(S("nr_max"), 1)
            e.wait_ge(S("nr_max"), base + a_.units)
            step(V.tensor_copy(qstack[:, :, 48], nm[:]))
            step.wait()
            step(V.tensor_tensor(nmr[:], nm[:], qstack[:, :, 48], ALU.subtract))
            step.wait()
            step(V.tensor_copy(qstack[:, :, 49], nmr[:]))
            step.wait()
            V.tensor_tensor(qstack[:, :, 50], nmr[:], qstack[:, :, 49], ALU.subtract)\
                .then_inc(S("nr_mstack"), 1)

        def narrow_second_tensor(e, a_, c):
            n, half = a_.n, c % 2
            base = a_.group_base(c)
            work = [(h, g) for h in range(H) for g in a_.groups(half)]
            per_head = len(a_.groups(half))

            def scores(i):
                (u, g), b0 = work[i], 2 * (i % 2)
                j, p = u // 2, u % 2
                rows, kj = parity_rows(p), a_.head(j, p)[1]
                if i >= 2:
                    e.wait_ge(S("nr_prob"), base + i - 1)
                if g is None:
                    for t in range(4):
                        b, at, q0 = b0 + t // 2, 192 * (t % 2), 512 * half + 128 * t
                        T.matmul(ps[:, b, at:at + 128], identb, B("wincT"), start=t % 2 == 0, stop=False,
                                 skip_group_check=True)
                        T.matmul(ps[:, b, at + 128:at + 192], identb, B("behindT"), start=False, stop=q0 == 0,
                                 skip_group_check=True)
                        mm = T.matmul(ps[:, b, at:at + 128], kT[rows, j, q0:q0 + 128], qT[rows, j, q0:q0 + 128],
                                      start=False, stop=True, skip_group_check=True)
                        if q0:
                            mm = T.matmul(ps[:, b, at + 128:at + 192], kT[rows, j, q0 - 128:q0],
                                          qT[rows, j, q0:q0 + 64], start=False, stop=True, skip_group_check=True)
                else:
                    for kt, k, q0, width in g:
                        q = 512 * half + q0
                        diag = kt >= 4 * half
                        if diag:
                            T.matmul(ps[:, b0 + k, 0:128], identb, B("causalT"), start=True, stop=False,
                                     skip_group_check=True)
                        mm = T.matmul(ps[:, b0 + k, 0:width], kT[rows, kj, 128 * kt:128 * kt + 128],
                                      qT[rows, j, q:q + width], start=not diag, stop=True, skip_group_check=True)
                mm.then_inc(S("nr_sT"), 1)

            def values(i):
                (u, g), slot = work[i], i % 3
                _, _, vh = a_.head(u // 2, u % 2)
                e.wait_ge(S("nr_prob"), base + i + 1)
                if i % (4 * per_head) == 0 and u >= 8:
                    e.wait_ge(S("ob"), a_.four_base(c) + u // 4 - 1)
                first, b = 32 * (u % 4), 6 + u // 4 % 2

                def region(lo, n):
                    return ps[first:first + HD + 1, b, lo:lo + n]

                if g is None:
                    for t in range(4):
                        at, q0, tile = 192 * (t % 2), 512 * half + 128 * t, 4 * half + t
                        pt = pT2[:, slot, t // 2, :]
                        mm = T.matmul(region(128 * t, 128), a_.values[:, c // 2 % 2, tile, vh, :], pt[:, at:at + 128],
                                      start=True, stop=not q0, skip_group_check=True)
                        if q0:
                            mm = T.matmul(region(128 * t, 64), a_.values[:, c // 2 % 2, tile - 1, vh, :],
                                          pt[:, at + 128:at + 192], start=False, stop=True, skip_group_check=True)
                else:
                    for kt, k, q0, width in g:
                        mm = T.matmul(region(q0, width), a_.values[:, c // 2 % 2, kt, vh, :], pT2[:, slot, k, 0:width],
                                      start=kt == 0, stop=kt == 4 * half + 3, skip_group_check=True)
                mm.then_inc(S("nr_pv"), 1)

            def turn_outputs(four):
                e.wait_ge(S("ob"), a_.four_base(c) + four + 1)
                if four:
                    e.wait_ge(S("nr_on"), a_.four_base(c) - 32 + four)
                for t in range(4):
                    mm = T.transpose(ps[:, 4, 128 * t:128 * t + 128], obuf[:, four % 2, 128 * t:128 * t + 128], ident)
                mm.then_inc(S("ob_turned"), 1)

            ends = {4 * per_head * (f + 1) + 3: f for f in range(3)}
            for i in range(len(work) + 2):
                if i < len(work):
                    scores(i)
                if i >= 2:
                    values(i - 2)
                if i in ends:
                    turn_outputs(ends[i])
            turn_outputs(3)

        def narrow_fill_scalar(e, a_, c):
            e.wait_ge(S("nr_kparts"), narrow_chunk(a_.n, c) + 1)
            fill_keys_scalar(e, 4 * a_.kv, "nr_kstack")

        def narrow_second_scalar(e, a_, c):
            n, half = a_.n, c % 2
            base = a_.group_base(c)
            work = [g for h in range(H) for g in a_.groups(half)]
            for i, g in enumerate(work):
                if i == len(work) // 2 and c + 1 < CHUNKS:
                    narrow_fill_scalar(e, a_, c + 1)
                e.wait_ge(S("nr_sT"), base + i + 1)
                if i >= 3:
                    e.wait_ge(S("nr_pv"), base + i - 2)
                banks = 2 if g is None or len(g) == 2 else 1
                width = 384 if g is None else g[0][3]
                b0 = 2 * (i % 2)
                A.activation(pT2[:, i % 3, 0:banks, 0:width], ps[:, b0:b0 + banks, 0:width],
                             ACT.Exp, scale=float(HD) ** -0.5).then_inc(S("nr_prob"), 1)

        def narrow_rope_vector(step, src, dst, heads_, tmp, half):
            n = 4 * heads_
            s3 = src[:, 0:n, :].rearrange("p (t h) d -> p t h d", t=4)
            d3 = dst[:, 0:n, :].rearrange("p (t h) d -> p t h d", t=4)
            t3 = tmp[:, 0:n, :].rearrange("p (t h) d -> p t h d", t=4)

            def table(name):
                tab = F(name).rearrange("p (t d) -> p t d", t=8)[:, 4 * half:4 * half + 4, :]
                return tab.unsqueeze(2).to_broadcast([128, 4, heads_, 8])

            cos, sin = table("cos"), table("sin")
            step(V.tensor_tensor(d3, s3, cos, ALU.mult))
            step(V.tensor_tensor(t3[:, :, :, 0:4], s3[:, :, :, 4:8], sin[:, :, :, 0:4], ALU.mult))
            step(V.tensor_tensor(t3[:, :, :, 4:8], s3[:, :, :, 0:4], sin[:, :, :, 4:8], ALU.mult))
            step.wait()
            step(V.tensor_tensor(dst[:, 0:n, :], dst[:, 0:n, :], tmp[:, 0:n, :], ALU.add))

        def narrow_stacks_vector(e, step, a_, c):
            n, half = a_.n, c % 2
            nk = 4 * a_.kv
            step.wait()
            e.wait_ge(S("nr_qk_sb"), 3 * (narrow_chunk(n, c) + 1))
            narrow_rope_vector(step, kf, kr, a_.kv, rot[:, 1], half)
            step.wait()
            split_parts(step, V, kr, kp, kf, nk, "nr_kparts")
            narrow_rope_vector(step, qf, qr, H, rot[:, 0], half)
            step.wait()
            split_parts(step, V, qr, qp, qf, 64)
            fill_slots(step, V, qp, qstack, 64, Q_SLOTS)
            step.wait()
            V.memset(qstack[:, :, 48:51], 0.0).then_inc(S("nr_qstack"), 1)

        def narrow_consts_gpsimd(e, step, a_):
            nk = 4 * a_.kv
            step(P.memset(kstack[:, 0:nk, 48:51], 1.0))
            step(P.memset(kstack[:, 0:nk, 51:64], 0.0))
            step(P.memset(qstack[:, :, 51:64], 0.0))
            step.wait()
            P.memset(kstack[:, 0:nk, 48:51], 1.0).then_inc(S("nr_consts"), 1)

        def narrow_first_half_tensor(e, a_, c):
            n, k = a_.n, narrow_chunk(a_.n, c)
            if c == 0:
                e.wait_ge(S("nr_consts"), 2 if n == 7 else 1)
            if c >= 2:
                e.wait_ge(S("xT"), n * CHUNKS + c - 1)
            e.wait_ge(S("nr_kstack"), 4 * (k + 1))
            e.wait_ge(S("nr_qstack"), k + 1)
            turn_stacks(e, a_.kv, "nr_kT", a_.key_turn(c), 5, "nr_qT", k, 7)
            e.wait_ge(S("nr_kT_sb"), a_.kv // 4 * (a_.key_turn(c) + 1))
            e.wait_ge(S("nr_qT_sb"), 4 * (k + 1))
            narrow_first_tensor(e, a_, c)
            e.wait_ge(S("nr_mstack"), k + 1)
            for g in range(4):
                if g >= 2:
                    e.wait_ge(S("nr_mT_act" if g % 2 else "nr_mT_dve"), 2 * k + 1)
                stack_transposes(qstack, H, "nr_mT", g, 5 if g % 2 else 7)

        def narrow_second_half_tensor(e, a_, c):
            k = narrow_chunk(a_.n, c)
            e.wait_ge(S("nr_mT_dve"), 2 * (k + 1))
            e.wait_ge(S("nr_mT_act"), 2 * (k + 1))
            if c + 1 < CHUNKS:
                e.wait_ge(S("nr_qk_sb"), 3 * (k + 2))
            narrow_second_tensor(e, a_, c)

        def turned_again(e, copy, done, k, first, b, half):
            for g in (first, first + 2):
                e.wait_ge(S("nr_mT_ps"), 4 * k + g + 1)
                copy(qT[:, 2 * g:2 * g + 2, 512 * half:512 * half + 512],
                     bank_bf(b).rearrange("p (a b) -> p a b", a=2)).then_inc(S(done), 1)

        def narrow_first_half_vector(e, step, a_, c):
            k, half = narrow_chunk(a_.n, c), c % 2
            stack_evac(e, V.tensor_copy, qT, H, "nr_qT", k, 7, half)
            narrow_first_vector(e, step, a_, c)
            turned_again(e, V.tensor_copy, "nr_mT_dve", k, 0, 7, half)

        def narrow_second_half_vector(e, step, a_, c):
            n, half = a_.n, c % 2
            per_head = len(a_.groups(half))
            for four in range(4):
                done = a_.four_base(c) + four
                e.wait_ge(S("nr_pv"), a_.group_base(c) + 4 * per_head * (four + 1))
                if four >= 2:
                    e.wait_ge(S("ob_turned"), done - 1)
                V.tensor_copy(obuf[:, four % 2, :], bank(6 + four % 2)).then_inc(S("ob"), 1)
                e.wait_ge(S("ob_turned"), done + 1)
                o = bank(4).rearrange("p (t h d) -> p t h d", t=4, h=4)
                rec = orec[:, :, 4 * four:4 * four + 4]
                step(V.reciprocal(rec, o[:, :, :, 8]))
                step.wait()
                for p in range(2):
                    first = a_.head(2 * four, p)[0]
                    stride = a_.head(2 * four + 1, p)[0] - first
                    dst = on[:].rearrange("p t (h d) -> p t h d", h=H)[:, :, first:first + stride + 1:stride, :]
                    ins = V.tensor_tensor(dst, o[:, :, p::2, 0:8],
                                          rec[:, :, p::2].unsqueeze(3).to_broadcast([128, 4, 2, 8]), ALU.mult)
                    if p:
                        ins.then_inc(S("nr_on"), 1)
                    else:
                        step(ins)

        kstack_g = kstack[:, 0:16, :]
        l2x = Experts(2, 16, 8, "sel8", lambda u: u // 2,
                      lambda u: w2g[:, u // 2, 128 * (u % 2):128 * (u % 2) + 128],
                      lambda u: w2u[:, u // 2, 128 * (u % 2):128 * (u % 2) + 128],
                      lambda u: w2d[:, u, :])

        def rms1(c):
            return c if c < 2 else 2 * c - 2

        def rms2(c):
            return min(2 * c + 3, CHUNKS + c)

        def l2_tensor(e):
            e.wait_ge(S("ld_w2"), 16 * 10)
            after_turn(e, 2, 0)

            def project(c):
                turn_tensor(e, hx1, "rms", c, 0)
                e.wait_ge(S("l2_hT"), c + 1)
                for t in range(4):
                    mm = T.matmul(ps[:, 1 + t // 2, 192 * (t % 2):192 * (t % 2) + 192],
                                  hT[:, 128 * t:128 * (t + 1)], w2[:], start=True, stop=True)
                mm.then_inc(S("nr_qkv"), 1)

            project(0)
            for c in range(CHUNKS):
                narrow_first_half_tensor(e, l2n, c)
                if c + 1 < CHUNKS:
                    project(c + 1)
                narrow_second_half_tensor(e, l2n, c)
                finish_tensor(e, 2, c, w2o[:], None, 0, 1)
                if c:
                    xT_tensor(e, 2, c - 1, 5)
                turn_tensor(e, hx, "rms2", c, 0)
                e.wait_ge(S("l2_hT2"), c + 1)
                for t in range(4):
                    mm = T.matmul(ps[:, 7, 8 * t:8 * t + 8], hT2[:, 128 * t:128 * (t + 1)], w2r[:],
                                  start=True, stop=True)
                mm.then_inc(S("logits"), 1)
                e.wait_ge(S("ld_w2x"), 64)
                experts_tensor(e, l2x, c, hT2)
            after_turn(e, 2, CHUNKS - 1)
            xT_tensor(e, 2, CHUNKS - 1, 5)

        def l2_scalar(e):
            e.wait_ge(S("ld_w2"), 16 * 10)
            after_chunk(e, 2, 0)

            def project(c):
                e.wait_ge(S("rms_T_ps"), c + 1)
                A.activation(hT[:], bank(0), ACT.Copy, scale=ln12[:, 0:1]).then_inc(S("l2_hT"), 1)
                e.wait_ge(S("nr_qkv"), c + 1)
                if c:
                    e.wait_ge(S("nr_qstack"), c)
                qkv = ps[:, 1:3, 0:384].rearrange("p b (t n) -> p b t n", t=2)
                A.activation(kf[:, 0:16, :].rearrange("p (b t h) d -> p b t (h d)", b=2, t=2),
                             qkv[:, :, :, 128:160], ACT.Copy).then_inc(S("nr_qk_sb"), 1)
                A.activation(qf[:].rearrange("p (b t h) d -> p b t (h d)", b=2, t=2),
                             qkv[:, :, :, 0:128], ACT.Copy).then_inc(S("nr_qk_sb"), 1)
                first, b = 4 * (c % 2), c // 2 % 2
                A.activation(values_g[:, b, first:first + 2, :, 0:8],
                             qkv[:, 0, :, 160:192].rearrange("p t (h d) -> p t h d", d=8),
                             ACT.Copy).then_inc(S("act_step"), 1)
                A.activation(values_g[:, b, first + 2:first + 4, :, 0:8],
                             qkv[:, 1, :, 160:192].rearrange("p t (h d) -> p t h d", d=8),
                             ACT.Copy).then_inc(S("nr_qk_sb"), 1)

            project(0)
            narrow_fill_scalar(e, l2n, 0)
            for c in range(CHUNKS):
                stack_evac(e, act_copy, kT, 4, "nr_kT", c, 5, c % 2)
                turned_again(e, act_copy, "nr_mT_act", c, 1, 5, c % 2)
                if c + 1 < CHUNKS:
                    project(c + 1)
                narrow_second_scalar(e, l2n, c)
                finish_scalar(e, 2, c, 0)
                if c:
                    xT_scalar(e, 2, c - 1, 5)
                e.wait_ge(S("rms2_T_ps"), c + 1)
                A.activation(hT2[:], bank(0), ACT.Copy, scale=ln12[:, 1:2]).then_inc(S("l2_hT2"), 1)
                e.wait_ge(S("shifted"), c + 1)
                A.activation(lge[:, :, 0:8], lge[:, :, 0:8], ACT.Exp).then_inc(S("exponentials"), 1)
                experts_scalar(e, l2x, c)
            xT_scalar(e, 2, CHUNKS - 1, 5)

        def l2_gpsimd(e, step):
            after_chunk(e, 2, 0)
            rms_gpsimd(e, step, "rms", rms1(0))
            narrow_consts_gpsimd(e, step, l2n)
            rms_gpsimd(e, step, "rms", rms1(1))
            for c in range(CHUNKS):
                if c:
                    ln_gpsimd(e, step, 2, c - 1)
                if c + 2 < CHUNKS:
                    rms_gpsimd(e, step, "rms", rms1(c + 2))
                rms_gpsimd(e, step, "rms", rms2(c))
                experts_gpsimd(e, l2x, c)
            ln_gpsimd(e, step, 2, CHUNKS - 1)

        def l2_vector(e, step):
            after_chunk(e, 2, 0)
            rms_vector(e, step, xs(2, 0), hx1, "rms", rms1(0))
            narrow_stacks_vector(e, step, l2n, 0)
            rms_vector(e, step, xs(2, 1), hx1, "rms", rms1(1))
            for c in range(CHUNKS):
                narrow_first_half_vector(e, step, l2n, c)
                if c + 1 < CHUNKS:
                    narrow_stacks_vector(e, step, l2n, c + 1)
                if c:
                    ln_vector(e, step, 2, c - 1)
                if c + 2 < CHUNKS:
                    rms_vector(e, step, xs(2, c + 2), hx1, "rms", rms1(c + 2))
                narrow_second_half_vector(e, step, l2n, c)
                e.wait_ge(S("nr_out"), c + 1)
                h1f = flat(h1)
                step(V.tensor_tensor(h1f, bank(1), flat(xs(2, c)), ALU.add))
                step.wait()
                step(V.tensor_scalar(h1f, h1f, -100.0, 100.0, ALU.max, ALU.min))
                step.wait()
                rms_vector(e, step, h1, hx, "rms", rms2(c), 1.0, "rms2_x")
                e.wait_ge(S("logits"), c + 1)
                l3 = lg[:, :, 0:8]
                step(V.tensor_copy(l3, ps[:, 7, 0:32].rearrange("p (t e) -> p t e", t=4)))
                step.wait()
                step(V.tensor_reduce(lgm[:], l3, AX.X, ALU.max))
                step.wait()
                V.tensor_tensor(lge[:, :, 0:8], l3, lgm[:].unsqueeze(2).to_broadcast([128, 4, 8]), ALU.subtract)\
                    .then_inc(S("shifted"), 1)
                rank_vector(step, l3, 4, 8, 2)
                e.wait_ge(S("exponentials"), c + 1)
                step(V.tensor_tensor(cw[:, :, 0:8], lge[:, :, 0:8],
                                     msk[:, 0:32].rearrange("p (t e) -> p t e", t=4), ALU.mult))
                step.wait()
                weights_vector(e, step, 8, 1.0, 0.0)
                experts_vector(e, l2x, c)
                e.wait_ge(S("ex_down"), 16 * (c + 1))
                yf = flat(y[:, c % 2])
                step(V.tensor_tensor(yf, bank(6), h1f, ALU.add))
                step.wait()
                step(V.tensor_scalar(yf, yf, -100.0, 100.0, ALU.max, ALU.min))
                step.wait()
                step(V.tensor_tensor(yf, yf, flat(xs(2, c)), ALU.add))
            ln_vector(e, step, 2, CHUNKS - 1)

        SCALE3 = float(D) ** -0.5
        sum3 = norm2r[:].rearrange("p a n -> p (a n)")

        def l3_tensor(e):
            after_turn(e, 3, 0)
            e.wait_ge(S("ld_w3"), 48)
            for i in range(3):
                mm = T.transpose(ps[:, 7, 128 * i:128 * (i + 1)], w3[:, i, :], ident)
            mm.then_inc(S("wT_ps"), 1)
            e.wait_ge(S("wT"), 2)

            def scores(i):
                qt = i % QT
                width = 128 * (qt + 1)
                if i % QT < 2:
                    e.wait_ge(S("l3_qkv_sb"), 6 * (i // QT + 1))
                if i >= 2:
                    e.wait_ge(S("l3_prob"), i - 1)
                b0, db, dcol = 2 * (i % 2), qt // 4, 128 * (qt % 4)
                T.matmul(ps[:, b0 + db, dcol:dcol + 128], identb, B("causal"), start=True, stop=False,
                         skip_group_check=True)
                for half in range(db + 1):
                    w = min(512, width - 512 * half)
                    mm = T.matmul(ps[:, b0 + half, 0:w], q3T[:, 128 * qt:128 * qt + 128],
                                  k3T[:, 512 * half:512 * half + w], start=half != db, stop=True,
                                  skip_group_check=True)
                mm.then_inc(S("l3_s"), 1)

            def turn(i):
                e.wait_ge(S("l3_prob"), i + 1)
                if i:
                    e.wait_ge(S("l3_pT_sb"), i)
                for kt in range(i % QT + 1):
                    mm = T.transpose(ps[:, 4 + kt // 4, 128 * (kt % 4):128 * (kt % 4) + 128],
                                     ring[:, i % RING, 128 * kt:128 * kt + 128], ident)
                mm.then_inc(S("l3_pT_ps"), 1)

            def values(i):
                qt = i % QT
                e.wait_ge(S("l3_pT_sb"), i + 1)
                if i >= 2:
                    e.wait_ge(S("l3_y"), i - 1)
                for kt in range(qt + 1):
                    mm = T.matmul(ps[:, 6 + i % 2, 0:128], pTr[:, i % 2, kt, :], v3[:, kt, :],
                                  start=kt == 0, stop=kt == qt)
                mm.then_inc(S("l3_pv"), 1)

            for b in range(SEQS):
                if b:
                    after_turn(e, 3, 2 * b)
                    e.wait_ge(S("l3_pT_sb"), QT * b)
                for half in range(2):
                    src = xT[:, SEQ * b + 512 * half:SEQ * b + 512 * half + 512]
                    T.matmul(bank(half), w3T[:, 0, :], src, start=True, stop=True).then_inc(S("l3_qkv"), 1)
                for half in range(2):
                    src = xT[:, SEQ * b + 512 * half:SEQ * b + 512 * half + 512]
                    T.matmul(bank(2 + half), w3T[:, 1, :], src, start=True, stop=True).then_inc(S("l3_qkv"), 1)
                for half in range(2):
                    for t in range(4):
                        at = SEQ * b + 512 * half + 128 * t
                        mm = T.matmul(ps[:, 4 + half, 128 * t:128 * t + 128], xT[:, at:at + 128], w3T[:, 2, :],
                                      start=True, stop=True)
                    mm.then_inc(S("l3_qkv"), 1)
                scores(QT * b)
                for r in range(QT + 1):
                    if r + 1 < QT:
                        scores(QT * b + r + 1)
                    if r < QT:
                        turn(QT * b + r)
                    if r:
                        values(QT * b + r - 1)
                for c in (2 * b, 2 * b + 1):
                    after_turn(e, 3, c)
                    xT_tensor(e, 3, c, 0)

        def l3_scalar(e):
            e.wait_ge(S("wT_ps"), 2)
            A.activation(flat(w3T), ps[:, 7, 0:384], ACT.Copy).then_inc(S("wT"), 1)
            for b in range(SEQS):
                for i, dst in enumerate((q3T[:, 0:512], q3T[:, 512:1024], k3T[:, 0:512], k3T[:, 512:1024],
                                         flat(v3[:, 0:4, :]), flat(v3[:, 4:8, :]))):
                    e.wait_ge(S("l3_qkv"), 6 * b + i + 1)
                    A.activation(dst, bank(i), ACT.Copy).then_inc(S("l3_qkv_sb"), 1)
                for i in range(QT * b, QT * b + QT):
                    width = 128 * (i % QT + 1)
                    e.wait_ge(S("l3_max"), i + 1)
                    if i >= RING:
                        e.wait_ge(S("l3_pT_ps"), i - RING + 1)
                    b0 = 2 * (i % 2)
                    s = ps[:, b0:b0 + 2, :].rearrange("p a b -> p (a b)")[:, 0:width]
                    A.activation(ring[:, i % RING, 0:width], s, ACT.Exp, bias=nmr[:, i:i + 1], scale=SCALE3,
                                 accum_out=sum3[:, i:i + 1]).then_inc(S("l3_prob"), 1)
                for c in (2 * b, 2 * b + 1):
                    xT_scalar(e, 3, c, 0)

        def l3_gpsimd(e, step):
            for c in range(CHUNKS):
                ln_gpsimd(e, step, 3, c)

        def l3_vector(e, step):
            def row_max(i):
                width, b0 = 128 * (i % QT + 1), 2 * (i % 2)
                e.wait_ge(S("l3_s"), i + 1)
                s = ps[:, b0:b0 + 2, :].rearrange("p a b -> p (a b)")[:, 0:width]
                step(V.tensor_reduce(nm[:, i:i + 1], s, AX.X, ALU.max, negate=True))
                step.wait()
                V.tensor_scalar(nmr[:, i:i + 1], nm[:, i:i + 1], SCALE3, None, ALU.mult).then_inc(S("l3_max"), 1)

            def evac(i):
                e.wait_ge(S("l3_pT_ps"), i + 1)
                if i >= 2:
                    e.wait_ge(S("l3_pv"), i - 1)
                n = i % QT + 1
                src = ps[:, 4:6, :].rearrange("p a b -> p (a b)")[:, 0:128 * n]
                V.tensor_copy(pTr[:, i % 2, 0:n, :].rearrange("p k q -> p (k q)"), src).then_inc(S("l3_pT_sb"), 1)

            def output(i):
                t, c = i % 4, i // 4
                if t == 0:
                    after_chunk(e, 3, c)
                e.wait_ge(S("l3_pv"), i + 1)
                step(V.reciprocal(m2[:, i % 16:i % 16 + 1], sum3[:, i:i + 1]))
                step.wait()
                V.scalar_tensor_tensor(y[:, c % 2, t, :], ps[:, 6 + i % 2, 0:128], m2[:, i % 16:i % 16 + 1],
                                       x[:, 4 * c + t, :], ALU.mult, ALU.add).then_inc(S("l3_y"), 1)

            for b in range(SEQS):
                base = QT * b
                row_max(base)
                for r in range(QT + 1):
                    if r + 1 < QT:
                        row_max(base + r + 1)
                    if r < QT:
                        evac(base + r)
                    if r:
                        output(base + r - 1)
                        if r % 4 == 0:
                            c = 2 * b + r // 4 - 1
                            e.wait_ge(S("l3_y"), 4 * (c + 1))
                            ln_vector(e, step, 3, c)

        l4x = Experts(4, 9, 16, "sel16", lambda u: u if u < 8 else None,
                      lambda u: w4T[:, u, :], lambda u: w4T[:, 9 + u, :], lambda u: w4T[:, 18 + u, :])

        def l4_tensor(e):
            after_turn(e, 4, 0)
            e.wait_ge(S("ld_w4"), 16 * 7)
            for g in range(7):
                for i in range(4 * g, min(4 * g + 4, 27)):
                    mm = T.transpose(ps[:, g, 128 * (i % 4):128 * (i % 4) + 128], w4n[:, i, :], ident)
                mm.then_inc(S("wT_ps"), 1)
            e.wait_ge(S("ld_w4r"), 32)
            T.transpose(ps[:, 7, 0:16], w4r[:], F("ident", 16)[:, 0:16]).then_inc(S("wT_ps"), 1)
            e.wait_ge(S("wT"), 10)
            def logits(c):
                for t in range(4):
                    at = 512 * c + 128 * t
                    mm = T.matmul(ps[:, 7, 16 * t:16 * t + 16], xT[:, at:at + 128], w4rT[:], start=True, stop=True)
                mm.then_inc(S("logits"), 1)

            logits(0)
            for c in range(CHUNKS):
                def between(u):
                    if u == 1 and c + 1 < CHUNKS:
                        if c >= 2:
                            after_turn(e, 4, c - 1)
                        logits(c + 1)
                    if u == 6 and c:
                        e.wait_ge(S("l4_sig"), min(c + 2, CHUNKS))
                        xT_tensor(e, 4, c - 1, 7)

                experts_tensor(e, l4x, c, xT[:, 512 * c:512 * c + 512], between)
            after_turn(e, 4, CHUNKS - 1)
            xT_tensor(e, 4, CHUNKS - 1, 7)

        def l4_scalar(e):
            for g in range(7):
                n = min(4, 27 - 4 * g)
                e.wait_ge(S("wT_ps"), g + 3)
                A.activation(flat(w4T[:, 4 * g:4 * g + n, :]), ps[:, g, 0:128 * n], ACT.Copy).then_inc(S("wT"), 1)
            e.wait_ge(S("wT_ps"), 10)
            A.activation(w4rT[:], ps[:, 7, 0:16], ACT.Copy).then_inc(S("wT"), 1)
            after_chunk(e, 4, 0)

            def sigmoids(c):
                e.wait_ge(S("logits"), CHUNKS + c + 1)
                if c:
                    e.wait_ge(S("ex_cpart"), CHUNKS + c)
                A.activation(lg[:].rearrange("p t e -> p (t e)"), ps[:, 7, 0:64], ACT.Sigmoid)\
                    .then_inc(S("l4_sig"), 1)

            sigmoids(0)
            for c in range(CHUNKS):
                def between(u):
                    if u == 2 and c + 1 < CHUNKS:
                        sigmoids(c + 1)
                    if u == 8 and c:
                        xT_scalar(e, 4, c - 1, 7)

                experts_scalar(e, l4x, c, between)
            xT_scalar(e, 4, CHUNKS - 1, 7)

        def l4_gpsimd(e, step):
            for c in range(CHUNKS):
                def between(u):
                    if u == 2 and c:
                        ln_gpsimd(e, step, 4, c - 1)

                experts_gpsimd(e, l4x, c, between)
            ln_gpsimd(e, step, 4, CHUNKS - 1)

        def l4_vector(e, step):
            pairs = gt[:, 0:96].rearrange("p (g k) -> p g k", k=6)
            g4 = lge[:].rearrange("p t (g k) -> p (t g) k", g=4)
            e.wait_ge(S("ld_w4r"), 32)
            after_chunk(e, 4, 0)

            def choose_groups(c):
                e.wait_ge(S("l4_sig"), c + 1)
                step.wait()
                step(V.tensor_tensor(lge[:], lg[:], ebias[:].unsqueeze(1).to_broadcast([128, 4, 16]), ALU.add))
                step.wait()
                step(V.tensor_tensor(pairs[:, :, 0:3], g4[:, :, 0:3], g4[:, :, 1:4], ALU.add))
                step(V.tensor_tensor(pairs[:, :, 3:5], g4[:, :, 0:2], g4[:, :, 2:4], ALU.add))
                step(V.tensor_tensor(pairs[:, :, 5:6], g4[:, :, 0:1], g4[:, :, 3:4], ALU.add))
                step.wait()
                step(V.tensor_reduce(cwr[:, :, 0:4], pairs.rearrange("p (t g) k -> p t g k", t=4), AX.X, ALU.max))
                rank_vector(step, cwr[:, :, 0:4], 4, 4, 2)
                step(V.tensor_tensor(cw[:].rearrange("p t (g k) -> p (t g) k", g=4), g4,
                                     msk[:, 0:16].unsqueeze(2).to_broadcast([128, 16, 4]), ALU.mult))

            def choose_experts(c):
                rank_vector(step, cw[:], 4, 16, 4)
                step(V.tensor_tensor(cw[:], lg[:], msk[:, 0:64].rearrange("p (t e) -> p t e", t=4), ALU.mult))

            def weigh(c):
                step.wait()
                e.wait_ge(S("ex_cT_ps"), CHUNKS + c)
                weights_vector(e, step, 16, 2.5, 1e-20)

            choose_groups(0)
            choose_experts(0)
            weigh(0)
            for c in range(CHUNKS):
                def between(u):
                    if u == 1 and c:
                        ln_vector(e, step, 4, c - 1)
                    if u == 3 and c + 1 < CHUNKS:
                        choose_groups(c + 1)
                    if u == 5 and c + 1 < CHUNKS:
                        choose_experts(c + 1)
                    if u == 7 and c + 1 < CHUNKS:
                        weigh(c + 1)

                experts_vector(e, l4x, c, between)
                e.wait_ge(S("ex_down"), 16 * CHUNKS + 9 * (c + 1))
                residual_vector(e, step, 4, c, 6)
            ln_vector(e, step, 4, CHUNKS - 1)

        HD5 = 64
        q5 = big[:, 0:4096].rearrange("p (s n) -> p s n", s=4)
        k5 = big[:, 4096:8192].rearrange("p (s n) -> p s n", s=4)
        v5 = tf[:, 4096:8192].rearrange("p (s n) -> p s n", s=4)
        prod5 = sf[:, 0:2048].rearrange("p (a n) -> p a n", a=2)
        pv5 = sf[:, 2048:4096].rearrange("p (a n) -> p a n", a=2)
        ctxT = hf[:, 0:1024]
        small5 = pTr[:].rearrange("p a k q -> p (a k q)")
        sc5 = small5[:, 0:256].rearrange("p (s t h) -> p s t h", s=4, t=4)
        qd5 = small5[:, 256:512].rearrange("p (s h r) -> p s h r", s=4, r=4)
        pj5 = small5[:, 512:768].rearrange("p (s h r) -> p s h r", s=4, r=4)
        mx5 = small5[:, 768:832].rearrange("p (s h) -> p s h", s=4)
        pjT = small5[0:64, 1024:1536]
        PAIRS5 = sorted(((s, t) for s in range(4) for t in range(4)), key=lambda st: (max(st), st))
        DVE5 = (2, 5, 8, 11, 13, 15)
        POOL5 = [i for i in range(16) if i not in DVE5]
        PROJ5 = [(part, s, half) for s in range(4) for part in (0, 1) for half in (0, 1)] + \
                [(2, s, half) for s in range(4) for half in (0, 1)]

        def by_offset(v, off):
            lo, hi = max(0, -off), min(4, 4 - off)
            st = v.rearrange("p s t h -> p (s t) h")
            first = 5 * lo + off
            return st[:, first:first + 5 * (hi - lo - 1) + 1:5, :], lo, hi

        def l5_tensor(e):
            after_turn(e, 5, 0)
            e.wait_ge(S("ld_w5"), 16 * 4)
            e.wait_ge(S("ld_w5s"), 16 * 25)
            for g in range(8):
                for i in range(4):
                    src = w5n[:, 4 * g + i, :] if g < 6 else w5on[:, 4 * (g - 6) + i, :]
                    mm = T.transpose(ps[:, g, 128 * i:128 * (i + 1)], src, ident)
                mm.then_inc(S("wT_ps"), 1)
            e.wait_ge(S("wT"), 18)
            for i in range(8):
                T.matmul(ps[:, 0, 8 * i:8 * i + 8], w5n[:, i, :], kdb[:], start=True, stop=True)
                T.matmul(ps[0:1, 1, 8 * i:8 * i + 8], b5q[:, i:i + 1], kdb[:], start=True, stop=True)
                mm = T.matmul(ps[0:64, 2, 0:128], vdb[:, 60 - 8 * i:124 - 8 * i], w5oT[:, i, :],
                              start=i == 0, stop=i == 7)
            mm.then_inc(S("l5_fold_ps"), 1)
            e.wait_ge(S("l5_fold"), 3)
            e.wait_ge(S("ld_b5row"), 48)
            for c in range(CHUNKS):
                for i in range(24):
                    part, s, half = PROJ5[i]
                    if i >= 4:
                        e.wait_ge(S("l5_qkv_sb"), 24 * c + i - 3)
                    tok = SEQ * s + 128 * c
                    cols = slice(1024 * part + 512 * half, 1024 * part + 512 * half + 512)
                    T.matmul(bank(i % 4), xT[:, tok:tok + 128], w5T[:, cols], start=True, stop=False)
                    T.matmul(bank(i % 4), B("ones", 3), b5row[0:3, cols], start=False, stop=True)\
                        .then_inc(S("l5_qkv"), 1)
                for s in range(4):
                    tok = SEQ * s + 128 * c
                    T.matmul(ps[:, 6, 64 * s:64 * s + 64], xT[:, tok:tok + 128], qk5[:], start=True, stop=False)
                    mm = T.matmul(ps[:, 6, 64 * s:64 * s + 64], ones_row, rb5[:], start=False, stop=True)
                mm.then_inc(S("l5_qd_ps"), 1)
                e.wait_ge(S("l5_pj"), c + 1)
                for s in range(4):
                    mm = T.transpose(ps[0:64, 4, 128 * s:128 * s + 128], pj5[:, s].rearrange("p h r -> p (h r)"), ident)
                mm.then_inc(S("l5_pjT_ps"), 1)
                if c:
                    after_turn(e, 5, c - 1)
                    xT_tensor(e, 5, c - 1, 7)
                e.wait_ge(S("l5_qkv_sb"), 24 * (c + 1))
                e.wait_ge(S("l5_pjT"), c + 1)

                def project(s):
                    e.wait_ge(S("l5_ctxT"), 4 * c + s + 1)
                    dst = ps[:, 5, 128 * s:128 * s + 128]
                    for i in range(8):
                        T.matmul(dst, ctxT[:, 128 * i:128 * i + 128], w5oT[:, i, :], start=i == 0, stop=False)
                    T.matmul(dst, pjT[:, 128 * s:128 * s + 128], vw5[:], start=False, stop=False)
                    T.matmul(dst, ones_row, b5o[:], start=False, stop=True).then_inc(S("l5_out"), 1)

                for s in range(4):
                    if s >= 2:
                        e.wait_ge(S("l5_ctxT"), 4 * c + s - 1)
                    for t in range(4):
                        j = 3 * s + t
                        if t == 3:
                            e.wait_ge(S("l5_pv_pool"), 4 * c + s + 1)
                            src = prod5[:, s % 2, :]
                        else:
                            e.wait_ge(S("l5_pv"), 12 * c + j + 1)
                            src = pv5[:, j % 2, :]
                        for k in range(8):
                            mm = T.matmul(ps[:, 2 * (s % 2) + k // 4, 128 * (k % 4):128 * (k % 4) + 128],
                                          src[:, 128 * k:128 * k + 128], ident, is_transpose=True,
                                          start=t == 0 and k % 4 == 0, stop=t == 3, skip_group_check=True)
                        mm.then_inc(S("l5_ctx"), 1)
                    if s:
                        project(s - 1)
                project(3)
            after_turn(e, 5, CHUNKS - 1)
            xT_tensor(e, 5, CHUNKS - 1, 7)

        def l5_scalar(e):
            after_chunk(e, 5, 0)
            for g in range(8):
                e.wait_ge(S("wT_ps"), g + 11)
                dst = w5T[:, 512 * g:512 * g + 512] if g < 6 else flat(w5oT[:, 4 * (g - 6):4 * (g - 6) + 4, :])
                A.activation(dst, bank(g), ACT.Copy).then_inc(S("wT"), 1)
            e.wait_ge(S("l5_fold_ps"), 1)
            A.activation(qk5[:], ps[:, 0, 0:64], ACT.Copy).then_inc(S("l5_fold"), 1)
            A.activation(rb5[:], ps[0:1, 1, 0:64], ACT.Copy).then_inc(S("l5_fold"), 1)
            A.activation(vw5[:], ps[0:64, 2, 0:128], ACT.Copy).then_inc(S("l5_fold"), 1)
            for c in range(CHUNKS):
                if c == 0:
                    e.wait_ge(S("ld_b5row"), 48)
                for i in range(24):
                    part, s, half = PROJ5[i]
                    e.wait_ge(S("l5_qkv"), 24 * c + i + 1)
                    A.activation((q5, k5, v5)[part][:, s, 512 * half:512 * half + 512], bank(i % 4), ACT.Copy,
                                 scale=HD5 ** -0.5 if part == 0 else 1.0).then_inc(S("l5_qkv_sb"), 1)
                e.wait_ge(S("l5_qd_ps"), c + 1)
                A.activation(qd5.rearrange("p s h r -> p (s h r)"), ps[:, 6, 0:256], ACT.Copy, scale=HD5 ** -0.5)\
                    .then_inc(S("l5_qd"), 1)
                e.wait_ge(S("shifted"), CHUNKS + c + 1)
                A.activation(sc5, sc5, ACT.Exp).then_inc(S("exponentials"), 1)
                e.wait_ge(S("l5_pjT_ps"), c + 1)
                A.activation(pjT, ps[0:64, 4, :], ACT.Copy).then_inc(S("l5_pjT"), 1)
                if c:
                    xT_scalar(e, 5, c - 1, 7)
                for s in range(4):
                    e.wait_ge(S("l5_ctx"), 16 * c + 4 * s + 4)
                    if s:
                        e.wait_ge(S("l5_out"), 4 * c + s)
                    b = 2 * (s % 2)
                    A.activation(ctxT, ps[:, b:b + 2, :].rearrange("p a b -> p (a b)"), ACT.Copy)\
                        .then_inc(S("l5_ctxT"), 1)
            xT_scalar(e, 5, CHUNKS - 1, 7)

        def l5_gpsimd(e, step):
            for c in range(CHUNKS):
                if c:
                    e.wait_ge(S("l5_ctx"), 16 * c)
                for j, i in enumerate(POOL5):
                    s, t = PAIRS5[i]
                    e.wait_ge(S("l5_qkv_sb"), 24 * c + 4 * max(s, t) + 4)
                    if j >= 2:
                        e.wait_ge(S("l5_dots"), 10 * c + j - 1)
                    P.tensor_tensor(prod5[:, j % 2, :], q5[:, s, :], k5[:, t, :], ALU.mult).then_inc(S("l5_prod"), 1)
                e.wait_ge(S("l5_dots"), 10 * (c + 1))
                e.wait_ge(S("l5_pj"), c + 1)
                e.wait_ge(S("l5_qkv_sb"), 24 * (c + 1))
                for s in range(4):
                    if s >= 2:
                        e.wait_ge(S("l5_ctx"), 16 * c + 4 * s - 4)
                    P.tensor_tensor(prod5[:, s % 2, :].rearrange("p (h d) -> p h d", h=H),
                                    v5[:, 3, :].rearrange("p (h d) -> p h d", h=H),
                                    sc5[:, s, 3, :].unsqueeze(2).to_broadcast([128, H, HD5]), ALU.mult)\
                        .then_inc(S("l5_pv_pool"), 1)
                ln_gpsimd(e, step, 5, c)

        def l5_vector(e, step):
            after_chunk(e, 5, 0)
            e.wait_ge(S("ld_b5"), 16)
            step(V.tensor_copy(b5p[:, 0, :], b5f))
            step.wait()
            step(V.tensor_tensor(b5f, b5f, b5p[:, 0, :], ALU.subtract))
            step.wait()
            step(V.tensor_copy(b5p[:, 1, :], b5f))
            step.wait()
            V.tensor_tensor(b5p[:, 2, :], b5f, b5p[:, 1, :], ALU.subtract).then_inc(S("l5_b5p"), 1)
            for c in range(CHUNKS):
                step(V.memset(pj5, 0.0))
                for i, (s, t) in enumerate(PAIRS5):
                    if i in DVE5:
                        step.wait()
                        e.wait_ge(S("l5_qkv_sb"), 24 * c + 4 * max(s, t) + 4)
                        step(V.tensor_tensor(pv5[:, 0, :], q5[:, s, :], k5[:, t, :], ALU.mult))
                        step.wait()
                        step(V.tensor_reduce(sc5[:, s, t, :], pv5[:, 0, :].rearrange("p (h d) -> p h d", h=H),
                                             AX.X, ALU.add))
                        continue
                    j = POOL5.index(i)
                    e.wait_ge(S("l5_prod"), 10 * c + j + 1)
                    V.tensor_reduce(sc5[:, s, t, :], prod5[:, j % 2, :].rearrange("p (h d) -> p h d", h=H),
                                    AX.X, ALU.add).then_inc(S("l5_dots"), 1)
                step.wait()
                e.wait_ge(S("l5_dots"), 10 * (c + 1))
                e.wait_ge(S("l5_qd"), c + 1)
                for off in range(-3, 4):
                    v, lo, hi = by_offset(sc5, off)
                    step(V.tensor_tensor(v, v, qd5[:, lo:hi, :, abs(off)], ALU.add))
                step.wait()
                by_t = sc5.rearrange("p s t h -> p s h t")
                step(V.tensor_reduce(mx5, by_t, AX.X, ALU.max))
                step.wait()
                V.tensor_tensor(sc5, sc5, mx5.unsqueeze(2).to_broadcast([128, 4, 4, H]), ALU.subtract)\
                    .then_inc(S("shifted"), 1)
                e.wait_ge(S("exponentials"), CHUNKS + c + 1)
                step(V.tensor_reduce(mx5, by_t, AX.X, ALU.add))
                step.wait()
                step(V.reciprocal(mx5, mx5))
                step.wait()
                step(V.tensor_tensor(sc5, sc5, mx5.unsqueeze(2).to_broadcast([128, 4, 4, H]), ALU.mult))
                step.wait()
                for off in (0, 1, 2, 3, -1, -2, -3):
                    v, lo, hi = by_offset(sc5, off)
                    dst = pj5[:, lo:hi, :, abs(off)]
                    if off == -1:
                        step.wait()
                    ins = V.tensor_tensor(dst, dst, v, ALU.add)
                    if off == -3:
                        ins.then_inc(S("l5_pj"), 1)
                    else:
                        step(ins)
                e.wait_ge(S("l5_qkv_sb"), 24 * (c + 1))
                for j in range(12):
                    s, t = j // 3, j % 3
                    if j >= 2:
                        e.wait_ge(S("l5_ctx"), 16 * c + 4 * ((j - 2) // 3) + (j - 2) % 3 + 1)
                    V.tensor_tensor(pv5[:, j % 2, :].rearrange("p (h d) -> p h d", h=H),
                                    v5[:, t, :].rearrange("p (h d) -> p h d", h=H),
                                    sc5[:, s, t, :].unsqueeze(2).to_broadcast([128, H, HD5]), ALU.mult)\
                        .then_inc(S("l5_pv"), 1)
                e.wait_ge(S("l5_out"), 4 * (c + 1))
                residual_vector(e, step, 5, c, 5)
                ln_vector(e, step, 5, c)

        PHASES = (13, 12, 12, 12)
        CAP = 60.0
        small6 = small5
        row6 = sf[0:4, :]
        s6, E6, junk6, kinv6 = row6[:, 0:1024], row6[:, 1024:2048], row6[:, 2048:3072], row6[:, 3072:4096]
        z6 = hf[0:4, 0:1024]
        col6 = small6[0:4, 0:16]
        smax6, L6, ctr6, tmp6, lnu6 = (col6[:, i:i + 1] for i in range(5))
        u6 = col6[:, 8:10]
        zcol, count6 = small6[:, 16:20], small6[:, 32:48]
        G6, e6, rank6 = small6[:, 64:68], small6[:, 68:72], small6[:, 72:76]
        zrows = (big[:, 0:1024], big[:, 3584:4608])
        hx6 = (hx, big[:, 7680:8192].rearrange("p (t d) -> p t d", t=4))
        zjunk = big[:, 1024:2048]
        hl6, hh6 = big[:, 2048:2560], big[:, 2560:3072]
        gl6 = big[0:64, 5120:5632]
        gh6 = big[:, 5632:7680].rearrange("p (k n) -> p k n", k=4)
        LOG_N_OVER_K = math.log(SEQ / K_EFF)

        def l6_tensor(e):
            after_turn(e, 6, 0)
            e.wait_ge(S("ld_w6"), 16 * 13)
            e.wait_ge(S("ld_w6h"), 16 * 6)
            for i in range(4):
                T.transpose(ps[:, 0, 128 * i:128 * i + 128], f1hn[:, i, :], ident)
                T.transpose(ps[:, 1, 128 * i:128 * i + 128], f2hn[:, i, :], ident)
            T.transpose(ps[:, 2, 0:64], f1ln[:], F("ident", 64)[:, 0:64])
            T.transpose(ps[0:64, 3, 0:128], f2ln[:], ident).then_inc(S("wT_ps"), 1)
            for half in range(2):
                for b in range(4):
                    at = SEQ * b + 512 * half
                    mm = T.matmul(ps[0:4, 4 + half, :], rt[:, b, :], xT[:, at:at + 512], start=b == 0, stop=b == 3)
            mm.then_inc(S("l6_s_ps"), 1)
            e.wait_ge(S("wT"), 22)
            for c in range(CHUNKS):
                b = c // 2
                if c:
                    e.wait_ge(S("l6_gelu"), 5 * c)
                turn_tensor(e, hx6[c % 2], "rms", CHUNKS + c, 2)
                e.wait_ge(S("l6_h"), 2 * (c + 1))
                T.matmul(ps[0:64, 3, :], f1lT[:], hl6, start=True, stop=True).then_inc(S("l6_up"), 1)
                for k in range(4):
                    if k >= 1:
                        e.wait_ge(S("l6_gelu"), 5 * c + k)
                    T.matmul(bank(2 + k % 2), f1hT[:, k, :], hh6, start=True, stop=True).then_inc(S("l6_up"), 1)
                e.wait_ge(S("l6_z"), 1)
                if c:
                    e.wait_ge(S("l6_zrow"), c)
                for half in range(2):
                    mm = T.matmul(bank(half), F("selb", 4)[:, 128 * b:128 * b + 128], z6[:, 512 * half:512 * half + 512],
                                  start=True, stop=True)
                mm.then_inc(S("l6_zrow_ps"), 1)
                e.wait_ge(S("l6_gelu"), 5 * (c + 1))
                if c:
                    e.wait_ge(S("ln_var"), 4 * (5 * CHUNKS + c))
                for t in range(4):
                    cols = slice(128 * t, 128 * t + 128)
                    T.matmul(ps[:, 4, cols], gl6[:, cols], f2lT[:], start=True, stop=False)
                    T.matmul(ps[:, 4, cols], ones_row, fb2[:, 0, :], start=False, stop=True)
                for t in range(4):
                    cols = slice(128 * t, 128 * t + 128)
                    for k in range(4):
                        T.matmul(ps[:, 5, cols], gh6[:, k, cols], f2hT[:, k, :], start=k == 0, stop=False)
                    mm = T.matmul(ps[:, 5, cols], ones_row, fb2[:, 1, :], start=False, stop=True)
                mm.then_inc(S("l6_out"), 1)
                if c:
                    after_turn(e, 6, c - 1)
                    xT_tensor(e, 6, c - 1, 7)
            after_turn(e, 6, CHUNKS - 1)
            xT_tensor(e, 6, CHUNKS - 1, 7)

        def l6_scalar(e):
            e.wait_ge(S("wT_ps"), 19)
            A.activation(flat(f1hT), bank(0), ACT.Copy).then_inc(S("wT"), 1)
            A.activation(flat(f2hT), bank(1), ACT.Copy).then_inc(S("wT"), 1)
            A.activation(f1lT[:], ps[:, 2, 0:64], ACT.Copy).then_inc(S("wT"), 1)
            A.activation(f2lT[:], ps[0:64, 3, 0:128], ACT.Copy).then_inc(S("wT"), 1)
            def hidden(c):
                e.wait_ge(S("rms_T_ps"), CHUNKS + c + 1)
                A.activation(hl6, bank(2), ACT.Copy, scale=gam[:, 0:1]).then_inc(S("l6_h"), 1)
                A.activation(hh6, bank(2), ACT.Copy, scale=gam[:, 1:2]).then_inc(S("l6_h"), 1)
                if c:
                    e.wait_ge(S("l6_out"), c)
                e.wait_ge(S("l6_up"), 5 * c + 1)
                A.activation(gl6, ps[0:64, 3, :], ACT.Gelu, bias=fb1l[:]).then_inc(S("l6_gelu"), 1)
                for k in range(4):
                    e.wait_ge(S("l6_up"), 5 * c + k + 2)
                    A.activation(gh6[:, k, :], bank(2 + k % 2), ACT.Gelu, bias=fb1h[:, k:k + 1])\
                        .then_inc(S("l6_gelu"), 1)

            hidden(0)
            for p in range(len(PHASES)):
                e.wait_ge(S("l6_centred"), p + 1)
                A.activation(E6, E6, ACT.Exp).then_inc(S("l6_exp"), 1)
                A.activation(u6[:, 0:1], tmp6, ACT.Exp).then_inc(S("l6_exp"), 1)
                e.wait_ge(S("l6_stepped"), p + 1)
                A.activation(lnu6, u6[:, PHASES[p] % 2:PHASES[p] % 2 + 1], ACT.Ln).then_inc(S("l6_ln"), 1)
            for c in range(CHUNKS):
                if c:
                    hidden(c)
                e.wait_ge(S("l6_zrow_ps"), c + 1)
                if c >= 2:
                    e.wait_ge(S("ln_var"), 4 * (5 * CHUNKS + c - 1))
                A.activation(zrows[c % 2], ps[:, 0:2, :].rearrange("p a b -> p (a b)"), ACT.Copy)\
                    .then_inc(S("l6_zrow"), 1)
                e.wait_ge(S("l6_zcol"), 4 * (c + 1))
                A.activation(e6, zcol, ACT.Exp).then_inc(S("l6_e"), 1)
                if c:
                    xT_scalar(e, 6, c - 1, 7)
            xT_scalar(e, 6, CHUNKS - 1, 7)

        def l6_gpsimd(e, step):
            after_chunk(e, 6, 0)
            P.memset(kinv6, 1.0 / K_EFF).then_inc(S("l6_kinv"), 1)
            rms_gpsimd(e, step, "rms", 16, 1.0, ALU.max, 1e-24)
            for c in range(CHUNKS):
                if c + 1 < CHUNKS:
                    rms_gpsimd(e, step, "rms", 17 + c, 1.0, ALU.max, 1e-24)
                ln_gpsimd(e, step, 6, c)

        def l6_vector(e, step):
            after_chunk(e, 6, 0)
            rms_vector(e, step, xs(6, 0), hx6[0], "rms", 16, float(D) ** 0.5)
            e.wait_ge(S("l6_s_ps"), 1)
            step(V.tensor_copy(s6, ps[0:4, 4:6, :].rearrange("p a b -> p (a b)")))
            step(V.memset(L6, LOG_N_OVER_K))
            step.wait()
            step(V.tensor_reduce(smax6, s6, AX.X, ALU.max))
            step.wait()
            e.wait_ge(S("l6_kinv"), 1)
            for p, n in enumerate(PHASES):
                step(V.tensor_tensor(ctr6, L6, smax6, ALU.min))
                step.wait()
                step(V.tensor_scalar(tmp6, L6, ctr6, CAP, ALU.subtract, ALU.min))
                step.wait()
                V.tensor_scalar(E6, s6, ctr6, CAP, ALU.subtract, ALU.min).then_inc(S("l6_centred"), 1)
                e.wait_ge(S("l6_exp"), 2 * (p + 1))
                for i in range(n):
                    ins = V.scalar_tensor_tensor(junk6, E6, u6[:, i % 2:i % 2 + 1], kinv6, ALU.min, ALU.mult,
                                                 accum_out=u6[:, (i + 1) % 2:(i + 1) % 2 + 1])
                    if i == n - 1:
                        ins.then_inc(S("l6_stepped"), 1)
                    else:
                        step(ins)
                        step.wait()
                e.wait_ge(S("l6_ln"), p + 1)
                step(V.tensor_tensor(L6, ctr6, lnu6, ALU.add))
                step.wait()
            V.tensor_scalar(z6, s6, L6, 0.0, ALU.subtract, ALU.min).then_inc(S("l6_z"), 1)

            for c in range(CHUNKS):
                half = c % 2
                zrow = zrows[half]
                if c + 1 < CHUNKS:
                    if c:
                        e.wait_ge(S("rms_T_ps"), CHUNKS + c)
                    rms_vector(e, step, xs(6, c + 1), hx6[(c + 1) % 2], "rms", 17 + c, float(D) ** 0.5)
                e.wait_ge(S("l6_zrow"), c + 1)
                step.wait()
                for t in range(4):
                    q = 128 * (4 * half + t)
                    step.wait()
                    V.scalar_tensor_tensor(zjunk[:, 0:128], zrow[:, q:q + 128], 1.0, ident, ALU.mult, ALU.mult,
                                           accum_out=zcol[:, t:t + 1]).then_inc(S("l6_zcol"), 1)
                    e.wait_ge(S("l6_zcol"), 4 * c + t + 1)
                    z, cnt = zcol[:, t:t + 1], count6[:, 4 * t:4 * t + 4]
                    if q:
                        step(V.tensor_scalar(zjunk[:, 0:q], zrow[:, 0:q], z, None, ALU.is_ge, ALU.add,
                                             accum_out=cnt[:, 0:1]))
                    else:
                        step(V.memset(cnt[:, 0:1], 0.0))
                    if q + 128 < SEQ:
                        step.wait()
                        step(V.tensor_scalar(zjunk[:, 0:SEQ - q - 128], zrow[:, q + 128:SEQ], z, None, ALU.is_gt,
                                             ALU.add, accum_out=cnt[:, 1:2]))
                    else:
                        step(V.memset(cnt[:, 1:2], 0.0))
                    step.wait()
                    step(V.tensor_scalar(zjunk[:, 0:128], zrow[:, q:q + 128], z, None, ALU.is_gt, ALU.add,
                                         accum_out=cnt[:, 2:3]))
                    step.wait()
                    step(V.scalar_tensor_tensor(zjunk[:, 0:128], zrow[:, q:q + 128], z, B("before"),
                                                ALU.is_equal, ALU.mult, accum_out=cnt[:, 3:4]))
                step.wait()
                step(V.tensor_reduce(rank6, count6.rearrange("p (t k) -> p t k", t=4), AX.X, ALU.add))
                step.wait()
                e.wait_ge(S("l6_e"), c + 1)
                step(V.tensor_scalar(G6, e6, -1.0, 1.0, ALU.mult, ALU.add))
                step(V.tensor_scalar(rank6, rank6, float(K_HEAVY), None, ALU.is_lt))
                step.wait()
                step(V.tensor_tensor(G6, G6, e6, ALU.add))
                step.wait()
                step(V.tensor_tensor(G6, G6, rank6, ALU.mult))
                e.wait_ge(S("l6_out"), c + 1)
                if c >= 2:
                    after_chunk(e, 6, c - 1)
                step(V.tensor_tensor(flat(y[:, half]), bank(4), flat(xs(6, c)), ALU.add))
                step.wait()
                for t in range(4):
                    step(V.scalar_tensor_tensor(y[:, half, t, :], ps[:, 5, 128 * t:128 * t + 128], G6[:, t:t + 1],
                                                y[:, half, t, :], ALU.mult, ALU.add))
                ln_vector(e, step, 6, c)

        def l7_tensor(e):
            e.wait_ge(S("ld_w7"), 32)
            after_turn(e, 7, 0)

            def project(c):
                for t in range(4):
                    mm = T.matmul(ps[:, t, 0:384], xT[:, 512 * c + 128 * t:512 * c + 128 * (t + 1)], w7[:],
                                  start=True, stop=True)
                mm.then_inc(S("nr_qkv"), 1)

            project(0)
            for c in range(CHUNKS):
                narrow_first_half_tensor(e, l7n, c)
                if c + 1 < CHUNKS:
                    project(c + 1)
                narrow_second_half_tensor(e, l7n, c)
                finish_tensor(e, 7, c, w7o[:], None, 0, 1)
                if c:
                    xT_tensor(e, 7, c - 1, 5)
            after_turn(e, 7, CHUNKS - 1)
            xT_tensor(e, 7, CHUNKS - 1, 5)

        def l7_scalar(e):
            view = "p (t h) d -> p t (h d)"
            after_chunk(e, 7, 0)

            def project(c):
                e.wait_ge(S("nr_qkv"), CHUNKS + c + 1)
                if c:
                    e.wait_ge(S("nr_qstack"), CHUNKS + c)
                qkv = ps[:, 0:4, :]
                A.activation(kf[:].rearrange(view, t=4), qkv[:, :, 128:256], ACT.Copy).then_inc(S("nr_qk_sb"), 1)
                A.activation(qf[:].rearrange(view, t=4), qkv[:, :, 0:128], ACT.Copy).then_inc(S("nr_qk_sb"), 1)
                A.activation(values[:, c // 2 % 2, 4 * (c % 2):4 * (c % 2) + 4, :, 0:8],
                             qkv[:, :, 256:384].rearrange("p t (h d) -> p t h d", d=8),
                             ACT.Copy).then_inc(S("nr_qk_sb"), 1)

            project(0)
            narrow_fill_scalar(e, l7n, 0)
            for c in range(CHUNKS):
                stack_evac(e, act_copy, kT, H, "nr_kT", c + 2, 5, c % 2)
                turned_again(e, act_copy, "nr_mT_act", CHUNKS + c, 1, 5, c % 2)
                if c + 1 < CHUNKS:
                    project(c + 1)
                narrow_second_scalar(e, l7n, c)
                finish_scalar(e, 7, c, 0)
                if c:
                    xT_scalar(e, 7, c - 1, 5)
            xT_scalar(e, 7, CHUNKS - 1, 5)

        def l7_gpsimd(e, step):
            after_chunk(e, 7, 0)
            narrow_consts_gpsimd(e, step, l7n)
            for c in range(CHUNKS):
                ln_gpsimd(e, step, 7, c)

        def l7_vector(e, step):
            after_chunk(e, 7, 0)
            narrow_stacks_vector(e, step, l7n, 0)
            for c in range(CHUNKS):
                narrow_first_half_vector(e, step, l7n, c)
                if c + 1 < CHUNKS:
                    narrow_stacks_vector(e, step, l7n, c + 1)
                if c:
                    ln_vector(e, step, 7, c - 1)
                narrow_second_half_vector(e, step, l7n, c)
                e.wait_ge(S("nr_out"), CHUNKS + c + 1)
                residual_vector(e, step, 7, c, 1)
            ln_vector(e, step, 7, CHUNKS - 1)

        mean8 = small5[:, 0:4]
        r8 = big[:, 0:2048].rearrange("p (k n) -> p k n", k=4)

        def l8_tensor(e):
            after_turn(e, 8, 0)
            for b in range(SEQS):
                for t in range(QT):
                    mm = T.matmul(ps[:, 0, b:b + 1], x[:, QT * b + t, :], F("mean"), start=t == 0, stop=t == QT - 1)
            mm.then_inc(S("l8_mean_ps"), 1)
            e.wait_ge(S("l8_mean"), 1)
            e.wait_ge(S("ld_w6"), 16 * 13)
            for b in range(SEQS):
                T.matmul(ps[0:1, 1, 8 * b:8 * b + 8], mean8[:, b:b + 1], w8r[:], start=True, stop=False)
                mm = T.matmul(ps[0:1, 1, 8 * b:8 * b + 8], ones_row[:, 0:1], b8r[:], start=False, stop=True)
            mm.then_inc(S("l8_scores"), 1)
            for c in range(CHUNKS):
                b = c // 2
                e.wait_ge(S(f"ld_w8e{b}"), 16 * 7)
                if c:
                    e.wait_ge(S("l8_relu"), 4 * c)
                for k in range(4):
                    T.matmul(bank(k), w8a[:, b % 2, 128 * k:128 * k + 128], xT[:, 512 * c:512 * c + 512],
                             start=True, stop=True).then_inc(S("l8_up"), 1)
                e.wait_ge(S("l8_relu"), 4 * (c + 1))
                if c >= 2:
                    after_chunk(e, 8, c - 1)
                for t in range(4):
                    cols = slice(128 * t, 128 * t + 128)
                    for k in range(4):
                        T.matmul(ps[:, 4 + c % 2, cols], r8[:, k, cols], w8b[:, b % 2, k, :], start=k == 0, stop=False)
                    mm = T.matmul(ps[:, 4 + c % 2, cols], ones_row, b8b2[:, b % 2, :], start=False, stop=True)
                mm.then_inc(S("l8_out"), 1)

        def l8_scalar(e):
            for c in range(CHUNKS):
                b = c // 2
                e.wait_ge(S(f"ld_w8e{b}"), 16 * 7)
                if c == 0:
                    after_chunk(e, 8, 0)
                else:
                    e.wait_ge(S("l8_out"), c)
                for k in range(4):
                    e.wait_ge(S("l8_up"), 4 * c + k + 1)
                    A.activation(r8[:, k, :], bank(k), ACT.Relu, bias=b8b1[:, b % 2, k:k + 1])\
                        .then_inc(S("l8_relu"), 1)

        def l8_gpsimd(e, step):
            for c in range(CHUNKS):
                ln_gpsimd(e, step, 8, c)

        def l8_vector(e, step):
            e.wait_ge(S("l8_mean_ps"), 1)
            V.tensor_copy(mean8, ps[:, 0, 0:4]).then_inc(S("l8_mean"), 1)
            e.wait_ge(S("l8_scores"), 1)
            step(V.tensor_copy(sc8[:], ps[0:1, 1, 0:32].rearrange("p (b e) -> p b e", b=4)))
            step.wait()
            for b in range(SEQS):
                step(V.max(top8[:, b, :], sc8[:, b, :]))
            step.wait()
            for b in range(SEQS):
                V.max_index(top_idx[:, b, :], top8[:, b, :], sc8[:, b, :]).then_inc(S("l8_top"), 1)
            for c in range(CHUNKS):
                e.wait_ge(S("l8_out"), c + 1)
                residual_vector(e, step, 8, c, 4 + c % 2)
                ln_vector(e, step, 8, c)


        @block.tensor
        def _(e):
            l1_tensor(e)
            l2_tensor(e)
            l3_tensor(e)
            l4_tensor(e)
            l5_tensor(e)
            l6_tensor(e)
            l7_tensor(e)
            l8_tensor(e)

        @block.scalar
        def _(e):
            l1_scalar(e)
            l2_scalar(e)
            l3_scalar(e)
            l4_scalar(e)
            l5_scalar(e)
            l6_scalar(e)
            l7_scalar(e)
            l8_scalar(e)

        @block.gpsimd
        def _(e):
            step = Chain(e, S("pool_step"))
            l1_gpsimd(e, step)
            l2_gpsimd(e, step)
            l3_gpsimd(e, step)
            l4_gpsimd(e, step)
            l5_gpsimd(e, step)
            l6_gpsimd(e, step)
            l7_gpsimd(e, step)
            l8_gpsimd(e, step)

        @block.vector
        def _(e):
            step = Chain(e, S("dve_step"))
            l1_vector(e, step)
            l2_vector(e, step)
            l3_vector(e, step)
            l4_vector(e, step)
            l5_vector(e, step)
            l6_vector(e, step)
            l7_vector(e, step)
            l8_vector(e, step)


_OUTS = [((SEQS, SEQ, D), "float32")]


def kernel(**inputs):
    import numpy as _np
    import concourse.bacc as _bacc
    from concourse import mybir as _mybir
    from concourse.bass_utils import run_bass_kernel_spmd as _run

    nc = _bacc.Bacc("TRN2", target_bir_lowering=False, num_devices=1)
    const_f, const_b = constants()
    every = dict(inputs)
    every["const_f"], every["const_b"] = const_f, const_b
    arrays, args = {}, {}
    for name, value in every.items():
        v = _np.ascontiguousarray(value)
        arrays[f"in_{name}_dram"] = v
        args[name] = nc.dram_tensor(f"in_{name}_dram", v.shape, _mybir.dt.from_np(v.dtype), kind="ExternalInput").ap()
    shape, dtype = _OUTS[0]
    out = nc.dram_tensor("out_0_dram", shape, _mybir.dt.from_np(_np.dtype(dtype)), kind="ExternalOutput").ap()
    program(nc, args, out)
    r = _run(nc, [arrays], core_ids=[0])
    return r.results[0]["out_0_dram"]
```
